# Optimizing a Trainium2 kernel written in Bass

```python
import numpy as np
import jax
import jax.numpy as jnp

def _softmax(x, axis=-1):
    return jax.nn.softmax(x, axis=axis)

def _gelu(x):
    return jax.nn.gelu(x, approximate=True)

def _silu(x):
    return jax.nn.silu(x)

def _sigmoid(x):
    return jax.nn.sigmoid(x)

def _layernorm(x, axis=-1, eps=1e-05):
    m = jnp.mean(x, axis=axis, keepdims=True)
    v = jnp.var(x, axis=axis, keepdims=True)
    return (x - m) / jnp.sqrt(v + eps)

def _scatter_add(tgt, idx, src, axis=0):
    return tgt.at[idx].add(src)

def _segment_sum(src, seg, n):
    return jax.ops.segment_sum(src, seg, n)
kernel_name = 'mk_prb_d2_jaxref_r8_e8c3ec'

def setup_inputs(seed: int=0):
    np.random.seed(seed)
    _w = jnp.asarray

    def _L0_attn_setup():
        import jax, jax.numpy as jnp
        import numpy as np
        LN_EPS = 1e-05

        def _layernorm(x):
            mu = jnp.mean(x, axis=-1, keepdims=True)
            var = jnp.var(x, axis=-1, keepdims=True)
            return (x - mu) * jax.lax.rsqrt(var + LN_EPS)
        key = jax.random.key(seed)
        k1, k2, k3 = jax.random.split(key, 3)
        B, L, D = (2, 512, 128)
        x = jax.random.normal(k1, (B, L, D), dtype=jnp.float32)
        W_qkv = jax.random.normal(k2, (3 * D, D), dtype=jnp.float32) * 0.02
        W_o = jax.random.normal(k3, (D, D), dtype=jnp.float32) * 0.02
        log_gamma = jnp.zeros((16,), dtype=jnp.float32)
        return {'x': x, 'W_qkv': W_qkv, 'W_o': W_o, 'log_gamma': log_gamma}
    _L0_attn_in = _L0_attn_setup()

    def _L0_ffn_setup():
        import jax, jax.numpy as jnp
        import numpy as np
        DIM = 128
        DEPTH = 6
        HEADS = 16
        DIM_HEAD = 64
        WINDOW = 32
        INNER = HEADS * DIM_HEAD
        DIM_INNER = int(DIM * 4 * 2 / 3)
        QK_SCALE = 8.0

        def shift_tokens(t):
            a, s = jnp.split(t, 2, -1)
            s = jnp.pad(s, ((0, 0), (1, 0), (0, 0)))[:, :-1]
            return jnp.concatenate([a, s], -1)

        def l2norm(t):
            return t / jnp.maximum(jnp.linalg.norm(t, axis=-1, keepdims=True), 1e-12)

        def rotate_half(x):
            x1, x2 = jnp.split(x, 2, -1)
            return jnp.concatenate([-x2, x1], -1)

        def rotary_tables(n):
            half = jnp.arange(0, DIM_HEAD, 2, dtype=jnp.float32)
            inv_freq = 1.0 / 10000.0 ** (half / DIM_HEAD)
            t = jnp.arange(n, dtype=jnp.float32)
            freqs = t[:, None] * inv_freq[None, :]
            freqs = jnp.concatenate([freqs, freqs], -1)
            base_scale = (half + 0.4 * DIM_HEAD) / (1.4 * DIM_HEAD)
            power = (t - n // 2) / (WINDOW // 2)
            scale = base_scale[None, :] ** power[:, None]
            scale = jnp.concatenate([scale, scale], -1)
            return (freqs, scale)

        def local_attention(q, k, v):
            b, h, n, d = q.shape
            w = WINDOW
            nw = n // w
            bq = q.reshape(b, h, nw, w, d)
            bk = k.reshape(b, h, nw, w, d)
            bv = v.reshape(b, h, nw, w, d)

            def look(t):
                p = jnp.pad(t, ((0, 0), (0, 0), (1, 0), (0, 0), (0, 0)))
                return jnp.concatenate([p[:, :, :nw], p[:, :, 1:]], axis=3)
            bk2, bv2 = (look(bk), look(bv))
            seq = jnp.arange(n).reshape(nw, w)
            seq_p = jnp.pad(seq, ((1, 0), (0, 0)), constant_values=-1)
            jt = jnp.concatenate([seq_p[:nw], seq_p[1:]], axis=1)
            it = seq[:, :, None]
            jb = jt[:, None, :]
            mask = (it < jb) | (it > jb + w) | (jb == -1)
            sim = jnp.einsum('bhwie,bhwje->bhwij', bq, bk2) * QK_SCALE
            sim = jnp.where(mask, -jnp.finfo(sim.dtype).max, sim)
            attn = jax.nn.softmax(sim, -1)
            out = jnp.einsum('bhwij,bhwje->bhwie', attn, bv2)
            return out.reshape(b, h, n, d)

        def attn_layer(x, Wqkv, qs, ksc, Wo):
            b, n, _ = x.shape
            qkv = x @ Wqkv
            q, k, v = jnp.split(qkv, 3, -1)
            sh = lambda t: t.reshape(b, n, HEADS, DIM_HEAD).transpose(0, 2, 1, 3)
            q, k, v = (sh(q), sh(k), sh(v))
            q = l2norm(q) * qs
            k = l2norm(k) * ksc
            freqs, scale = rotary_tables(n)
            cos, sin = (jnp.cos(freqs), jnp.sin(freqs))
            q = q * cos * scale + rotate_half(q) * sin * scale
            inv = 1.0 / scale
            k = k * cos * inv + rotate_half(k) * sin * inv
            out = local_attention(q, k, v)
            out = out.transpose(0, 2, 1, 3).reshape(b, n, INNER)
            return out @ Wo

        def ffn_layer(x, g, bln, W1, b1, W2, b2):
            mu = x.mean(-1, keepdims=True)
            var = ((x - mu) ** 2).mean(-1, keepdims=True)
            xn = (x - mu) / jnp.sqrt(var + 1e-05) * g + bln
            hg = xn @ W1 + b1
            a, gate = jnp.split(hg, 2, -1)
            return a * jax.nn.gelu(gate, approximate=False) @ W2 + b2
        key = jax.random.key(seed)
        ks = jax.random.split(key, 8)
        B, N = (2, 256)
        init = lambda k, shape: jax.random.normal(k, shape, jnp.float32) * 0.02
        return {'x': jax.random.normal(ks[0], (B, N, DIM), jnp.float32), 'Wqkv': init(ks[1], (DEPTH, DIM, 3 * INNER)), 'q_scale': jnp.ones((DEPTH, DIM_HEAD), jnp.float32), 'k_scale': jnp.ones((DEPTH, DIM_HEAD), jnp.float32), 'Wo': init(ks[2], (DEPTH, INNER, DIM)), 'ln_g': jnp.ones((DEPTH, DIM), jnp.float32), 'ln_b': jnp.zeros((DEPTH, DIM), jnp.float32), 'W1': init(ks[3], (DEPTH, DIM, 2 * DIM_INNER)), 'b1': jnp.zeros((DEPTH, 2 * DIM_INNER), jnp.float32), 'W2': init(ks[4], (DEPTH, DIM_INNER, DIM)), 'b2': jnp.zeros((DEPTH, DIM), jnp.float32)}
    _L0_ffn_in = _L0_ffn_setup()

    def _L1_attn_setup():
        import jax, jax.numpy as jnp
        import numpy as np
        NUM_HEADS = 16
        EMBED_DIM = 128
        HEAD_DIM = EMBED_DIM // NUM_HEADS
        ROPE_BASE = 10000.0

        def _split_heads(x):
            B, T, _ = x.shape
            return x.reshape(B, T, NUM_HEADS, HEAD_DIM).transpose(0, 2, 1, 3)

        def _rope(q, k):
            T = q.shape[-2]
            half = HEAD_DIM // 2
            dtype = q.dtype
            pos = jnp.arange(T, dtype=dtype)[:, None]
            idx = jnp.arange(half, dtype=dtype)[None, :]
            inv_freq = 1.0 / ROPE_BASE ** (idx / jnp.asarray(half, dtype))
            angles = pos * inv_freq
            sin = jnp.sin(angles)[None, None]
            cos = jnp.cos(angles)[None, None]

            def rot(x):
                x1, x2 = jnp.split(x, 2, axis=-1)
                return jnp.concatenate([x1 * cos - x2 * sin, x1 * sin + x2 * cos], axis=-1)
            return (rot(q), rot(k))
        key = jax.random.key(seed)
        ks = jax.random.split(key, 5)
        B, T, D = (2, 256, EMBED_DIM)
        s = 1.0 / np.sqrt(D)
        return {'x': jax.random.normal(ks[0], (B, T, D), jnp.float32), 'wq_w': jax.random.normal(ks[1], (D, D), jnp.float32) * s, 'wq_b': jnp.zeros((D,), jnp.float32), 'wk_w': jax.random.normal(ks[2], (D, D), jnp.float32) * s, 'wk_b': jnp.zeros((D,), jnp.float32), 'wv_w': jax.random.normal(ks[3], (D, D), jnp.float32) * s, 'wv_b': jnp.zeros((D,), jnp.float32), 'wo_w': jax.random.normal(ks[4], (D, D), jnp.float32) * s, 'wo_b': jnp.zeros((D,), jnp.float32)}
    _L1_attn_in = _L1_attn_setup()

    def _L1_ffn_setup():
        import jax, jax.numpy as jnp
        import numpy as np
        EPS = 1e-06
        LN_EPS = 1e-05

        def _absmean_core(W):
            gamma = jnp.mean(jnp.abs(W)) + EPS
            Ws = W / gamma
            Wq = jnp.sign(Ws) * jnp.minimum(jnp.round(jnp.abs(Ws)), 1.0)
            return (Wq, gamma)

        @jax.custom_vjp
        def absmean(W):
            return _absmean_core(W)[0]

        def _absmean_fwd(W):
            Wq, gamma = _absmean_core(W)
            return (Wq, gamma)

        def _absmean_bwd(gamma, g):
            return (g / gamma,)
        absmean.defvjp(_absmean_fwd, _absmean_bwd)

        def layernorm(x, w, b, eps=LN_EPS):
            mu = jnp.mean(x, axis=-1, keepdims=True)
            var = jnp.mean((x - mu) ** 2, axis=-1, keepdims=True)
            return (x - mu) * jax.lax.rsqrt(var + eps) * w + b
        key = jax.random.key(seed)
        k1, k2, k3 = jax.random.split(key, 3)
        d, h = (128, 512)
        B, T = (8, 256)
        return {'x': jax.random.normal(k1, (B, T, d), jnp.float32), 'W_fc': jax.random.normal(k2, (h, d), jnp.float32), 'ln_w': jnp.ones((h,), jnp.float32), 'ln_b': jnp.zeros((h,), jnp.float32), 'W_proj': jax.random.normal(k3, (d, h), jnp.float32)}
    _L1_ffn_in = _L1_ffn_setup()
    _d = {'L0_attn_x': _L0_attn_in['x'], 'L0_attn_W_qkv': _L0_attn_in['W_qkv'], 'L0_attn_W_o': _L0_attn_in['W_o'], 'L0_attn_log_gamma': _L0_attn_in['log_gamma'], 'L0_ffn_Wqkv': _L0_ffn_in['Wqkv'], 'L0_ffn_q_scale': _L0_ffn_in['q_scale'], 'L0_ffn_k_scale': _L0_ffn_in['k_scale'], 'L0_ffn_Wo': _L0_ffn_in['Wo'], 'L0_ffn_ln_g': _L0_ffn_in['ln_g'], 'L0_ffn_ln_b': _L0_ffn_in['ln_b'], 'L0_ffn_W1': _L0_ffn_in['W1'], 'L0_ffn_b1': _L0_ffn_in['b1'], 'L0_ffn_W2': _L0_ffn_in['W2'], 'L0_ffn_b2': _L0_ffn_in['b2'], 'L1_attn_wq_w': _L1_attn_in['wq_w'], 'L1_attn_wq_b': _L1_attn_in['wq_b'], 'L1_attn_wk_w': _L1_attn_in['wk_w'], 'L1_attn_wk_b': _L1_attn_in['wk_b'], 'L1_attn_wv_w': _L1_attn_in['wv_w'], 'L1_attn_wv_b': _L1_attn_in['wv_b'], 'L1_attn_wo_w': _L1_attn_in['wo_w'], 'L1_attn_wo_b': _L1_attn_in['wo_b'], 'L1_ffn_W_fc': _L1_ffn_in['W_fc'], 'L1_ffn_ln_w': _L1_ffn_in['ln_w'], 'L1_ffn_ln_b': _L1_ffn_in['ln_b'], 'L1_ffn_W_proj': _L1_ffn_in['W_proj']}
    _x0 = _d['L0_attn_x']
    _d['L0_attn_x'] = jax.random.normal(jax.random.fold_in(jax.random.key(seed), 1), (8, 512, 128), dtype=_x0.dtype)
    del _x0
    return _d

def reference(L0_attn_x, L0_attn_W_qkv, L0_attn_W_o, L0_attn_log_gamma, L0_ffn_Wqkv, L0_ffn_q_scale, L0_ffn_k_scale, L0_ffn_Wo, L0_ffn_ln_g, L0_ffn_ln_b, L0_ffn_W1, L0_ffn_b1, L0_ffn_W2, L0_ffn_b2, L1_attn_wq_w, L1_attn_wq_b, L1_attn_wk_w, L1_attn_wk_b, L1_attn_wv_w, L1_attn_wv_b, L1_attn_wo_w, L1_attn_wo_b, L1_ffn_W_fc, L1_ffn_ln_w, L1_ffn_ln_b, L1_ffn_W_proj):

    def _L0_attn_ref(x, W_qkv, W_o, log_gamma):
        import jax, jax.numpy as jnp
        import numpy as np
        LN_EPS = 1e-05

        def _layernorm(x):
            mu = jnp.mean(x, axis=-1, keepdims=True)
            var = jnp.var(x, axis=-1, keepdims=True)
            return (x - mu) * jax.lax.rsqrt(var + LN_EPS)
        B, L, D = x.shape
        H = log_gamma.shape[0]
        dk = D // H
        qkv = (x @ W_qkv.T).reshape(B, L, 3, H, dk)
        q, k, v = (qkv[:, :, 0], qkv[:, :, 1], qkv[:, :, 2])
        k = _layernorm(k)
        gamma = jax.nn.sigmoid(log_gamma).reshape(1, H, 1, 1)
        qT = jnp.transpose(q, (1, 0, 2, 3))
        kT = jnp.transpose(k, (1, 0, 2, 3))
        vT = jnp.transpose(v, (1, 0, 2, 3))

        def step(S, qkv_t):
            q_t, k_t, v_t = qkv_t
            S = gamma * S + v_t[..., :, None] * k_t[..., None, :]
            y_t = jnp.einsum('bhde,bhe->bhd', S, q_t)
            return (S, y_t)
        S0 = jnp.zeros((B, H, dk, dk), dtype=x.dtype)
        _, ys = jax.lax.scan(step, S0, (qT, kT, vT))
        y = jnp.transpose(ys, (1, 0, 2, 3)).reshape(B, L, D)
        return y @ W_o.T

    def _L0_ffn_ref(x, Wqkv, q_scale, k_scale, Wo, ln_g, ln_b, W1, b1, W2, b2):
        import jax, jax.numpy as jnp
        import numpy as np
        DIM = 128
        DEPTH = 6
        HEADS = 16
        DIM_HEAD = 64
        WINDOW = 32
        INNER = HEADS * DIM_HEAD
        DIM_INNER = int(DIM * 4 * 2 / 3)
        QK_SCALE = 8.0

        def shift_tokens(t):
            a, s = jnp.split(t, 2, -1)
            s = jnp.pad(s, ((0, 0), (1, 0), (0, 0)))[:, :-1]
            return jnp.concatenate([a, s], -1)

        def l2norm(t):
            return t / jnp.maximum(jnp.linalg.norm(t, axis=-1, keepdims=True), 1e-12)

        def rotate_half(x):
            x1, x2 = jnp.split(x, 2, -1)
            return jnp.concatenate([-x2, x1], -1)

        def rotary_tables(n):
            half = jnp.arange(0, DIM_HEAD, 2, dtype=jnp.float32)
            inv_freq = 1.0 / 10000.0 ** (half / DIM_HEAD)
            t = jnp.arange(n, dtype=jnp.float32)
            freqs = t[:, None] * inv_freq[None, :]
            freqs = jnp.concatenate([freqs, freqs], -1)
            base_scale = (half + 0.4 * DIM_HEAD) / (1.4 * DIM_HEAD)
            power = (t - n // 2) / (WINDOW // 2)
            scale = base_scale[None, :] ** power[:, None]
            scale = jnp.concatenate([scale, scale], -1)
            return (freqs, scale)

        def local_attention(q, k, v):
            b, h, n, d = q.shape
            w = WINDOW
            nw = n // w
            bq = q.reshape(b, h, nw, w, d)
            bk = k.reshape(b, h, nw, w, d)
            bv = v.reshape(b, h, nw, w, d)

            def look(t):
                p = jnp.pad(t, ((0, 0), (0, 0), (1, 0), (0, 0), (0, 0)))
                return jnp.concatenate([p[:, :, :nw], p[:, :, 1:]], axis=3)
            bk2, bv2 = (look(bk), look(bv))
            seq = jnp.arange(n).reshape(nw, w)
            seq_p = jnp.pad(seq, ((1, 0), (0, 0)), constant_values=-1)
            jt = jnp.concatenate([seq_p[:nw], seq_p[1:]], axis=1)
            it = seq[:, :, None]
            jb = jt[:, None, :]
            mask = (it < jb) | (it > jb + w) | (jb == -1)
            sim = jnp.einsum('bhwie,bhwje->bhwij', bq, bk2) * QK_SCALE
            sim = jnp.where(mask, -jnp.finfo(sim.dtype).max, sim)
            attn = jax.nn.softmax(sim, -1)
            out = jnp.einsum('bhwij,bhwje->bhwie', attn, bv2)
            return out.reshape(b, h, n, d)

        def attn_layer(x, Wqkv, qs, ksc, Wo):
            b, n, _ = x.shape
            qkv = x @ Wqkv
            q, k, v = jnp.split(qkv, 3, -1)
            sh = lambda t: t.reshape(b, n, HEADS, DIM_HEAD).transpose(0, 2, 1, 3)
            q, k, v = (sh(q), sh(k), sh(v))
            q = l2norm(q) * qs
            k = l2norm(k) * ksc
            freqs, scale = rotary_tables(n)
            cos, sin = (jnp.cos(freqs), jnp.sin(freqs))
            q = q * cos * scale + rotate_half(q) * sin * scale
            inv = 1.0 / scale
            k = k * cos * inv + rotate_half(k) * sin * inv
            out = local_attention(q, k, v)
            out = out.transpose(0, 2, 1, 3).reshape(b, n, INNER)
            return out @ Wo

        def ffn_layer(x, g, bln, W1, b1, W2, b2):
            mu = x.mean(-1, keepdims=True)
            var = ((x - mu) ** 2).mean(-1, keepdims=True)
            xn = (x - mu) / jnp.sqrt(var + 1e-05) * g + bln
            hg = xn @ W1 + b1
            a, gate = jnp.split(hg, 2, -1)
            return a * jax.nn.gelu(gate, approximate=False) @ W2 + b2
        for i in range(DEPTH):
            x = attn_layer(shift_tokens(x), Wqkv[i], q_scale[i], k_scale[i], Wo[i]) + x
            x = ffn_layer(shift_tokens(x), ln_g[i], ln_b[i], W1[i], b1[i], W2[i], b2[i]) + x
        return x

    def _L1_attn_ref(x, wq_w, wq_b, wk_w, wk_b, wv_w, wv_b, wo_w, wo_b):
        import jax, jax.numpy as jnp
        import numpy as np
        NUM_HEADS = 16
        EMBED_DIM = 128
        HEAD_DIM = EMBED_DIM // NUM_HEADS
        ROPE_BASE = 10000.0

        def _split_heads(x):
            B, T, _ = x.shape
            return x.reshape(B, T, NUM_HEADS, HEAD_DIM).transpose(0, 2, 1, 3)

        def _rope(q, k):
            T = q.shape[-2]
            half = HEAD_DIM // 2
            dtype = q.dtype
            pos = jnp.arange(T, dtype=dtype)[:, None]
            idx = jnp.arange(half, dtype=dtype)[None, :]
            inv_freq = 1.0 / ROPE_BASE ** (idx / jnp.asarray(half, dtype))
            angles = pos * inv_freq
            sin = jnp.sin(angles)[None, None]
            cos = jnp.cos(angles)[None, None]

            def rot(x):
                x1, x2 = jnp.split(x, 2, axis=-1)
                return jnp.concatenate([x1 * cos - x2 * sin, x1 * sin + x2 * cos], axis=-1)
            return (rot(q), rot(k))
        B, T, D = x.shape
        q = _split_heads(x @ wq_w + wq_b)
        k = _split_heads(x @ wk_w + wk_b)
        v = _split_heads(x @ wv_w + wv_b)
        q, k = _rope(q, k)
        scale = HEAD_DIM ** (-0.5)
        logits = jnp.einsum('bhqd,bhkd->bhqk', q, k) * scale
        attn = jax.nn.softmax(logits, axis=-1)
        y = jnp.einsum('bhqk,bhkd->bhqd', attn, v)
        y = y.transpose(0, 2, 1, 3).reshape(B, T, D)
        return y @ wo_w + wo_b

    def _L1_ffn_ref(x, W_fc, ln_w, ln_b, W_proj):
        import jax, jax.numpy as jnp
        import numpy as np
        EPS = 1e-06
        LN_EPS = 1e-05

        def _absmean_core(W):
            gamma = jnp.mean(jnp.abs(W)) + EPS
            Ws = W / gamma
            Wq = jnp.sign(Ws) * jnp.minimum(jnp.round(jnp.abs(Ws)), 1.0)
            return (Wq, gamma)

        @jax.custom_vjp
        def absmean(W):
            return _absmean_core(W)[0]

        def _absmean_fwd(W):
            Wq, gamma = _absmean_core(W)
            return (Wq, gamma)

        def _absmean_bwd(gamma, g):
            return (g / gamma,)
        absmean.defvjp(_absmean_fwd, _absmean_bwd)

        def layernorm(x, w, b, eps=LN_EPS):
            mu = jnp.mean(x, axis=-1, keepdims=True)
            var = jnp.mean((x - mu) ** 2, axis=-1, keepdims=True)
            return (x - mu) * jax.lax.rsqrt(var + eps) * w + b
        h = jnp.einsum('btd,hd->bth', x, absmean(W_fc))
        h = jax.nn.gelu(h, approximate=False)
        h = layernorm(h, ln_w, ln_b)
        return jnp.einsum('bth,dh->btd', h, absmean(W_proj))
    x = L0_attn_x
    xn = _layernorm(x, axis=-1)
    x = x + _L0_attn_ref(xn, L0_attn_W_qkv, L0_attn_W_o, L0_attn_log_gamma) + _L0_ffn_ref(xn, L0_ffn_Wqkv, L0_ffn_q_scale, L0_ffn_k_scale, L0_ffn_Wo, L0_ffn_ln_g, L0_ffn_ln_b, L0_ffn_W1, L0_ffn_b1, L0_ffn_W2, L0_ffn_b2)
    xn = _layernorm(x, axis=-1)
    x = x + _L1_attn_ref(xn, L1_attn_wq_w, L1_attn_wq_b, L1_attn_wk_w, L1_attn_wk_b, L1_attn_wv_w, L1_attn_wv_b, L1_attn_wo_w, L1_attn_wo_b) + _L1_ffn_ref(xn, L1_ffn_W_fc, L1_ffn_ln_w, L1_ffn_ln_b, L1_ffn_W_proj)
    return x

_drawn_inputs = setup_inputs


def setup_inputs(seed=0):
    import zlib

    import numpy as np

    out = dict(_drawn_inputs(seed))
    spreads = {'L0_attn_log_gamma': (0.0, 2.0),
     'L0_ffn_q_scale': (1.0, 0.6),
     'L0_ffn_k_scale': (1.0, 0.6),
     'L0_ffn_ln_g': (1.0, 0.6),
     'L0_ffn_ln_b': (0.0, 0.8),
     'L0_ffn_b1': (0.0, 0.799),
     'L0_ffn_b2': (0.0, 0.1),
     'L1_attn_wq_b': (0.0, 0.8),
     'L1_attn_wk_b': (0.0, 0.8),
     'L1_attn_wv_b': (0.0, 0.8),
     'L1_attn_wo_b': (0.0, 2.0),
     'L1_ffn_ln_w': (1.0, 0.2),
     'L1_ffn_ln_b': (0.0, 0.1)}
    factors = {'L0_ffn_W1': 3.091,
     'L0_ffn_W2': 3.024,
     'L1_attn_wq_w': 8.0,
     'L1_attn_wk_w': 8.0,
     'L1_attn_wv_w': 7.462,
     'L1_attn_wo_w': 5.956}
    for name, (base, spread) in spreads.items():
        noise = np.random.default_rng([zlib.crc32(name.encode()), seed]).standard_normal(out[name].shape)
        drawn = base * np.exp(spread * noise) if base else spread * noise
        out[name] = jnp.asarray(drawn.astype(out[name].dtype))
    for name, factor in factors.items():
        out[name] = (out[name] * factor).astype(out[name].dtype)
    return out
```

```python
import concourse.bass as bass
from concourse import mybir
from contextlib import ExitStack
import numpy as np

FP32 = mybir.dt.float32
BF16 = mybir.dt.bfloat16
ALU = mybir.AluOpType
ACT = mybir.ActivationFunctionType
AX = mybir.AxisListType

D = 128
SEQS = 8
L = 512
TOK = SEQS * L
CH = 512
TILE = 128
TPS = L // TILE
HEADS = 16
DK = D // HEADS
SLOT = 32
QUADS = HEADS * SLOT // 128
LN_EPS = 1e-5

DEPTH = 6
DH = 64
INNER = HEADS * DH
PAIRS = HEADS // 2
WIN = 32
WPT = TILE // WIN
HID = 341
HT = 3
HW = [128, 128, HID - 256]
PAD = 64
SEQP = L + 1
XCOLS = PAD + (SEQS + 1) * SEQP
MLP = 512
MT = MLP // 128


def col(b, t=0):
    return b * SEQP + (PAD + 1 + t)


def stand_alone(engine, passed):
    engine.sem_inc(passed, 1)


def layernorm_stage(nc, ps, sem, tag, src, dst, ones, eps, src2=None):
    with ExitStack() as c:
        sq = c.enter_context(nc.sbuf_tensor(f"sq_{tag}", [128, TOK], FP32))
        sd = c.enter_context(nc.sbuf_tensor(f"sd_{tag}", [128, TOK], FP32))
        summed = sem(f"summed_{tag}")
        mean_done = sem(f"mean_done_{tag}")
        centered = sem(f"centered_{tag}")
        squared = sem(f"squared_{tag}")
        var_done = sem(f"var_done_{tag}")
        std_done = sem(f"std_done_{tag}")
        rstd_done = sem(f"rstd_done_{tag}")
        with nc.Block() as block:

            @block.tensor
            def _(pe):
                with pe.Fori(0, SEQS) as i:
                    if src2 is not None:
                        pe.wait_ge(summed, i + 1)
                    nc.tensor.matmul(ps[:, bass.ds(i * CH, CH)], ones[:, :], src(i),
                                     start=True, stop=True).then_inc(mean_done, 1)
                with pe.Fori(0, SEQS) as i:
                    pe.wait_ge(squared, i + 1)
                    nc.tensor.matmul(ps[:, bass.ds(i * CH, CH)], ones[:, :], sq[:, bass.ds(i * CH, CH)],
                                     start=True, stop=True).then_inc(var_done, 1)

            @block.vector
            def _(dve):
                if src2 is not None:
                    with dve.Fori(0, SEQS) as i:
                        nc.vector.tensor_tensor(src(i), src(i), src2(i), ALU.add).then_inc(summed, 1)
                with dve.Fori(0, SEQS) as i:
                    dve.wait_ge(mean_done, i + 1)
                    nc.vector.tensor_tensor(dst(i), src(i), ps[:, bass.ds(i * CH, CH)],
                                            ALU.subtract).then_inc(centered, 1)
                with dve.Fori(0, SEQS) as i:
                    dve.wait_ge(std_done, i + 1)
                    nc.vector.reciprocal(sd[:, bass.ds(i * CH, CH)],
                                         sd[:, bass.ds(i * CH, CH)]).then_inc(rstd_done, 1)
                with dve.Fori(0, SEQS) as i:
                    dve.wait_ge(rstd_done, i + 1)
                    nc.vector.tensor_tensor(dst(i), dst(i), sd[:, bass.ds(i * CH, CH)], ALU.mult)

            @block.scalar
            def _(act):
                with act.Fori(0, SEQS) as i:
                    act.wait_ge(centered, i + 1)
                    nc.scalar.activation(sq[:, bass.ds(i * CH, CH)], dst(i), ACT.Square).then_inc(squared, 1)
                with act.Fori(0, SEQS) as i:
                    act.wait_ge(var_done, i + 1)
                    nc.scalar.activation(sd[:, bass.ds(i * CH, CH)], ps[:, bass.ds(i * CH, CH)], ACT.Sqrt,
                                         bias=eps[:, 0:1]).then_inc(std_done, 1)



def retention_stage(nc, ps, sem, w, xn, xr, eps):
    with ExitStack() as c:
        def sb(name, shape, dt=FP32):
            return c.enter_context(nc.sbuf_tensor(f"ret_{name}", shape, dt))

        wq = sb("wq", [128, 512])
        wk = sb("wk", [128, 512])
        wkc = sb("wkc", [128, 128])
        wv = sb("wv", [128, 512])
        wo = sb("wo", [128, QUADS, 128])
        small = sb("small", [128, HEADS])
        gam = sb("gam", [128, HEADS])
        lag = sb("lag", [128, L])
        decay = sb("decay", [128, HEADS, L])
        xcur = sb("xcur", [128, L])
        qt = sb("qt", [128, QUADS, L])
        kt = sb("kt", [128, QUADS, L])
        vp = sb("vp", [128, TPS, 512])
        ksq = sb("ksq", [128, TPS, 128])
        krs = sb("krs", [128, TPS, HEADS])
        at = sb("at", [128, 2, TPS, L])
        yt = sb("yt", [128, QUADS, L])
        loaded = sem("ret_loaded")
        prep = sem("ret_prep")
        w_ready = sem("ret_w_ready")
        neg_ready = sem("ret_neg_ready")
        exp_ready = sem("ret_exp_ready")
        gamma_ready = sem("ret_gamma_ready")
        ln_ready = sem("ret_ln_ready")
        power_ready = sem("ret_power_ready")
        decay_ready = sem("ret_decay_ready")
        x_ready = sem("ret_x_ready")
        proj_done = sem("ret_proj_done")
        qk_read = sem("ret_qk_read")
        ksq_done = sem("ret_ksq_done")
        ksum_done = sem("ret_ksum_done")
        kstd_done = sem("ret_kstd_done")
        krs_done = sem("ret_krs_done")
        v_ready = sem("ret_v_ready")
        scores_done = sem("ret_scores_done")
        weights_done = sem("ret_weights_done")
        y_done = sem("ret_y_done")
        y_read = sem("ret_y_read")
        out_done = sem("ret_out_done")
        out_read = sem("ret_out_read")

        PQ = [ps[:, 0:CH], ps[:, CH:2 * CH]]
        PS = [ps[:, (2 + j) * CH:(3 + j) * CH] for j in range(TPS)]
        PY = ps[:, 6 * CH:7 * CH]
        PO = ps[:, 7 * CH:8 * CH]
        NQK = 2 * QUADS
        UNITS = NQK + 2 * TPS

        with nc.Block() as block:

            @block.sync
            def _(sp):
                sp.dma_start(wq[:, :], w["ret_wq"]).then_inc(loaded, 16)
                sp.dma_start(wkc[:, :], w["ret_wk"]).then_inc(loaded, 16)
                sp.dma_start(wv[:, :], w["ret_wv"]).then_inc(loaded, 16)
                sp.dma_start(wo[:, :, :], w["ret_wo"]).then_inc(loaded, 16)
                sp.dma_start(gam[:, :], w["log_gamma"].partition_broadcast(128)).then_inc(loaded, 16)
                sp.dma_start(lag[:, :], w["c_lag"]).then_inc(loaded, 16)

            @block.gpsimd
            def _(pool):
                nc.gpsimd.tensor_copy(xcur[:, :], xn(0)).then_inc(x_ready, 1)
                pool.wait_ge(power_ready, 1)
                nc.gpsimd.affine_select(out=decay[:, :, :], in_=decay[:, :, :], compare_op=ALU.is_ge, fill=0.0,
                                        base=0, pattern=[[0, HEADS], [1, L]],
                                        channel_multiplier=-1).then_inc(decay_ready, 1)
                with pool.Fori(1, SEQS) as b:
                    pool.wait_ge(proj_done, b * UNITS)
                    nc.gpsimd.tensor_copy(xcur[:, :], xn(b)).then_inc(x_ready, 1)

            @block.tensor
            def _(pe):
                def score(b, h):
                    g, r = h // 4, SLOT * (h % 4)
                    for j in range(TPS):
                        pe.wait_ge(weights_done, (b * HEADS + h) * TPS + (0 if h == 0 else j + 1 - TPS))
                        nc.tensor.matmul(PS[j][:, 0:L - j * TILE],
                                         kt[r:r + SLOT, g, j * TILE:(j + 1) * TILE],
                                         qt[r:r + SLOT, g, j * TILE:L], start=True, stop=True).then_inc(scores_done, 1)

                def weigh(b, h):
                    g, r = h // 4, SLOT * (h % 4)
                    if h % 4 == 0:
                        pe.wait_ge(y_read, b * QUADS + g)
                    for j in range(TPS):
                        pe.wait_ge(weights_done, (b * HEADS + h) * TPS + (j + 1))
                        last = nc.tensor.matmul(PY[r:r + SLOT, j * TILE:L], vp[:, j, h * SLOT:(h + 1) * SLOT],
                                                at[:, h % 2, j, 0:L - j * TILE],
                                                start=(j == 0), stop=(j == TPS - 1))
                    last.then_inc(y_done, 1)

                pe.wait_ge(w_ready, 1)
                with pe.Fori(0, SEQS) as b:
                    pe.wait_ge(x_ready, b + 1)
                    for u in range(UNITS):
                        if u == 0:
                            pe.wait_ge(ksq_done, b * TPS)
                        elif u == 1:
                            pe.wait_ge(v_ready, b * TPS)
                        elif u < NQK + 2:
                            pe.wait_ge(qk_read, b * NQK + (u - 1))
                        else:
                            pe.wait_ge((ksq_done, v_ready)[u % 2], b * TPS + (u - NQK) // 2)
                        if u < NQK:
                            g = u // 2
                            nc.tensor.matmul(PQ[u % 2], (wq, wk)[u % 2][:, g * 128:(g + 1) * 128], xcur[:, :],
                                             start=True, stop=True).then_inc(proj_done, 1)
                        else:
                            t = (u - NQK) // 2
                            rhs, n = ((wkc, 128), (wv, 512))[u % 2]
                            nc.tensor.matmul(PQ[u % 2][:, 0:n], xcur[:, t * TILE:(t + 1) * TILE], rhs[:, :],
                                             start=True, stop=True).then_inc(proj_done, 1)
                    pe.wait_ge(v_ready, b * TPS + TPS)
                    pe.wait_ge(qk_read, b * NQK + NQK)
                    score(b, 0)
                    for h in range(1, HEADS):
                        score(b, h)
                        weigh(b, h - 1)
                    weigh(b, HEADS - 1)
                    pe.wait_ge(y_read, b * QUADS + QUADS)
                    pe.wait_ge(out_read, b)
                    for g in range(QUADS):
                        last = nc.tensor.matmul(PO, wo[:, g, :], yt[:, g, :],
                                                start=(g == 0), stop=(g == QUADS - 1))
                    last.then_inc(out_done, 1)

            @block.vector
            def _(dve):
                steps = [0]

                def link(ins):
                    steps[0] += 1
                    ins.then_inc(prep, 1)
                    dve.wait_ge(prep, steps[0])

                dve.wait_ge(loaded, 96)
                wk3 = wkc[:, :].rearrange("p (h d) -> p h d", d=DK)
                link(nc.vector.tensor_reduce(small[:, :], wk3, AX.X, ALU.add))
                link(nc.vector.tensor_scalar(small[:, :], small[:, :], 1.0 / DK, None, ALU.mult))
                link(nc.vector.memset(wk[:, :], 0.0))
                link(nc.vector.tensor_tensor(wk3, wk3, small[:, :].unsqueeze(2).broadcast_to([128, HEADS, DK]),
                                             ALU.subtract))
                nc.vector.tensor_copy(wk[:, :].rearrange("p (h s) -> p h s", s=SLOT)[:, :, 0:DK],
                                      wk3).then_inc(w_ready, 1)
                link(nc.vector.tensor_scalar(gam[:, :], gam[:, :], -1.0, 80.0, ALU.mult, ALU.min))
                nc.vector.tensor_scalar(gam[:, :], gam[:, :], -80.0, None, ALU.max).then_inc(neg_ready, 1)
                dve.wait_ge(exp_ready, 1)
                link(nc.vector.tensor_scalar(gam[:, :], gam[:, :], 1.0, None, ALU.add))
                link(nc.vector.reciprocal(gam[:, :], gam[:, :]))
                nc.vector.tensor_scalar(gam[:, :], gam[:, :], 2.0 ** -64, None, ALU.max).then_inc(gamma_ready, 1)
                with dve.Fori(0, SEQS) as b:
                    for u in range(UNITS):
                        dve.wait_ge(proj_done, b * UNITS + (u + 1))
                        t = (u - NQK) // 2
                        if u < NQK:
                            nc.vector.tensor_copy((qt, kt)[u % 2][:, u // 2, :], PQ[u % 2]).then_inc(qk_read, 1)
                        elif u % 2 == 0:
                            dve.wait_ge(ksq_done, b * TPS + (t + 1))
                            nc.vector.tensor_reduce(krs[:, t, :], ksq[:, t, :].rearrange("p (h d) -> p h d", d=DK),
                                                    AX.X, ALU.add).then_inc(ksum_done, 1)
                        else:
                            dve.wait_ge(kstd_done, b * TPS + (t + 1))
                            nc.vector.reciprocal(krs[:, t, :], krs[:, t, :]).then_inc(krs_done, 1)
                            dve.wait_ge(krs_done, b * TPS + (t + 1))
                            nc.vector.tensor_tensor(vp[:, t, :].rearrange("p (h s) -> p h s", s=SLOT),
                                                    PQ[1].rearrange("p (h s) -> p h s", s=SLOT),
                                                    krs[:, t, :].unsqueeze(2).broadcast_to([128, HEADS, SLOT]),
                                                    ALU.mult).then_inc(v_ready, 1)
                    dve.wait_ge(decay_ready, 1)
                    for h in range(HEADS):
                        for j in range(TPS):
                            dve.wait_ge(scores_done, (b * HEADS + h) * TPS + (j + 1))
                            if j == 0 and h >= 2:
                                dve.wait_ge(y_done, b * HEADS + (h - 1))
                            n = L - j * TILE
                            nc.vector.tensor_tensor(at[:, h % 2, j, 0:n], PS[j][:, 0:n], decay[:, h, 0:n],
                                                    ALU.mult).then_inc(weights_done, 1)
                    dve.wait_ge(out_done, b + 1)
                    nc.vector.tensor_tensor(xr(b), xr(b), PO, ALU.add).then_inc(out_read, 1)

            @block.scalar
            def _(act):
                act.wait_ge(neg_ready, 1)
                nc.scalar.activation(gam[:, :], gam[:, :], ACT.Exp).then_inc(exp_ready, 1)
                act.wait_ge(gamma_ready, 1)
                nc.scalar.activation(small[:, :], gam[:, :], ACT.Ln).then_inc(ln_ready, 1)
                act.wait_ge(ln_ready, 1)
                for h in range(HEADS):
                    last = nc.scalar.activation(decay[:, h, :], lag[:, :], ACT.Exp, scale=small[:, h:h + 1])
                last.then_inc(power_ready, 1)
                with act.Fori(0, SEQS) as b:
                    for t in range(TPS):
                        act.wait_ge(proj_done, b * UNITS + (NQK + 2 * t + 1))
                        nc.scalar.activation(ksq[:, t, :], PQ[0][:, 0:128], ACT.Square).then_inc(ksq_done, 1)
                        act.wait_ge(ksum_done, b * TPS + (t + 1))
                        nc.scalar.activation(krs[:, t, :], krs[:, t, :], ACT.Sqrt, scale=1.0 / DK,
                                             bias=eps[:, 0:1]).then_inc(kstd_done, 1)
                    for g in range(QUADS):
                        act.wait_ge(y_done, b * HEADS + 4 * (g + 1))
                        nc.scalar.activation(yt[:, g, :], PY, ACT.Copy).then_inc(y_read, 1)


def softmax_stage(nc, ps, sem, w, xn, xr, ident):
    with ExitStack() as c:
        def sb(name, shape, dt=FP32):
            return c.enter_context(nc.sbuf_tensor(f"sm_{name}", shape, dt))

        NP = 4 * QUADS
        wp = sb("wp", [128, 4, 512])
        bp = sb("bp", [128, 4, QUADS])
        wv = sb("wv", [128, 512])
        bv = sb("bv", [128, 512])
        wo = sb("wo", [128, QUADS, 128])
        bo = sb("bo", [128, 1])
        rope = sb("rope", [128, 4, L])
        bsel = sb("bsel", [128, 128])
        xcur = sb("xcur", [128, L])
        qk = sb("qk", [128, 2 * QUADS, L])
        part = sb("part", [128, 2 * QUADS, L])
        vp = sb("vp", [128, TPS, 512])
        nmax = sb("nmax", [128, QUADS, TPS, 128])
        pt = sb("pt", [128, 2, TPS, L])
        yt = sb("yt", [128, QUADS, L])
        rden = sb("rden", [128, QUADS, L])
        loaded = sem("sm_loaded")
        nmax_zero = sem("sm_nmax_zero")
        pool_passed = sem("sm_pool_passed")
        x_ready = sem("sm_x_ready")
        proj_done = sem("sm_proj_done")
        proj_read = sem("sm_proj_read")
        rot_ready = sem("sm_rot_ready")
        scores_done = sem("sm_scores_done")
        max_done = sem("sm_max_done")
        maxt_done = sem("sm_maxt_done")
        q_ready = sem("sm_q_ready")
        keyed_done = sem("sm_keyed_done")
        exp_done = sem("sm_exp_done")
        y_done = sem("sm_y_done")
        y_read = sem("sm_y_read")
        den_done = sem("sm_den_done")
        rden_done = sem("sm_rden_done")
        norm_done = sem("sm_norm_done")
        out_done = sem("sm_out_done")
        out_read = sem("sm_out_read")

        PQ = [ps[:, 0:CH], ps[:, CH:2 * CH]]
        PS = [ps[:, (2 + j) * CH:(3 + j) * CH] for j in range(TPS)]
        PY = ps[:, 6 * CH:7 * CH]
        PO = ps[:, 7 * CH:8 * CH]
        UNITS = NP + TPS

        with nc.Block() as block:

            @block.sync
            def _(sp):
                for dst, name in ((wp[:, :, :], "sm_wp"), (bp[:, :, :], "sm_bp"), (wv[:, :], "sm_wv"),
                                  (wo[:, :, :], "sm_wo"), (bo[:, :], "sm_bo"), (rope[:, :, :], "c_rope"),
                                  (bsel[:, :], "c_bsel")):
                    sp.dma_start(dst, w[name]).then_inc(loaded, 16)
                sp.dma_start(bv[:, :], w["sm_bv"].partition_broadcast(128)).then_inc(loaded, 16)

            @block.gpsimd
            def _(pool):
                nc.gpsimd.memset(nmax[:, :, :, :], 0.0).then_inc(nmax_zero, 1)
                nc.gpsimd.tensor_copy(xcur[:, :], xn(0)).then_inc(x_ready, 1)
                with pool.Fori(0, SEQS) as b:
                    for i in range(2 * QUADS):
                        pool.wait_ge(proj_read, b * UNITS + 2 * (i + 1))
                        nc.gpsimd.tensor_tensor(qk[:, i, :], qk[:, i, :], part[:, i, :],
                                                ALU.add).then_inc(rot_ready, 1)
                    pool.wait_ge(proj_done, b * UNITS + UNITS)
                    stand_alone(pool, pool_passed)
                    nc.gpsimd.tensor_copy(xcur[:, :], xn(b + 1)).then_inc(x_ready, 1)

            @block.tensor
            def _(pe):
                def maxima(b, g):
                    if g == 0:
                        pe.wait_ge(rot_ready, b * 2 * QUADS + 2 * QUADS)
                        pe.wait_ge(rden_done, b * QUADS)
                    elif g == 1:
                        pe.wait_ge(max_done, b * HEADS * TPS + 4 * TPS)
                    else:
                        pe.wait_ge(exp_done, b * HEADS * TPS + 4 * (g - 1) * TPS)
                    for i in range(TPS):
                        for r in range(4):
                            n = (g * TPS + i) * 4 + r
                            if i:
                                pe.wait_ge(max_done, b * HEADS * TPS + (n - 3))
                            nc.tensor.matmul(PS[r], qk[r * SLOT:(r + 1) * SLOT, g, i * TILE:(i + 1) * TILE],
                                             qk[r * SLOT:(r + 1) * SLOT, QUADS + g, :],
                                             start=True, stop=True).then_inc(scores_done, 1)

                def transposed_maxima(b, g):
                    pe.wait_ge(max_done, b * HEADS * TPS + (g + 1) * 4 * TPS)
                    if g == 0:
                        pe.wait_ge(out_read, b)
                    else:
                        pe.wait_ge(q_ready, b * QUADS + g)
                    for i in range(TPS):
                        last = nc.tensor.transpose(PO[:, i * TILE:(i + 1) * TILE], nmax[:, g, i, :], ident[:, :])
                    last.then_inc(maxt_done, 1)

                def keyed(b, h):
                    g, r = h // 4, SLOT * (h % 4)
                    if r == 0:
                        pe.wait_ge(q_ready, b * QUADS + (g + 1))
                        if g + 1 < QUADS:
                            pe.wait_ge(max_done, b * HEADS * TPS + (g + 2) * 4 * TPS)
                        else:
                            pe.wait_ge(exp_done, (b * HEADS + h) * TPS)
                    for j in range(TPS):
                        if r:
                            pe.wait_ge(exp_done, (b * HEADS + h) * TPS + (j + 1 - TPS))
                        nc.tensor.matmul(PS[j], qk[r:r + SLOT, QUADS + g, j * TILE:(j + 1) * TILE],
                                         qk[r:r + SLOT, g, :], start=True, stop=True).then_inc(keyed_done, 1)

                def weigh(b, h):
                    g, r = h // 4, SLOT * (h % 4)
                    if r == 0:
                        pe.wait_ge(y_read, b * QUADS + g)
                    for j in range(TPS):
                        pe.wait_ge(exp_done, (b * HEADS + h) * TPS + (j + 1))
                        last = nc.tensor.matmul(PY[r:r + SLOT, :], vp[:, j, h * SLOT:(h + 1) * SLOT],
                                                pt[:, h % 2, j, :], start=(j == 0), stop=(j == TPS - 1))
                    last.then_inc(y_done, 1)

                pe.wait_ge(loaded, 128)
                pe.wait_ge(nmax_zero, 1)
                with pe.Fori(0, SEQS) as b:
                    pe.wait_ge(x_ready, b + 1)
                    for u in range(UNITS):
                        pe.wait_ge(proj_read, b * UNITS + max(u - 1, 0))
                        if u < NP:
                            g, kind = (u // 2) % QUADS, 2 * (u // (2 * QUADS)) + u % 2
                            nc.tensor.matmul(PQ[u % 2], wp[:, kind, g * 128:(g + 1) * 128], xcur[:, :],
                                             start=True, stop=True).then_inc(proj_done, 1)
                        else:
                            t = u - NP
                            nc.tensor.matmul(PQ[u % 2], xcur[:, t * TILE:(t + 1) * TILE], wv[:, :],
                                             start=True, stop=True).then_inc(proj_done, 1)
                    maxima(b, 0)
                    pe.wait_ge(proj_read, b * UNITS + UNITS)
                    for h in range(HEADS):
                        if h % 4 == 0:
                            if h // 4 + 1 < QUADS:
                                maxima(b, h // 4 + 1)
                            transposed_maxima(b, h // 4)
                        keyed(b, h)
                        if h:
                            weigh(b, h - 1)
                    weigh(b, HEADS - 1)
                    for g in range(QUADS):
                        pe.wait_ge(y_read, b * QUADS + (g + 1))
                        nc.tensor.matmul(PS[g], bsel[:, :], yt[:, g, :], start=True, stop=True).then_inc(den_done, 1)
                    for g in range(QUADS):
                        pe.wait_ge(norm_done, b * QUADS + (g + 1))
                        last = nc.tensor.matmul(PO, wo[:, g, :], yt[:, g, :], start=(g == 0), stop=(g == QUADS - 1))
                    last.then_inc(out_done, 1)

            @block.vector
            def _(dve):
                dve.wait_ge(loaded, 128)
                dve.wait_ge(nmax_zero, 1)
                with dve.Fori(0, SEQS) as b:
                    for u in range(UNITS):
                        dve.wait_ge(proj_done, b * UNITS + (u + 1))
                        if u < NP:
                            g, kind = (u // 2) % QUADS, 2 * (u // (2 * QUADS)) + u % 2
                            nc.vector.scalar_tensor_tensor((qk, part)[u % 2][:, u // 2, :], PQ[u % 2],
                                                           bp[:, kind, g:g + 1], rope[:, kind, :], ALU.add,
                                                           ALU.mult).then_inc(proj_read, 1)
                        else:
                            nc.vector.tensor_tensor(vp[:, u - NP, :], PQ[u % 2], bv[:, :],
                                                    ALU.add).then_inc(proj_read, 1)

                    def take_maxima(g):
                        for i in range(TPS):
                            for r in range(4):
                                n = (g * TPS + i) * 4 + r
                                dve.wait_ge(scores_done, b * HEADS * TPS + (n + 1))
                                nc.vector.tensor_reduce(nmax[:, g, i, r * SLOT + DK:r * SLOT + DK + 1], PS[r],
                                                        AX.X, ALU.max, negate=True).then_inc(max_done, 1)

                    take_maxima(0)
                    for g in range(QUADS):
                        if g + 1 < QUADS:
                            take_maxima(g + 1)
                        dve.wait_ge(maxt_done, b * QUADS + (g + 1))
                        nc.vector.tensor_tensor(qk[:, g, :], qk[:, g, :], PO, ALU.add).then_inc(q_ready, 1)
                    for g in range(QUADS):
                        dve.wait_ge(den_done, b * QUADS + (g + 1))
                        nc.vector.reciprocal(rden[:, g, :], PS[g]).then_inc(rden_done, 1)
                    for g in range(QUADS):
                        dve.wait_ge(rden_done, b * QUADS + (g + 1))
                        nc.vector.tensor_tensor(yt[:, g, :], yt[:, g, :], rden[:, g, :], ALU.mult).then_inc(norm_done, 1)
                    dve.wait_ge(out_done, b + 1)
                    nc.vector.scalar_tensor_tensor(xr(b), PO, bo[:, 0:1], xr(b), ALU.add, ALU.add).then_inc(out_read, 1)

            @block.scalar
            def _(act):
                with act.Fori(0, SEQS) as b:
                    for h in range(HEADS):
                        for j in range(TPS):
                            act.wait_ge(keyed_done, (b * HEADS + h) * TPS + (j + 1))
                            if j == 0 and h >= 2:
                                act.wait_ge(y_done, b * HEADS + (h - 1))
                            nc.scalar.activation(pt[:, h % 2, j, :], PS[j], ACT.Exp).then_inc(exp_done, 1)
                        if h % 4 == 3:
                            g = h // 4
                            act.wait_ge(y_done, b * HEADS + (h + 1))
                            nc.scalar.activation(yt[:, g, :], PY, ACT.Copy).then_inc(y_read, 1)

def transformer_stage(nc, ps, sem, w, xa, xb, ones, eps, ident):
    with ExitStack() as c:
        def sb(name, shape, dt=FP32):
            return c.enter_context(nc.sbuf_tensor(f"tr_{name}", shape, dt))

        NQKV = TPS * SEQS + 1
        UNITS = 8
        QKV0 = 3 * INNER

        wqkv = sb("wqkv", [128, QKV0])
        wo = sb("wo", [128, PAIRS, 128])
        w1 = sb("w1", [128, 2 * HID])
        w2 = sb("w2", [128, HT, 128])
        b1 = sb("b1", [128, 2 * HT])
        b2 = sb("b2", [128, 1])
        lng = sb("lng", [128, 1])
        lnb = sb("lnb", [128, 1])
        qks = sb("qks", [128, 2, DH])
        base = sb("base", [128, 4, TPS, DH])
        rope = sb("rope", [128, 4, TPS, DH])
        identb = sb("identb", [128, 128], BF16)
        mask = sb("mask", [128, 2, PAIRS * 2 * WIN], BF16)
        half = sb("half", [128, 2 * HEADS])
        xs = sb("xs", [128, 2, WIN + TILE])
        va = sb("va", [128, 2, INNER])
        vb = sb("vb", [128, 2, INNER])
        qm = sb("qm", [128, 2, 4, CH])
        raw = sb("raw", [128, 4, CH])
        ss = sb("ss", [128, 2 * HEADS])
        rn = sb("rn", [128, 2, 2 * HEADS])
        qt = sb("qt", [128, PAIRS, TILE])
        kt = sb("kt", [128, 2, PAIRS, WIN + TILE])
        mx = sb("mx", [128, 2, PAIRS])
        nb = sb("nb", [128, 2, PAIRS])
        pw = sb("pw", [128, HEADS + 1, 2 * WIN])
        rs = sb("rs", [128, HEADS])
        rr = sb("rr", [128, HEADS])
        pt = sb("pt", [128, HEADS, TILE])
        on = sb("on", [128, INNER])
        ot = sb("ot", [128, PAIRS, L])
        xf = sb("xf", [128, TOK])
        hb = sb("hb", [128, 2, HT, CH])
        fsq = ot[:, :, :].rearrange("p a b -> p (a b)")
        fsd = qm[:, :, :, :].rearrange("p a b c -> p (a b c)")

        const_loaded = sem("tr_const_loaded")
        pe_passed = sem("tr_pe_passed")
        dve_passed = sem("tr_dve_passed")
        pool_passed = sem("tr_pool_passed")
        attn_loaded = sem("tr_attn_loaded")
        mlp_loaded = sem("tr_mlp_loaded")
        init_done = sem("tr_init_done")
        scales_done = sem("tr_scales_done")
        xs_ready = sem("tr_xs_ready")
        proj_done = sem("tr_proj_done")
        v_copied = sem("tr_v_copied")
        rot_done = sem("tr_rot_done")
        raw_ready = sem("tr_raw_ready")
        sq_done = sem("tr_sq_done")
        ss_done = sem("tr_ss_done")
        pool_step = sem("tr_pool_step")
        q_ready = sem("tr_q_ready")
        norms_ready = sem("tr_norms_ready")
        k_ready = sem("tr_k_ready")
        turn_done = sem("tr_turn_done")
        turn_read = sem("tr_turn_read")
        kprev_done = sem("tr_kprev_done")
        scores_done = sem("tr_scores_done")
        max_done = sem("tr_max_done")
        bias_ready = sem("tr_bias_ready")
        exp_done = sem("tr_exp_done")
        again_done = sem("tr_again_done")
        pv_done = sem("tr_pv_done")
        rsum_done = sem("tr_rsum_done")
        on_ready = sem("tr_on_ready")
        wo_done = sem("tr_wo_done")
        xb_ready = sem("tr_xb_ready")
        xf_ready = sem("tr_xf_ready")
        mean_done = sem("tr_mean_done")
        centered = sem("tr_centered")
        squared = sem("tr_squared")
        var_done = sem("tr_var_done")
        std_done = sem("tr_std_done")
        rstd_done = sem("tr_rstd_done")
        normed = sem("tr_normed")
        xn_ready = sem("tr_xn_ready")
        hid_done = sem("tr_hid_done")
        gelu_done = sem("tr_gelu_done")
        hid_ready = sem("tr_hid_ready")
        mlp_done = sem("tr_mlp_done")
        xa_ready = sem("tr_xa_ready")

        P2 = [ps[:, 0:CH], ps[:, CH:2 * CH]]
        PT = [ps[:, 2 * CH:3 * CH], ps[:, 3 * CH:4 * CH]]
        PS = [ps[:, 4 * CH:5 * CH], ps[:, 5 * CH:6 * CH]]
        PV = [ps[:, 6 * CH:7 * CH], ps[:, 7 * CH:8 * CH]]
        TURNS = 10
        MLPU = 2 * HT

        attn_weights = ((wqkv[:, :], "tr_wqkv"), (wo[:, :, :].rearrange("p a b -> p (a b)"), "tr_wo"))
        mlp_weights = ((w1[:, :], "tr_w1"), (w2[:, :, :].rearrange("p a b -> p (a b)"), "tr_w2"),
                       (b1[:, :], "tr_b1"), (b2[:, :], "tr_b2"), (lng[:, :], "tr_lng"), (lnb[:, :], "tr_lnb"))
        CONST_LOADS = 48
        ATTN_LOADS = 16 * (len(attn_weights) + 1)
        MLP_LOADS = 16 * len(mlp_weights)

        def tile_heads(ap):
            return ap.rearrange("p (h d) -> p h d", d=DH)

        with nc.Block() as block:

            @block.sync
            def _(sp):
                sp.dma_start(base[:, :, :, :], w["c_xpos"]).then_inc(const_loaded, 16)
                sp.dma_start(identb[:, :], w["c_identb"]).then_inc(const_loaded, 16)
                sp.dma_start(mask[:, :, :], w["c_mask"]).then_inc(const_loaded, 16)
                with sp.Fori(0, DEPTH) as l:
                    sp.wait_ge(xb_ready, l * 2 * SEQS)
                    for dst, name in attn_weights:
                        sp.dma_start(dst, w[name][bass.ds(l * 128, 128), :]).then_inc(attn_loaded, 16)
                    sp.dma_start(qks[:, :, :].rearrange("p a b -> p (a b)"),
                                 w["tr_qks"][bass.ds(l * 128, 128), :]).then_inc(attn_loaded, 16)
                    sp.wait_ge(xa_ready, l * SEQS)
                    for dst, name in mlp_weights:
                        sp.dma_start(dst, w[name][bass.ds(l * 128, 128), :]).then_inc(mlp_loaded, 16)

            @block.gpsimd
            def _(pool):
                def finish(q, par):
                    for u in range(4):
                        pool.wait_ge(rot_done, q * 4 + (u + 1))
                        nc.gpsimd.tensor_tensor(raw[:, u, :], raw[:, u, :], raw[:, u, :],
                                                ALU.mult).then_inc(sq_done, 1)
                    nc.gpsimd.tensor_tensor(qm[:, 0, 0:2, :], qm[:, 0, 0:2, :], qm[:, 1, 0:2, :],
                                            ALU.add).then_inc(q_ready, 1)
                    nc.gpsimd.tensor_tensor(qm[:, 0, 2:4, :], qm[:, 0, 2:4, :], qm[:, 1, 2:4, :],
                                            ALU.add).then_inc(pool_step, 1)
                    pool.wait_ge(ss_done, q * 2 + 2)
                    stand_alone(pool, pool_passed)
                    nc.gpsimd.tensor_scalar(ss[:, :], ss[:, :], 1e-24, None, ALU.max).then_inc(pool_step, 1)
                    pool.wait_ge(pool_step, q * 3 + 2)
                    nc.gpsimd.tensor_tensor(rn[:, par, :], ss[:, :], half[:, :], ALU.pow).then_inc(pool_step, 1)
                    pool.wait_ge(pool_step, q * 3 + 3)
                    stand_alone(pool, pool_passed)
                    nc.gpsimd.tensor_scalar(rn[:, par, 0:HEADS], rn[:, par, 0:HEADS], 8.0, None,
                                            ALU.mult).then_inc(norms_ready, 1)
                    k3 = qm[:, 0, 2:4, :].rearrange("p a (h d) -> p (a h) d", d=DH)
                    nc.gpsimd.tensor_tensor(k3, k3, rn[:, par, HEADS:].unsqueeze(2).broadcast_to([128, HEADS, DH]),
                                            ALU.mult).then_inc(k_ready, 1)

                nc.gpsimd.memset(half[:, :], -0.5).then_inc(init_done, 1)
                nc.gpsimd.memset(kt[:, :, :, :], 0.0).then_inc(init_done, 1)
                pool.wait_ge(init_done, 2)
                with pool.Fori(0, DEPTH) as l:
                    pool.wait_ge(exp_done, l * (HEADS * TPS * SEQS))
                    finish(l * NQKV, 0)
                    with pool.Fori(0, SEQS) as b:
                        for p in range(TPS):
                            q = l * NQKV + b * TPS + (p + 1)
                            par = (p + 1) % 2
                            pool.wait_ge(exp_done, ((l * SEQS + b) * TPS + p) * HEADS + 1)
                            stand_alone(pool, pool_passed)
                            nc.gpsimd.tensor_copy(pw[:, HEADS, :], pw[:, 0, :]).then_inc(again_done, 1)
                            pool.wait_ge(exp_done, ((l * SEQS + b) * TPS + p) * HEADS)
                            finish(q, par)

            @block.tensor
            def _(pe):
                def project(q, par):
                    pe.wait_ge(xs_ready, q * 2 + 2)
                    for u in range(UNITS):
                        if u == 0:
                            pe.wait_ge(raw_ready, q * 4)
                        elif 2 <= u < 6:
                            pe.wait_ge(v_copied, q * 4 + (u - 1))
                        elif u >= 6:
                            pe.wait_ge(raw_ready, q * 4 + (u - 5))
                        lhs = xs[:, par, 0:TILE] if u in (2, 3) else xs[:, par, WIN:WIN + TILE]
                        at = 2 * INNER + (u % 2) * CH if u < 4 else (u - 4) * CH
                        nc.tensor.matmul(P2[u % 2], lhs, wqkv[:, at:at + CH], start=True, stop=True).then_inc(proj_done, 1)

                def turn(seq, p, k):
                    if p == 0 and k < 2:
                        pe.wait_ge(xb_ready, seq * 2)
                    else:
                        pe.wait_ge(turn_read, seq * (TPS * TURNS) + (p * TURNS + k - 1))
                    return PT[k % 2]

                with pe.Fori(0, DEPTH) as l:
                    pe.wait_ge(attn_loaded, (l + 1) * ATTN_LOADS)
                    project(l * NQKV, 0)
                    with pe.Fori(0, SEQS) as b:
                        for p in range(TPS):
                            q = l * NQKV + b * TPS + p
                            seq = l * SEQS + b
                            n = seq * TPS + p
                            par = p % 2
                            for k in range(4):
                                bank = turn(seq, p, k)
                                pe.wait_ge((q_ready, k_ready)[k // 2], q + 1)
                                for i in range(4):
                                    last = nc.tensor.transpose(bank[:, i * 128:(i + 1) * 128],
                                                               qm[:, 0, k, i * 128:(i + 1) * 128], ident[:, :])
                                last.then_inc(turn_done, 1)
                            pe.wait_ge(exp_done, n * HEADS)
                            pe.wait_ge(max_done, n * 2)
                            for e in range(2):
                                nc.tensor.matmul(PS[e], identb[:, :], mask[:, min(p, 1), :], start=True, stop=False,
                                                 skip_group_check=True)
                            pe.wait_ge(turn_read, seq * (TPS * TURNS) + (p * TURNS + 4))
                            pe.wait_ge(kprev_done, n + 1)
                            stand_alone(pe, pe_passed)
                            for hp in range(PAIRS):
                                for e in range(2):
                                    r = slice(64 * e, 64 * e + 64)
                                    for wi in range(WPT):
                                        last = nc.tensor.matmul(
                                            PS[e][wi * WIN:(wi + 1) * WIN, hp * 2 * WIN:(hp + 1) * 2 * WIN],
                                            qt[r, hp, wi * WIN:(wi + 1) * WIN],
                                            kt[r, par, hp, wi * WIN:(wi + 2) * WIN],
                                            start=False, stop=(hp == PAIRS - 1), skip_group_check=True)
                            last.then_inc(scores_done, 1)
                            project(q + 1, 1 - par)
                            for k in range(4):
                                bank = turn(seq, p, 4 + k)
                                pe.wait_ge(exp_done, n * HEADS + min(4 * (k + 1) + 1, HEADS))
                                if k == 3:
                                    pe.wait_ge(again_done, n + 1)
                                for i in range(4):
                                    h = 4 * k + i
                                    last = nc.tensor.transpose(bank[:, i * 128:(i + 1) * 128],
                                                               pw[:, h:h + 2, :].rearrange("p a b -> p (a b)"),
                                                               ident[:, :])
                                last.then_inc(turn_done, 1)
                            pe.wait_ge(on_ready, n * 2)
                            pe.wait_ge(v_copied, q * 4 + 4)
                            for up in range(2):
                                for hh in range(2):
                                    pe.wait_ge(turn_read, seq * (TPS * TURNS) + p * TURNS + (8 if up else 6 + 2 * hh))
                                    stand_alone(pe, pe_passed)
                                    for h in range(8 * hh, 8 * hh + 8):
                                        for wi in (2 * up, 2 * up + 1):
                                            r = slice(64 * up, 64 * up + 64)
                                            last = nc.tensor.matmul(
                                                PV[hh][wi * WIN:(wi + 1) * WIN, (h % 8) * DH:(h % 8 + 1) * DH],
                                                pt[r, (h - up) % HEADS, wi * WIN:(wi + 1) * WIN],
                                                (vb, va)[wi % 2][r, par, h * DH:(h + 1) * DH], start=True, stop=True)
                                    if up:
                                        last.then_inc(pv_done, 1)
                            for k in range(2):
                                bank = turn(seq, p, 8 + k)
                                pe.wait_ge(on_ready, n * 2 + (k + 1))
                                for i in range(4):
                                    a = (4 * k + i) * 128
                                    last = nc.tensor.transpose(bank[:, i * 128:(i + 1) * 128], on[:, a:a + 128],
                                                               ident[:, :])
                                last.then_inc(turn_done, 1)
                        for k in range(2):
                            pe.wait_ge(turn_read, (l * SEQS + b) * (TPS * TURNS) + TPS * TURNS)
                            for hp in range(PAIRS):
                                last = nc.tensor.matmul(PT[k][:, 0:L // 2], wo[:, hp, :],
                                                        ot[:, hp, k * (L // 2):(k + 1) * (L // 2)],
                                                        start=(hp == 0), stop=(hp == PAIRS - 1))
                            last.then_inc(wo_done, 1)
                    with pe.Fori(0, SEQS) as i:
                        pe.wait_ge(xf_ready, l * SEQS + (i + 1))
                        nc.tensor.matmul(ps[:, bass.ds(i * CH, CH)], ones[:, :], xf[:, bass.ds(i * CH, CH)],
                                         start=True, stop=True).then_inc(mean_done, 1)
                    with pe.Fori(0, SEQS) as i:
                        pe.wait_ge(squared, l * SEQS + (i + 1))
                        nc.tensor.matmul(ps[:, bass.ds(i * CH, CH)], ones[:, :], fsq[:, bass.ds(i * CH, CH)],
                                         start=True, stop=True).then_inc(var_done, 1)
                    pe.wait_ge(mlp_loaded, (l + 1) * MLP_LOADS)
                    pe.wait_ge(std_done, (l + 1) * SEQS)
                    stand_alone(pe, pe_passed)
                    with pe.Fori(0, SEQS // 2) as i2:
                        for par in range(2):
                            i = i2 * 2 + par
                            ch = l * SEQS + i
                            pe.wait_ge(xn_ready, ch + 1)
                            for j in range(HT):
                                for kind in range(2):
                                    pe.wait_ge((gelu_done, hid_ready)[kind], ch * HT)
                                    at = (1 - kind) * HID + j * 128
                                    nc.tensor.matmul(ps[0:HW[j], (2 * j + kind) * CH:(2 * j + kind + 1) * CH],
                                                     w1[:, at:at + HW[j]], xf[:, bass.ds(i * CH, CH)],
                                                     start=True, stop=True).then_inc(hid_done, 1)
                            pe.wait_ge(xa_ready, ch - par)
                            for j in range(HT):
                                pe.wait_ge(hid_ready, ch * HT + (j + 1))
                                last = nc.tensor.matmul(PV[par], w2[0:HW[j], j, :], hb[0:HW[j], par, j, :],
                                                        start=(j == 0), stop=(j == HT - 1))
                            last.then_inc(mlp_done, 1)

            @block.vector
            def _(dve):
                def shift(par, b, t):
                    c0 = b * SEQP + (PAD + 1 + t * TILE - WIN)
                    nc.vector.tensor_copy(xs[0:64, par, :], xa[0:64, bass.ds(c0, WIN + TILE)]).then_inc(xs_ready, 1)
                    nc.vector.tensor_copy(xs[64:128, par, :],
                                          xa[64:128, bass.ds(c0 - 1, WIN + TILE)]).then_inc(xs_ready, 1)

                def take(q, par, p):
                    for u in range(4):
                        dve.wait_ge(proj_done, q * UNITS + (u + 1))
                        dst = (va, vb)[u // 2]
                        nc.vector.tensor_copy(dst[:, par, (u % 2) * CH:(u % 2 + 1) * CH], P2[u % 2]).then_inc(v_copied, 1)
                    for u in range(4):
                        dve.wait_ge(raw_ready, q * 4 + (u + 1))
                        src = tile_heads(raw[:, u, :])
                        cos, sin = (rope[:, 2 * (u // 2) + s, p, :].unsqueeze(1) for s in range(2))
                        nc.vector.tensor_tensor(tile_heads(qm[:, 0, u, :]), src,
                                                cos.broadcast_to([128, 8, DH]), ALU.mult)
                        rot = tile_heads(qm[:, 1, u, :])
                        h = DH // 2
                        nc.vector.tensor_tensor(rot[:, :, 0:h], src[:, :, h:DH],
                                                sin[:, :, 0:h].broadcast_to([128, 8, h]), ALU.mult)
                        nc.vector.tensor_tensor(rot[:, :, h:DH], src[:, :, 0:h],
                                                sin[:, :, h:DH].broadcast_to([128, 8, h]), ALU.mult).then_inc(rot_done, 1)

                def sum_squares(q):
                    dve.wait_ge(norms_ready, q)
                    for u in range(0, 4, 2):
                        dve.wait_ge(sq_done, q * 4 + (u + 2))
                        nc.vector.tensor_reduce(ss[:, u * 8:(u + 2) * 8],
                                                raw[:, u:u + 2, :].rearrange("p a (h d) -> p (a h) d", d=DH),
                                                AX.X, ALU.add).then_inc(ss_done, 1)

                dve.wait_ge(const_loaded, CONST_LOADS)
                with dve.Fori(0, DEPTH) as l:
                    dve.wait_ge(attn_loaded, (l + 1) * ATTN_LOADS)
                    h = DH // 2
                    for s in range(2):
                        row = qks[:, s, :].unsqueeze(1)
                        nc.vector.tensor_tensor(rope[:, 2 * s, :, :], base[:, 2 * s, :, :],
                                                row.broadcast_to([128, TPS, DH]), ALU.mult)
                        nc.vector.tensor_tensor(rope[:, 2 * s + 1, :, 0:h], base[:, 2 * s + 1, :, 0:h],
                                                row[:, :, h:DH].broadcast_to([128, TPS, h]), ALU.mult)
                        last = nc.vector.tensor_tensor(rope[:, 2 * s + 1, :, h:DH], base[:, 2 * s + 1, :, h:DH],
                                                       row[:, :, 0:h].broadcast_to([128, TPS, h]), ALU.mult)
                    last.then_inc(scales_done, 1)
                    dve.wait_ge(scales_done, l + 1)
                    dve.wait_ge(xa_ready, l * SEQS)
                    shift(0, 0, 0)
                    take(l * NQKV, 0, 0)
                    sum_squares(l * NQKV)
                    with dve.Fori(0, SEQS) as b:
                        for p in range(TPS):
                            q = l * NQKV + b * TPS + p
                            seq = l * SEQS + b
                            n = seq * TPS + p
                            par = p % 2
                            dve.wait_ge(proj_done, q * UNITS)
                            shift(1 - par, b + (p + 1) // TPS, (p + 1) % TPS)
                            dve.wait_ge(scores_done, n + 1)
                            for e in range(2):
                                nc.vector.tensor_reduce(mx[:, e, :], PS[e].rearrange("p (h j) -> p h j", j=2 * WIN),
                                                        AX.X, ALU.max).then_inc(max_done, 1)
                            dve.wait_ge(max_done, n * 2 + 2)
                            dve.wait_ge(norms_ready, q + 1)
                            nc.vector.scalar_tensor_tensor(
                                nb[:, :, :], mx[:, :, :], -1.0,
                                rn[:, par, 0:HEADS].rearrange("p (h e) -> p e h", e=2), ALU.mult,
                                ALU.mult).then_inc(bias_ready, 1)
                            dve.wait_ge(pv_done, n * 2)
                            take(q + 1, 1 - par, (p + 1) % TPS)
                            sum_squares(q + 1)
                            dve.wait_ge(exp_done, n * HEADS + HEADS)
                            nc.vector.reciprocal(rr[:, :], rs[:, :]).then_inc(rsum_done, 1)
                            dve.wait_ge(rsum_done, n + 1)
                            for hh in range(2):
                                dve.wait_ge(pv_done, n * 2 + (hh + 1))
                                nc.vector.tensor_tensor(
                                    tile_heads(on[:, hh * CH:(hh + 1) * CH]), tile_heads(PV[hh]),
                                    rr[:, hh * 8:(hh + 1) * 8].unsqueeze(2).broadcast_to([128, 8, DH]),
                                    ALU.mult).then_inc(on_ready, 1)
                        for k in range(2):
                            dve.wait_ge(wo_done, (l * SEQS + b) * 2 + (k + 1))
                            cols = bass.ds(b * SEQP + (PAD + 1 + k * (L // 2)), L // 2)
                            nc.vector.tensor_tensor(xb[:, cols], PT[k][:, 0:L // 2], xa[:, cols],
                                                    ALU.add).then_inc(xb_ready, 1)
                    dve.wait_ge(xb_ready, (l + 1) * 2 * SEQS)
                    stand_alone(dve, dve_passed)
                    with dve.Fori(0, SEQS) as i:
                        nc.vector.tensor_copy(xf[0:64, bass.ds(i * CH, CH)], xb[0:64, bass.ds(i * SEQP + (PAD + 1), L)])
                        nc.vector.tensor_copy(xf[64:128, bass.ds(i * CH, CH)],
                                              xb[64:128, bass.ds(i * SEQP + PAD, L)]).then_inc(xf_ready, 1)
                    with dve.Fori(0, SEQS) as i:
                        dve.wait_ge(mean_done, l * SEQS + (i + 1))
                        x = xf[:, bass.ds(i * CH, CH)]
                        nc.vector.tensor_tensor(x, x, ps[:, bass.ds(i * CH, CH)], ALU.subtract).then_inc(centered, 1)
                    with dve.Fori(0, SEQS) as i:
                        dve.wait_ge(std_done, l * SEQS + (i + 1))
                        s = fsd[:, bass.ds(i * CH, CH)]
                        nc.vector.reciprocal(s, s).then_inc(rstd_done, 1)
                    with dve.Fori(0, SEQS) as i:
                        dve.wait_ge(rstd_done, l * SEQS + (i + 1))
                        x = xf[:, bass.ds(i * CH, CH)]
                        nc.vector.tensor_tensor(x, x, fsd[:, bass.ds(i * CH, CH)], ALU.mult).then_inc(normed, 1)
                    with dve.Fori(0, SEQS // 2) as i2:
                        for par in range(2):
                            i = i2 * 2 + par
                            ch = l * SEQS + i
                            for j in range(HT):
                                dve.wait_ge(hid_done, ch * MLPU + (2 * j + 2))
                                dve.wait_ge(gelu_done, ch * HT + (j + 1))
                                o = hb[0:HW[j], par, j, :]
                                nc.vector.scalar_tensor_tensor(o, ps[0:HW[j], (2 * j + 1) * CH:(2 * j + 2) * CH],
                                                               b1[0:HW[j], j:j + 1], o, ALU.add,
                                                               ALU.mult).then_inc(hid_ready, 1)
                            dve.wait_ge(mlp_done, ch + 1)
                            cols = bass.ds(i * SEQP + (PAD + 1), L)
                            nc.vector.scalar_tensor_tensor(xa[:, cols], PV[par], b2[:, 0:1], xb[:, cols], ALU.add,
                                                           ALU.add).then_inc(xa_ready, 1)

            @block.scalar
            def _(act):
                def take_raw(q, u):
                    act.wait_ge(ss_done, q * 2)
                    act.wait_ge(proj_done, q * UNITS + (u + 5))
                    nc.scalar.activation(raw[:, u, :], P2[u % 2], ACT.Copy).then_inc(raw_ready, 1)

                act.wait_ge(init_done, 2)
                with act.Fori(0, DEPTH) as l:
                    for u in range(4):
                        take_raw(l * NQKV, u)
                    with act.Fori(0, SEQS) as b:
                        for p in range(TPS):
                            q = l * NQKV + b * TPS + p
                            seq = l * SEQS + b
                            n = seq * TPS + p
                            par = p % 2
                            t0 = seq * (TPS * TURNS)
                            nc.scalar.activation(kt[:, par, :, 0:WIN], kt[:, 1 - par, :, TILE:WIN + TILE],
                                                 ACT.Copy).then_inc(kprev_done, 1)
                            for k in range(4):
                                act.wait_ge(turn_done, t0 + (p * TURNS + k + 1))
                                src = PT[k % 2].rearrange("p (i t) -> p i t", t=TILE)
                                o = 4 * (k % 2)
                                dst = qt[:, o:o + 4, :] if k < 2 else kt[:, par, o:o + 4, WIN:WIN + TILE]
                                nc.scalar.activation(dst, src, ACT.Copy).then_inc(turn_read, 1)
                            act.wait_ge(bias_ready, n + 1)
                            for j in range(4):
                                for hd in range(4 * j, 4 * j + 4):
                                    e, hp = hd % 2, hd // 2
                                    nc.scalar.activation(pw[:, hd, :], PS[e][:, hp * 2 * WIN:(hp + 1) * 2 * WIN],
                                                         ACT.Exp, bias=nb[:, e, hp:hp + 1],
                                                         scale=rn[:, par, hd:hd + 1],
                                                         accum_out=rs[:, hd:hd + 1]).then_inc(exp_done, 1)
                                take_raw(q + 1, j)
                            for k in range(4):
                                act.wait_ge(turn_done, t0 + (p * TURNS + k + 5))
                                nc.scalar.activation(pt[:, 4 * k:4 * k + 4, :],
                                                     PT[k % 2].rearrange("p (i t) -> p i t", t=TILE),
                                                     ACT.Copy).then_inc(turn_read, 1)
                            for k in range(2):
                                act.wait_ge(turn_done, t0 + (p * TURNS + k + 9))
                                nc.scalar.activation(ot[:, 4 * k:4 * k + 4, p * TILE:(p + 1) * TILE],
                                                     PT[k % 2].rearrange("p (i t) -> p i t", t=TILE),
                                                     ACT.Copy).then_inc(turn_read, 1)
                    with act.Fori(0, SEQS) as i:
                        act.wait_ge(centered, l * SEQS + (i + 1))
                        nc.scalar.activation(fsq[:, bass.ds(i * CH, CH)], xf[:, bass.ds(i * CH, CH)],
                                             ACT.Square).then_inc(squared, 1)
                    act.wait_ge(k_ready, (l + 1) * NQKV)
                    with act.Fori(0, SEQS) as i:
                        act.wait_ge(var_done, l * SEQS + (i + 1))
                        nc.scalar.activation(fsd[:, bass.ds(i * CH, CH)], ps[:, bass.ds(i * CH, CH)], ACT.Sqrt,
                                             bias=eps[:, 0:1]).then_inc(std_done, 1)
                    act.wait_ge(mlp_loaded, (l + 1) * MLP_LOADS)
                    with act.Fori(0, SEQS) as i:
                        act.wait_ge(normed, l * SEQS + (i + 1))
                        x = xf[:, bass.ds(i * CH, CH)]
                        nc.scalar.activation(x, x, ACT.Identity, bias=lnb[:, 0:1], scale=lng[:, 0:1]).then_inc(xn_ready, 1)
                    with act.Fori(0, SEQS // 2) as i2:
                        for par in range(2):
                            ch = l * SEQS + (i2 * 2 + par)
                            for j in range(HT):
                                act.wait_ge(hid_done, ch * MLPU + (2 * j + 1))
                                if j == 0:
                                    act.wait_ge(mlp_done, ch - par)
                                nc.scalar.activation(hb[0:HW[j], par, j, :], ps[0:HW[j], 2 * j * CH:(2 * j + 1) * CH],
                                                     ACT.Gelu, bias=b1[0:HW[j], HT + j:HT + j + 1]).then_inc(gelu_done, 1)


def mlp_stage(nc, ps, sem, w, xn, xr, xcat, ones4, eps):
    with ExitStack() as c:
        def sb(name, shape, dt=FP32):
            return c.enter_context(nc.sbuf_tensor(f"ml_{name}", shape, dt))

        wf = sb("wf", [128, MLP])
        wp = sb("wp", [128, MT, 128])
        neg = sb("neg", [128, MLP])
        lnw = sb("lnw", [128, MT])
        lnb = sb("lnb", [128, MT])
        asum = sb("asum", [128, 2])
        ga = sb("ga", [128, 4])
        hid = sb("hid", [128, MT, TOK])
        sq = sb("sq", [128, 2, MT, CH])
        sd = sb("sd", [128, 2, CH])
        loaded = sem("ml_loaded")
        prep = sem("ml_prep")
        asum_done = sem("ml_asum_done")
        gamma_done = sem("ml_gamma_done")
        w_ready = sem("ml_w_ready")
        hid_done = sem("ml_hid_done")
        gelu_done = sem("ml_gelu_done")
        mean_done = sem("ml_mean_done")
        centered = sem("ml_centered")
        squared = sem("ml_squared")
        var_done = sem("ml_var_done")
        std_done = sem("ml_std_done")
        rstd_done = sem("ml_rstd_done")
        normed = sem("ml_normed")
        affine_done = sem("ml_affine_done")
        out_done = sem("ml_out_done")
        out_read = sem("ml_out_read")
        stored = sem("ml_stored")
        act_passed = sem("ml_act_passed")

        def bank(k):
            return ps[:, k * CH:(k + 1) * CH]

        with nc.Block() as block:

            @block.sync
            def _(sp):
                sp.dma_start(wf[:, :], w["ml_wf"]).then_inc(loaded, 16)
                sp.dma_start(wp[:, :, :], w["ml_wp"]).then_inc(loaded, 16)
                sp.dma_start(lnw[:, :], w["ml_lnw"]).then_inc(loaded, 16)
                sp.dma_start(lnb[:, :], w["ml_lnb"]).then_inc(loaded, 16)
                with sp.Fori(0, SEQS) as i:
                    sp.wait_ge(out_read, i + 1)
                    sp.dma_start(xcat[:, bass.ds(i * CH, CH)], xr(i)).then_inc(stored, 16)
                sp.wait_ge(stored, 16 * SEQS)

            @block.tensor
            def _(pe):
                pe.wait_ge(asum_done, 1)
                nc.tensor.matmul(bank(0)[:, 0:2], ones4[:, :], asum[:, :], start=True, stop=True).then_inc(gamma_done, 1)
                pe.wait_ge(w_ready, 1)
                with pe.Fori(0, SEQS) as i:
                    for j in range(MT):
                        pe.wait_ge(gelu_done, i * MT)
                        nc.tensor.matmul(bank(j), wf[:, j * 128:(j + 1) * 128], xn(i),
                                         start=True, stop=True).then_inc(hid_done, 1)
                with pe.Fori(0, SEQS // 2) as i2:
                    for par in range(2):
                        i = i2 * 2 + par
                        pe.wait_ge(gelu_done, SEQS * MT)
                        pe.wait_ge(centered, i * MT)
                        for j in range(MT):
                            last = nc.tensor.matmul(bank(par), ones4[:, :], hid[:, j, bass.ds(i * CH, CH)],
                                                    start=(j == 0), stop=(j == MT - 1))
                        last.then_inc(mean_done, 1)
                        pe.wait_ge(std_done, i)
                        for j in range(MT):
                            pe.wait_ge(squared, i * MT + (j + 1))
                            last = nc.tensor.matmul(bank(2 + par), ones4[:, :], sq[:, par, j, :],
                                                    start=(j == 0), stop=(j == MT - 1))
                        last.then_inc(var_done, 1)
                        pe.wait_ge(out_read, i)
                        for j in range(MT):
                            pe.wait_ge(affine_done, i * MT + (j + 1))
                            last = nc.tensor.matmul(bank(4 + par), wp[:, j, :], hid[:, j, bass.ds(i * CH, CH)],
                                                    start=(j == 0), stop=(j == MT - 1))
                        last.then_inc(out_done, 1)

            @block.vector
            def _(dve):
                steps = [0]

                def link(ins):
                    steps[0] += 1
                    ins.then_inc(prep, 1)
                    dve.wait_ge(prep, steps[0])

                dve.wait_ge(loaded, 64)
                link(nc.vector.tensor_reduce(asum[:, 0:1], wf[:, :], AX.X, ALU.add, apply_absolute_value=True))
                nc.vector.tensor_reduce(asum[:, 1:2], wp[:, :, :], AX.XY, ALU.add,
                                        apply_absolute_value=True).then_inc(asum_done, 1)
                dve.wait_ge(gamma_done, 1)
                link(nc.vector.tensor_scalar(ga[:, 0:2], bank(0)[:, 0:2], 1.0 / 128, 1e-6, ALU.mult, ALU.add))
                link(nc.vector.tensor_scalar(ga[:, 0:2], ga[:, 0:2], 0.5, None, ALU.mult))
                link(nc.vector.tensor_scalar(ga[:, 2:4], ga[:, 0:2], -1.0, None, ALU.mult))
                for k, m in ((0, wf[:, :]), (1, wp[:, :, :].rearrange("p a b -> p (a b)"))):
                    link(nc.vector.tensor_scalar(neg[:, :], m, ga[:, 2 + k:3 + k], None, ALU.is_lt))
                    link(nc.vector.tensor_scalar(m, m, ga[:, k:k + 1], None, ALU.is_gt))
                    link(nc.vector.tensor_tensor(m, m, neg[:, :], ALU.subtract))
                nc.vector.tensor_copy(ga[:, 0:1], ga[:, 1:2]).then_inc(w_ready, 1)
                with dve.Fori(0, SEQS // 2) as i2:
                    for par in range(2):
                        i = i2 * 2 + par
                        dve.wait_ge(mean_done, i + 1)
                        for j in range(MT):
                            h = hid[:, j, bass.ds(i * CH, CH)]
                            nc.vector.tensor_tensor(h, h, bank(par), ALU.subtract).then_inc(centered, 1)
                        dve.wait_ge(std_done, i + 1)
                        nc.vector.reciprocal(sd[:, par, :], sd[:, par, :]).then_inc(rstd_done, 1)
                        dve.wait_ge(rstd_done, i + 1)
                        for j in range(MT):
                            h = hid[:, j, bass.ds(i * CH, CH)]
                            nc.vector.scalar_tensor_tensor(h, h, lnw[:, j:j + 1], sd[:, par, :], ALU.mult,
                                                           ALU.mult).then_inc(normed, 1)
                        dve.wait_ge(out_done, i + 1)
                        nc.vector.tensor_tensor(xr(i), xr(i), bank(4 + par), ALU.add).then_inc(out_read, 1)

            @block.scalar
            def _(act):
                with act.Fori(0, SEQS) as i:
                    for j in range(MT):
                        act.wait_ge(hid_done, i * MT + (j + 1))
                        nc.scalar.activation(hid[:, j, bass.ds(i * CH, CH)], bank(j), ACT.Gelu).then_inc(gelu_done, 1)
                with act.Fori(0, SEQS // 2) as i2:
                    for par in range(2):
                        i = i2 * 2 + par
                        for j in range(MT):
                            act.wait_ge(centered, i * MT + (j + 1))
                            nc.scalar.activation(sq[:, par, j, :], hid[:, j, bass.ds(i * CH, CH)],
                                                 ACT.Square).then_inc(squared, 1)
                        act.wait_ge(var_done, i + 1)
                        nc.scalar.activation(sd[:, par, :], bank(2 + par), ACT.Sqrt, bias=eps[:, 0:1]).then_inc(std_done, 1)
                        for j in range(MT):
                            act.wait_ge(normed, i * MT + (j + 1))
                            stand_alone(act, act_passed)
                            h = hid[:, j, bass.ds(i * CH, CH)]
                            nc.scalar.activation(h, h, ACT.Identity, bias=lnb[:, j:j + 1]).then_inc(affine_done, 1)


def program(nc, w, out):
    ctx = ExitStack()
    with ctx:
        def sem(name):
            return ctx.enter_context(nc.semaphore(name))

        def sb(name, shape, dt=FP32):
            return ctx.enter_context(nc.sbuf_tensor(name, shape, dt))

        xr = sb("xr", [128, TOK])
        xa = sb("xa", [128, XCOLS])
        xb = sb("xb", [128, XCOLS])
        ones = sb("ones", [128, 128])
        ones4 = sb("ones4", [128, 128])
        eps = sb("eps", [128, 1])
        ident = sb("ident", [128, 128])
        ps = ctx.enter_context(nc.psum_tensor("ps", [128, 8 * CH], FP32))
        x_loaded = sem("x_loaded")

        def plain(i):
            return xr[:, bass.ds(i * L, L)]

        def padded(buf):
            return lambda i: buf[:, bass.ds(i * SEQP + (PAD + 1), L)]

        with nc.Block() as block:

            @block.sync
            def _(sp):
                sp.dma_start(xr[:, :], w["x"]).then_inc(x_loaded, 16)
                sp.dma_start(ident[:, :], w["c_ident"]).then_inc(x_loaded, 16)
                sp.wait_ge(x_loaded, 32)

            @block.vector
            def _(dve):
                nc.vector.memset(xa[:, :], 0.0)
                nc.vector.memset(ones[:, :], 1.0 / D)
                nc.vector.memset(ones4[:, :], 1.0 / MLP)
                nc.vector.memset(eps[:, :], LN_EPS)

            @block.gpsimd
            def _(pool):
                nc.gpsimd.memset(xb[:, :], 0.0)

        layernorm_stage(nc, ps, sem, "a", plain, padded(xa), ones, eps)
        retention_stage(nc, ps, sem, w, padded(xa), plain, eps)
        transformer_stage(nc, ps, sem, w, xa, xb, ones, eps, ident)
        layernorm_stage(nc, ps, sem, "b", plain, padded(xb), ones, eps, src2=padded(xa))
        softmax_stage(nc, ps, sem, w, padded(xb), plain, ident)
        mlp_stage(nc, ps, sem, w, padded(xb), plain, out, ones4, eps)


def constants():
    f = np.float32
    t = {}
    c = np.arange(L)[None, :] - np.arange(128)[:, None]
    t["c_lag"] = np.maximum(c, 0).astype(f)
    t["c_ident"] = np.eye(128, dtype=f)
    bf = mybir.dt.np(BF16)
    t["c_identb"] = np.eye(128).astype(bf)
    i, j = (np.arange(128) % WIN)[:, None], np.arange(2 * WIN)[None, :]
    seen = (j >= i) & (j <= i + WIN)
    first = seen & ((j >= WIN) | (np.arange(128) >= WIN)[:, None])
    m = np.stack([np.where(first, 0.0, -1e30), np.where(seen, 0.0, -1e30)], 1)
    t["c_mask"] = np.ascontiguousarray(np.tile(m, (1, 1, PAIRS))).astype(bf)
    half = np.arange(0, DH, 2, dtype=f)
    inv = (f(1.0) / f(10000.0) ** (half / f(DH))).astype(f)
    pos = np.arange(L, dtype=f)
    fr = pos[:, None] * inv[None, :]
    fr = np.concatenate([fr, fr], -1)
    bs = (half + f(0.4 * DH)) / f(1.4 * DH)
    power = (pos - L // 2) / f(WIN // 2)
    sc = bs[None, :] ** power[:, None]
    sc = np.concatenate([sc, sc], -1).astype(f)
    sgn = np.where(np.arange(DH) < DH // 2, -1, 1).astype(f)
    tb = np.stack([np.cos(fr) * sc, np.sin(fr) * sc * sgn, np.cos(fr) / sc, np.sin(fr) / sc * sgn])
    t["c_xpos"] = np.ascontiguousarray(tb.reshape(4, TPS, 128, DH).transpose(2, 0, 1, 3).astype(f))
    hh = DK // 2
    inv = (f(1.0) / f(10000.0) ** (np.arange(hh, dtype=f) / f(hh))).astype(f)
    ang = pos[:, None] * inv[None, :]
    rt = np.zeros((SLOT, 4, L), f)
    for k, s in ((0, f(DK ** -0.5)), (2, f(1.0))):
        rt[0:hh, k], rt[hh:DK, k] = np.cos(ang).T * s, np.cos(ang).T * s
        rt[0:hh, k + 1], rt[hh:DK, k + 1] = -np.sin(ang).T * s, np.sin(ang).T * s
    rt[DK, 2] = 1.0
    t["c_rope"] = np.ascontiguousarray(np.tile(rt, (4, 1, 1)))
    b = np.zeros((SLOT, SLOT), f)
    b[DK, :] = 1.0
    t["c_bsel"] = np.kron(np.eye(4, dtype=f), b)
    return t


def slots(m):
    p = np.zeros((m.shape[0], HEADS, SLOT), m.dtype)
    p[:, :, :DK] = m.reshape(m.shape[0], HEADS, DK)
    return p.reshape(m.shape[0], HEADS * SLOT)


def slot_rows(m):
    return np.ascontiguousarray(slots(np.ascontiguousarray(m.T)).T.reshape(QUADS, 128, -1).transpose(1, 0, 2))


def layout(inp):
    f = {k: np.asarray(v) for k, v in inp.items()}
    w = constants()
    w["x"] = np.ascontiguousarray(f["L0_attn_x"].reshape(TOK, D).T)
    qkv = f["L0_attn_W_qkv"]
    w["ret_wq"] = slots(qkv[0:D].T)
    w["ret_wk"] = np.ascontiguousarray(qkv[D:2 * D].T)
    w["ret_wv"] = slots(qkv[2 * D:3 * D].T)
    w["ret_wo"] = slot_rows(f["L0_attn_W_o"].T)
    w["log_gamma"] = f["L0_attn_log_gamma"]
    w["tr_wqkv"] = f["L0_ffn_Wqkv"].reshape(DEPTH * D, 3 * INNER)
    w["tr_wo"] = np.ascontiguousarray(f["L0_ffn_Wo"].reshape(DEPTH, PAIRS, 128, D).transpose(0, 2, 1, 3)
                                      ).reshape(DEPTH * 128, PAIRS * D)
    w["tr_w1"] = f["L0_ffn_W1"].reshape(DEPTH * D, 2 * HID)
    w2 = np.zeros((DEPTH, HT * 128, D), np.float32)
    w2[:, :HID] = f["L0_ffn_W2"]
    w["tr_w2"] = np.ascontiguousarray(w2.reshape(DEPTH, HT, 128, D).transpose(0, 2, 1, 3)).reshape(DEPTH * 128, HT * D)
    b1 = np.zeros((DEPTH, 2, HT * 128), np.float32)
    b1[:, :, :HID] = f["L0_ffn_b1"].reshape(DEPTH, 2, HID)
    w["tr_b1"] = np.ascontiguousarray(b1.reshape(DEPTH, 2 * HT, 128).transpose(0, 2, 1)).reshape(DEPTH * 128, 2 * HT)
    for name, key in (("tr_b2", "L0_ffn_b2"), ("tr_lng", "L0_ffn_ln_g"), ("tr_lnb", "L0_ffn_ln_b")):
        w[name] = f[key].reshape(DEPTH * 128, 1)
    s = np.concatenate([f["L0_ffn_q_scale"], f["L0_ffn_k_scale"]], 1)
    w["tr_qks"] = np.ascontiguousarray(np.repeat(s, 128, 0))
    def swap(m):
        return np.ascontiguousarray(m.reshape(-1, HEADS, 2, DK // 2)[:, :, ::-1]).reshape(m.shape)
    ws, bs = [], []
    for n in "qk":
        for fn in (lambda m: m, swap):
            ws.append(slots(fn(f[f"L1_attn_w{n}_w"])))
            bs.append(slots(fn(f[f"L1_attn_w{n}_b"][None])))
    w["sm_wp"] = np.ascontiguousarray(np.stack(ws, 1))
    bs[2].reshape(HEADS, SLOT)[:, DK] = 1.0
    w["sm_bp"] = np.ascontiguousarray(np.stack(bs).reshape(4, QUADS, 128).transpose(2, 0, 1))
    w["sm_wv"] = slots(f["L1_attn_wv_w"])
    bv = slots(f["L1_attn_wv_b"][None])
    bv.reshape(HEADS, SLOT)[:, DK] = 1.0
    w["sm_bv"] = bv.reshape(-1)
    w["sm_wo"] = slot_rows(f["L1_attn_wo_w"])
    w["sm_bo"] = f["L1_attn_wo_b"].reshape(128, 1)
    w["ml_wf"] = np.ascontiguousarray(f["L1_ffn_W_fc"].T)
    w["ml_wp"] = np.ascontiguousarray(f["L1_ffn_W_proj"].T.reshape(MT, 128, D).transpose(1, 0, 2))
    w["ml_lnw"] = np.ascontiguousarray(f["L1_ffn_ln_w"].reshape(MT, 128).T)
    w["ml_lnb"] = np.ascontiguousarray(f["L1_ffn_ln_b"].reshape(MT, 128).T)
    return w


def kernel(**inputs):
    import concourse.bacc as bacc
    from concourse.bass_utils import run_bass_kernel_spmd

    nc = bacc.Bacc("TRN2", target_bir_lowering=False, num_devices=1)
    arrays, aps = {}, {}
    for name, a in layout(inputs).items():
        a = np.ascontiguousarray(a)
        arrays[f"in_{name}"] = a
        aps[name] = nc.dram_tensor(f"in_{name}", a.shape, mybir.dt.from_np(a.dtype), kind="ExternalInput").ap()
    out = nc.dram_tensor("out_x", (128, TOK), FP32, kind="ExternalOutput").ap()
    program(nc, aps, out)
    r = run_bass_kernel_spmd(nc, [arrays], core_ids=[0])
    return np.ascontiguousarray(r.results[0]["out_x"].T).reshape(SEQS, L, D)
```

```python
import concourse.bass as bass
from concourse import mybir
from contextlib import ExitStack
import numpy as np

FP32 = mybir.dt.float32
BF16 = mybir.dt.bfloat16
F32R = mybir.dt.float32r
ALU = mybir.AluOpType
ACT = mybir.ActivationFunctionType
AX = mybir.AxisListType

D = 128
SEQS = 8
L = 512
TOK = SEQS * L
CH = 512
TILE = 128
TPS = L // TILE
HEADS = 16
DK = D // HEADS
SLOT = 32
SPLIT = 3
MROW = SPLIT * DK
QUADS = HEADS * SLOT // 128
LN_EPS = 1e-5

DEPTH = 6
DH = 64
INNER = HEADS * DH
PAIRS = HEADS // 2
WIN = 32
WPT = TILE // WIN
HID = 341
HT = 3
HW = [128, 128, HID - 256]
PAD = 64
SEQP = L + 1
XCOLS = PAD + (SEQS + 1) * SEQP
MLP = 512
MT = MLP // 128


def col(b, t=0):
    return b * SEQP + (PAD + 1 + t)


def stand_alone(engine, passed):
    engine.sem_inc(passed, 1)


def layernorm_stage(nc, ps, sem, tag, src, dst, ones, eps, src2=None):
    with ExitStack() as c:
        sq = c.enter_context(nc.sbuf_tensor(f"sq_{tag}", [128, TOK], FP32))
        sd = c.enter_context(nc.sbuf_tensor(f"sd_{tag}", [128, TOK], FP32))
        summed = sem(f"summed_{tag}")
        mean_done = sem(f"mean_done_{tag}")
        centered = sem(f"centered_{tag}")
        squared = sem(f"squared_{tag}")
        var_done = sem(f"var_done_{tag}")
        std_done = sem(f"std_done_{tag}")
        rstd_done = sem(f"rstd_done_{tag}")
        with nc.Block() as block:

            @block.tensor
            def _(pe):
                with pe.Fori(0, SEQS) as i:
                    if src2 is not None:
                        pe.wait_ge(summed, i + 1)
                    nc.tensor.matmul(ps[:, bass.ds(i * CH, CH)], ones[:, :], src(i),
                                     start=True, stop=True).then_inc(mean_done, 1)
                with pe.Fori(0, SEQS) as i:
                    pe.wait_ge(squared, i + 1)
                    nc.tensor.matmul(ps[:, bass.ds(i * CH, CH)], ones[:, :], sq[:, bass.ds(i * CH, CH)],
                                     start=True, stop=True).then_inc(var_done, 1)

            @block.vector
            def _(dve):
                if src2 is not None:
                    with dve.Fori(0, SEQS) as i:
                        nc.vector.tensor_tensor(src(i), src(i), src2(i), ALU.add).then_inc(summed, 1)
                with dve.Fori(0, SEQS) as i:
                    dve.wait_ge(mean_done, i + 1)
                    nc.vector.tensor_tensor(dst(i), src(i), ps[:, bass.ds(i * CH, CH)],
                                            ALU.subtract).then_inc(centered, 1)
                with dve.Fori(0, SEQS) as i:
                    dve.wait_ge(std_done, i + 1)
                    nc.vector.reciprocal(sd[:, bass.ds(i * CH, CH)],
                                         sd[:, bass.ds(i * CH, CH)]).then_inc(rstd_done, 1)
                with dve.Fori(0, SEQS) as i:
                    dve.wait_ge(rstd_done, i + 1)
                    nc.vector.tensor_tensor(dst(i), dst(i), sd[:, bass.ds(i * CH, CH)], ALU.mult)

            @block.scalar
            def _(act):
                with act.Fori(0, SEQS) as i:
                    act.wait_ge(centered, i + 1)
                    nc.scalar.activation(sq[:, bass.ds(i * CH, CH)], dst(i), ACT.Square).then_inc(squared, 1)
                with act.Fori(0, SEQS) as i:
                    act.wait_ge(var_done, i + 1)
                    nc.scalar.activation(sd[:, bass.ds(i * CH, CH)], ps[:, bass.ds(i * CH, CH)], ACT.Sqrt,
                                         bias=eps[:, 0:1]).then_inc(std_done, 1)



def retention_stage(nc, ps, sem, w, xn, xr, eps):
    with ExitStack() as c:
        def sb(name, shape, dt=FP32):
            return c.enter_context(nc.sbuf_tensor(f"ret_{name}", shape, dt))

        wq = sb("wq", [128, 512])
        wk = sb("wk", [128, 512])
        wkc = sb("wkc", [128, 128])
        wv = sb("wv", [128, 512])
        wo = sb("wo", [128, QUADS, 128])
        small = sb("small", [128, HEADS])
        gam = sb("gam", [128, HEADS])
        lag = sb("lag", [128, L])
        decay = sb("decay", [128, HEADS, L])
        xcur = sb("xcur", [128, L])
        qt = sb("qt", [128, QUADS, L], F32R)
        kt = sb("kt", [128, QUADS, L], F32R)
        rest = sb("rest", [128, 2 * QUADS, L])
        split = sb("split", [128, 2, 2])
        vp = sb("vp", [128, TPS, 512])
        ksq = sb("ksq", [128, TPS, 128])
        krs = sb("krs", [128, TPS, HEADS])
        at = sb("at", [128, 2, TPS, L])
        yt = sb("yt", [128, QUADS, L])
        loaded = sem("ret_loaded")
        prep = sem("ret_prep")
        w_ready = sem("ret_w_ready")
        neg_ready = sem("ret_neg_ready")
        exp_ready = sem("ret_exp_ready")
        gamma_ready = sem("ret_gamma_ready")
        ln_ready = sem("ret_ln_ready")
        power_ready = sem("ret_power_ready")
        decay_ready = sem("ret_decay_ready")
        x_ready = sem("ret_x_ready")
        proj_done = sem("ret_proj_done")
        qk_read = sem("ret_qk_read")
        qk_ready = sem("ret_qk_ready")
        ksq_done = sem("ret_ksq_done")
        ksum_done = sem("ret_ksum_done")
        kstd_done = sem("ret_kstd_done")
        krs_done = sem("ret_krs_done")
        v_ready = sem("ret_v_ready")
        scores_done = sem("ret_scores_done")
        weights_done = sem("ret_weights_done")
        y_done = sem("ret_y_done")
        y_read = sem("ret_y_read")
        out_done = sem("ret_out_done")
        out_read = sem("ret_out_read")

        PQ = [ps[:, 0:CH], ps[:, CH:2 * CH]]
        PS = [ps[:, (2 + j) * CH:(3 + j) * CH] for j in range(TPS)]
        PY = ps[:, 6 * CH:7 * CH]
        PO = ps[:, 7 * CH:8 * CH]
        NQK = 2 * QUADS
        UNITS = NQK + 2 * TPS

        with nc.Block() as block:

            @block.sync
            def _(sp):
                sp.dma_start(wq[:, :], w["ret_wq"]).then_inc(loaded, 16)
                sp.dma_start(wkc[:, :], w["ret_wk"]).then_inc(loaded, 16)
                sp.dma_start(wv[:, :], w["ret_wv"]).then_inc(loaded, 16)
                sp.dma_start(wo[:, :, :], w["ret_wo"]).then_inc(loaded, 16)
                sp.dma_start(gam[:, :], w["log_gamma"].partition_broadcast(128)).then_inc(loaded, 16)
                sp.dma_start(lag[:, :], w["c_lag"]).then_inc(loaded, 16)
                sp.dma_start(split[:, :, :], w["c_split"]).then_inc(loaded, 16)

            @block.gpsimd
            def _(pool):
                nc.gpsimd.tensor_copy(xcur[:, :], xn(0)).then_inc(x_ready, 1)
                pool.wait_ge(power_ready, 1)
                nc.gpsimd.affine_select(out=decay[:, :, :], in_=decay[:, :, :], compare_op=ALU.is_ge, fill=0.0,
                                        base=0, pattern=[[0, HEADS], [1, L]],
                                        channel_multiplier=-1).then_inc(decay_ready, 1)
                with pool.Fori(1, SEQS) as b:
                    pool.wait_ge(proj_done, b * UNITS)
                    nc.gpsimd.tensor_copy(xcur[:, :], xn(b)).then_inc(x_ready, 1)

            @block.tensor
            def _(pe):
                def score(b, h):
                    g, r = h // 4, SLOT * (h % 4)
                    for j in range(TPS):
                        pe.wait_ge(weights_done, (b * HEADS + h) * TPS + (0 if h == 0 else j + 1 - TPS))
                        t0 = min(j * TILE, L - 2 * TILE)
                        nc.tensor.matmul(PS[j][:, 0:L - t0], kt[r:r + SLOT, g, j * TILE:(j + 1) * TILE],
                                         qt[r:r + SLOT, g, t0:L], start=True, stop=True).then_inc(scores_done, 1)

                def weigh(b, h):
                    g, r = h // 4, SLOT * (h % 4)
                    if h % 4 == 0:
                        pe.wait_ge(y_read, b * QUADS + g)
                    for j in range(TPS):
                        pe.wait_ge(weights_done, (b * HEADS + h) * TPS + (j + 1))
                        last = nc.tensor.matmul(PY[r:r + SLOT, j * TILE:L], vp[:, j, h * SLOT:(h + 1) * SLOT],
                                                at[:, h % 2, j, 0:L - j * TILE],
                                                start=(j == 0), stop=(j == TPS - 1))
                    last.then_inc(y_done, 1)

                pe.wait_ge(w_ready, SPLIT)
                with pe.Fori(0, SEQS) as b:
                    pe.wait_ge(x_ready, b + 1)
                    for u in range(UNITS):
                        if u == 0:
                            pe.wait_ge(ksq_done, b * TPS)
                        elif u == 1:
                            pe.wait_ge(v_ready, b * TPS)
                        elif u < NQK + 2:
                            pe.wait_ge(qk_read, b * NQK + (u - 1))
                        else:
                            pe.wait_ge((ksq_done, v_ready)[u % 2], b * TPS + (u - NQK) // 2)
                        if u < NQK:
                            g = u // 2
                            nc.tensor.matmul(PQ[u % 2], (wq, wk)[u % 2][:, g * 128:(g + 1) * 128], xcur[:, :],
                                             start=True, stop=True).then_inc(proj_done, 1)
                        else:
                            t = (u - NQK) // 2
                            rhs, n = ((wkc, 128), (wv, 512))[u % 2]
                            nc.tensor.matmul(PQ[u % 2][:, 0:n], xcur[:, t * TILE:(t + 1) * TILE], rhs[:, :],
                                             start=True, stop=True).then_inc(proj_done, 1)
                    pe.wait_ge(v_ready, b * TPS + TPS)
                    pe.wait_ge(qk_ready, b * NQK + NQK)
                    score(b, 0)
                    for h in range(1, HEADS):
                        score(b, h)
                        weigh(b, h - 1)
                    weigh(b, HEADS - 1)
                    pe.wait_ge(y_read, b * QUADS + QUADS)
                    pe.wait_ge(out_read, b)
                    for g in range(QUADS):
                        last = nc.tensor.matmul(PO, wo[:, g, :], yt[:, g, :],
                                                start=(g == 0), stop=(g == QUADS - 1))
                    last.then_inc(out_done, 1)

            @block.vector
            def _(dve):
                steps = [0]

                def link(ins):
                    steps[0] += 1
                    ins.then_inc(prep, 1)
                    dve.wait_ge(prep, steps[0])

                dve.wait_ge(loaded, 112)
                wk3 = wkc[:, :].rearrange("p (h d) -> p h d", d=DK)
                link(nc.vector.tensor_reduce(small[:, :], wk3, AX.X, ALU.add))
                link(nc.vector.tensor_scalar(small[:, :], small[:, :], 1.0 / DK, None, ALU.mult))
                link(nc.vector.memset(wk[:, :], 0.0))
                link(nc.vector.tensor_tensor(wk3, wk3, small[:, :].unsqueeze(2).broadcast_to([128, HEADS, DK]),
                                             ALU.subtract))
                for i in range(SPLIT):
                    nc.vector.tensor_copy(wk[:, :].rearrange("p (h s) -> p h s", s=SLOT)[:, :, i * DK:(i + 1) * DK],
                                          wk3).then_inc(w_ready, 1)
                link(nc.vector.tensor_scalar(gam[:, :], gam[:, :], -1.0, 80.0, ALU.mult, ALU.min))
                nc.vector.tensor_scalar(gam[:, :], gam[:, :], -80.0, None, ALU.max).then_inc(neg_ready, 1)
                dve.wait_ge(exp_ready, 1)
                link(nc.vector.tensor_scalar(gam[:, :], gam[:, :], 1.0, None, ALU.add))
                link(nc.vector.reciprocal(gam[:, :], gam[:, :]))
                nc.vector.tensor_scalar(gam[:, :], gam[:, :], 2.0 ** -64, None, ALU.max).then_inc(gamma_ready, 1)
                with dve.Fori(0, SEQS) as b:
                    for u in range(UNITS):
                        t = (u - NQK) // 2
                        if u < NQK:
                            dve.wait_ge(qk_read, b * NQK + (u + 1))
                            o = (qt, kt)[u % 2][:, u // 2, :]
                            nc.vector.scalar_tensor_tensor(o, o.bitcast(FP32), split[:, u % 2, 0:1], rest[:, u, :],
                                                           ALU.mult, ALU.add).then_inc(qk_ready, 1)
                        elif u % 2 == 0:
                            dve.wait_ge(ksq_done, b * TPS + (t + 1))
                            nc.vector.tensor_reduce(krs[:, t, :], ksq[:, t, :].rearrange("p (h d) -> p h d", d=DK),
                                                    AX.X, ALU.add).then_inc(ksum_done, 1)
                        else:
                            dve.wait_ge(proj_done, b * UNITS + (u + 1))
                            dve.wait_ge(kstd_done, b * TPS + (t + 1))
                            nc.vector.reciprocal(krs[:, t, :], krs[:, t, :]).then_inc(krs_done, 1)
                            dve.wait_ge(krs_done, b * TPS + (t + 1))
                            nc.vector.tensor_tensor(vp[:, t, :].rearrange("p (h s) -> p h s", s=SLOT),
                                                    PQ[1].rearrange("p (h s) -> p h s", s=SLOT),
                                                    krs[:, t, :].unsqueeze(2).broadcast_to([128, HEADS, SLOT]),
                                                    ALU.mult).then_inc(v_ready, 1)
                    dve.wait_ge(decay_ready, 1)
                    for h in range(HEADS):
                        for j in range(TPS):
                            dve.wait_ge(scores_done, (b * HEADS + h) * TPS + (j + 1))
                            if j == 0 and h >= 2:
                                dve.wait_ge(y_done, b * HEADS + (h - 1))
                            n = L - j * TILE
                            o = j * TILE - min(j * TILE, L - 2 * TILE)
                            nc.vector.tensor_tensor(at[:, h % 2, j, 0:n], PS[j][:, o:o + n], decay[:, h, 0:n],
                                                    ALU.mult).then_inc(weights_done, 1)
                    dve.wait_ge(out_done, b + 1)
                    nc.vector.tensor_tensor(xr(b), xr(b), PO, ALU.add).then_inc(out_read, 1)

            @block.scalar
            def _(act):
                act.wait_ge(neg_ready, 1)
                nc.scalar.activation(gam[:, :], gam[:, :], ACT.Exp).then_inc(exp_ready, 1)
                act.wait_ge(gamma_ready, 1)
                nc.scalar.activation(small[:, :], gam[:, :], ACT.Ln).then_inc(ln_ready, 1)
                act.wait_ge(ln_ready, 1)
                for h in range(HEADS):
                    last = nc.scalar.activation(decay[:, h, :], lag[:, :], ACT.Exp, scale=small[:, h:h + 1])
                last.then_inc(power_ready, 1)
                with act.Fori(0, SEQS) as b:
                    for u in range(NQK):
                        act.wait_ge(proj_done, b * UNITS + (u + 1))
                        nc.scalar.activation((qt, kt)[u % 2][:, u // 2, :], PQ[u % 2], ACT.Copy)
                        nc.scalar.activation(rest[:, u, :], PQ[u % 2], ACT.Copy,
                                             scale=split[:, u % 2, 1:2]).then_inc(qk_read, 1)
                    for t in range(TPS):
                        act.wait_ge(proj_done, b * UNITS + (NQK + 2 * t + 1))
                        nc.scalar.activation(ksq[:, t, :], PQ[0][:, 0:128], ACT.Square).then_inc(ksq_done, 1)
                        act.wait_ge(ksum_done, b * TPS + (t + 1))
                        nc.scalar.activation(krs[:, t, :], krs[:, t, :], ACT.Sqrt, scale=1.0 / DK,
                                             bias=eps[:, 0:1]).then_inc(kstd_done, 1)
                    for g in range(QUADS):
                        act.wait_ge(y_done, b * HEADS + 4 * (g + 1))
                        nc.scalar.activation(yt[:, g, :], PY, ACT.Copy).then_inc(y_read, 1)


def softmax_stage(nc, ps, sem, w, xn, xr, ident):
    with ExitStack() as c:
        def sb(name, shape, dt=FP32):
            return c.enter_context(nc.sbuf_tensor(f"sm_{name}", shape, dt))

        NP = 4 * QUADS
        wp = sb("wp", [128, 4, 512])
        bp = sb("bp", [128, 4, QUADS])
        wv = sb("wv", [128, 512])
        bv = sb("bv", [128, 512])
        wo = sb("wo", [128, QUADS, 128])
        bo = sb("bo", [128, 1])
        rope = sb("rope", [128, 4, L])
        bsel = sb("bsel", [128, 128])
        xcur = sb("xcur", [128, L])
        raw = sb("raw", [128, 2 * QUADS, L])
        part = sb("part", [128, 2 * QUADS, L])
        qk = sb("qk", [128, 2 * QUADS, L], F32R)
        split = sb("split", [128, 2, 2])
        vp = sb("vp", [128, TPS, 512])
        nmax = sb("nmax", [128, QUADS, TPS, 128])
        pt = sb("pt", [128, 2, TPS, L])
        yt = sb("yt", [128, QUADS, L])
        rden = sb("rden", [128, QUADS, L])
        loaded = sem("sm_loaded")
        nmax_zero = sem("sm_nmax_zero")
        pool_passed = sem("sm_pool_passed")
        x_ready = sem("sm_x_ready")
        proj_done = sem("sm_proj_done")
        proj_read = sem("sm_proj_read")
        rot_ready = sem("sm_rot_ready")
        hi_ready = sem("sm_hi_ready")
        qk_ready = sem("sm_qk_ready")
        scores_done = sem("sm_scores_done")
        max_done = sem("sm_max_done")
        maxt_done = sem("sm_maxt_done")
        q_ready = sem("sm_q_ready")
        keyed_done = sem("sm_keyed_done")
        exp_done = sem("sm_exp_done")
        y_done = sem("sm_y_done")
        y_read = sem("sm_y_read")
        den_done = sem("sm_den_done")
        rden_done = sem("sm_rden_done")
        norm_done = sem("sm_norm_done")
        out_done = sem("sm_out_done")
        out_read = sem("sm_out_read")

        PQ = [ps[:, 0:CH], ps[:, CH:2 * CH]]
        PS = [ps[:, (2 + j) * CH:(3 + j) * CH] for j in range(TPS)]
        PY = ps[:, 6 * CH:7 * CH]
        PO = ps[:, 7 * CH:8 * CH]
        UNITS = NP + TPS

        with nc.Block() as block:

            @block.sync
            def _(sp):
                for dst, name in ((wp[:, :, :], "sm_wp"), (bp[:, :, :], "sm_bp"), (wv[:, :], "sm_wv"),
                                  (wo[:, :, :], "sm_wo"), (bo[:, :], "sm_bo"), (rope[:, :, :], "c_rope"),
                                  (bsel[:, :], "c_bsel"), (split[:, :, :], "c_split")):
                    sp.dma_start(dst, w[name]).then_inc(loaded, 16)
                sp.dma_start(bv[:, :], w["sm_bv"].partition_broadcast(128)).then_inc(loaded, 16)

            @block.gpsimd
            def _(pool):
                nc.gpsimd.memset(nmax[:, :, :, :], 0.0).then_inc(nmax_zero, 1)
                nc.gpsimd.tensor_copy(xcur[:, :], xn(0)).then_inc(x_ready, 1)
                with pool.Fori(0, SEQS) as b:
                    for i in range(2 * QUADS):
                        pool.wait_ge(proj_read, b * UNITS + 2 * (i + 1))
                        nc.gpsimd.tensor_tensor(raw[:, i, :], raw[:, i, :], part[:, i, :],
                                                ALU.add).then_inc(rot_ready, 1)
                    pool.wait_ge(proj_done, b * UNITS + UNITS)
                    stand_alone(pool, pool_passed)
                    nc.gpsimd.tensor_copy(xcur[:, :], xn(b + 1)).then_inc(x_ready, 1)

            @block.tensor
            def _(pe):
                def maxima(b, g):
                    if g == 0:
                        pe.wait_ge(qk_ready, b * 2 * QUADS + 2 * QUADS)
                        pe.wait_ge(rden_done, b * QUADS)
                    elif g == 1:
                        pe.wait_ge(max_done, b * HEADS * TPS + 4 * TPS)
                    else:
                        pe.wait_ge(exp_done, b * HEADS * TPS + 4 * (g - 1) * TPS)
                    for i in range(TPS):
                        for r in range(4):
                            n = (g * TPS + i) * 4 + r
                            if i:
                                pe.wait_ge(max_done, b * HEADS * TPS + (n - 3))
                            nc.tensor.matmul(PS[r], qk[r * SLOT:(r + 1) * SLOT, g, i * TILE:(i + 1) * TILE],
                                             qk[r * SLOT:(r + 1) * SLOT, QUADS + g, :],
                                             start=True, stop=True).then_inc(scores_done, 1)

                def transposed_maxima(b, g):
                    pe.wait_ge(max_done, b * HEADS * TPS + (g + 1) * 4 * TPS)
                    if g == 0:
                        pe.wait_ge(out_read, b)
                    else:
                        pe.wait_ge(q_ready, b * QUADS + g)
                    for i in range(TPS):
                        last = nc.tensor.transpose(PO[:, i * TILE:(i + 1) * TILE], nmax[:, g, i, :], ident[:, :])
                    last.then_inc(maxt_done, 1)

                def keyed(b, h):
                    g, r = h // 4, SLOT * (h % 4)
                    if r == 0:
                        pe.wait_ge(q_ready, b * QUADS + (g + 1))
                        if g + 1 < QUADS:
                            pe.wait_ge(max_done, b * HEADS * TPS + (g + 2) * 4 * TPS)
                        else:
                            pe.wait_ge(exp_done, (b * HEADS + h) * TPS)
                    for j in range(TPS):
                        if r:
                            pe.wait_ge(exp_done, (b * HEADS + h) * TPS + (j + 1 - TPS))
                        nc.tensor.matmul(PS[j], qk[r:r + SLOT, QUADS + g, j * TILE:(j + 1) * TILE],
                                         qk[r:r + SLOT, g, :], start=True, stop=True).then_inc(keyed_done, 1)

                def weigh(b, h):
                    g, r = h // 4, SLOT * (h % 4)
                    if r == 0:
                        pe.wait_ge(y_read, b * QUADS + g)
                    for j in range(TPS):
                        pe.wait_ge(exp_done, (b * HEADS + h) * TPS + (j + 1))
                        last = nc.tensor.matmul(PY[r:r + SLOT, :], vp[:, j, h * SLOT:(h + 1) * SLOT],
                                                pt[:, h % 2, j, :], start=(j == 0), stop=(j == TPS - 1))
                    last.then_inc(y_done, 1)

                pe.wait_ge(loaded, 144)
                pe.wait_ge(nmax_zero, 1)
                with pe.Fori(0, SEQS) as b:
                    pe.wait_ge(x_ready, b + 1)
                    for u in range(UNITS):
                        pe.wait_ge(proj_read, b * UNITS + max(u - 1, 0))
                        if u < NP:
                            g, kind = (u // 2) % QUADS, 2 * (u // (2 * QUADS)) + u % 2
                            nc.tensor.matmul(PQ[u % 2], wp[:, kind, g * 128:(g + 1) * 128], xcur[:, :],
                                             start=True, stop=True).then_inc(proj_done, 1)
                        else:
                            t = u - NP
                            nc.tensor.matmul(PQ[u % 2], xcur[:, t * TILE:(t + 1) * TILE], wv[:, :],
                                             start=True, stop=True).then_inc(proj_done, 1)
                    maxima(b, 0)
                    pe.wait_ge(proj_read, b * UNITS + UNITS)
                    for h in range(HEADS):
                        if h % 4 == 0:
                            if h // 4 + 1 < QUADS:
                                maxima(b, h // 4 + 1)
                            transposed_maxima(b, h // 4)
                        keyed(b, h)
                        if h:
                            weigh(b, h - 1)
                    weigh(b, HEADS - 1)
                    for g in range(QUADS):
                        pe.wait_ge(y_read, b * QUADS + (g + 1))
                        nc.tensor.matmul(PS[g], bsel[:, :], yt[:, g, :], start=True, stop=True).then_inc(den_done, 1)
                    for g in range(QUADS):
                        pe.wait_ge(norm_done, b * QUADS + (g + 1))
                        last = nc.tensor.matmul(PO, wo[:, g, :], yt[:, g, :], start=(g == 0), stop=(g == QUADS - 1))
                    last.then_inc(out_done, 1)

            @block.vector
            def _(dve):
                dve.wait_ge(loaded, 144)
                dve.wait_ge(nmax_zero, 1)
                with dve.Fori(0, SEQS) as b:
                    def unite(i):
                        dve.wait_ge(hi_ready, b * 2 * QUADS + (i + 1))
                        nc.vector.scalar_tensor_tensor(qk[:, i, :], qk[:, i, :].bitcast(FP32),
                                                       split[:, i // QUADS, 0:1], part[:, i, :], ALU.mult,
                                                       ALU.add).then_inc(qk_ready, 1)

                    for u in range(UNITS):
                        dve.wait_ge(proj_done, b * UNITS + (u + 1))
                        if u < NP:
                            g, kind = (u // 2) % QUADS, 2 * (u // (2 * QUADS)) + u % 2
                            nc.vector.scalar_tensor_tensor((raw, part)[u % 2][:, u // 2, :], PQ[u % 2],
                                                           bp[:, kind, g:g + 1], rope[:, kind, :], ALU.add,
                                                           ALU.mult).then_inc(proj_read, 1)
                        else:
                            nc.vector.tensor_tensor(vp[:, u - NP, :], PQ[u % 2], bv[:, :],
                                                    ALU.add).then_inc(proj_read, 1)
                        if u >= 4 and u % 2 == 0:
                            unite((u - 4) // 2)

                    def take_maxima(g):
                        for i in range(TPS):
                            for r in range(4):
                                n = (g * TPS + i) * 4 + r
                                dve.wait_ge(scores_done, b * HEADS * TPS + (n + 1))
                                nc.vector.tensor_reduce(nmax[:, g, i, r * SLOT + MROW:r * SLOT + MROW + 1],
                                                        PS[r],
                                                        AX.X, ALU.max, negate=True).then_inc(max_done, 1)

                    take_maxima(0)
                    for g in range(QUADS):
                        if g + 1 < QUADS:
                            take_maxima(g + 1)
                        dve.wait_ge(maxt_done, b * QUADS + (g + 1))
                        nc.vector.tensor_tensor(qk[:, g, :], qk[:, g, :].bitcast(FP32), PO,
                                                ALU.add).then_inc(q_ready, 1)
                    for g in range(QUADS):
                        dve.wait_ge(den_done, b * QUADS + (g + 1))
                        nc.vector.reciprocal(rden[:, g, :], PS[g]).then_inc(rden_done, 1)
                    for g in range(QUADS):
                        dve.wait_ge(rden_done, b * QUADS + (g + 1))
                        nc.vector.tensor_tensor(yt[:, g, :], yt[:, g, :], rden[:, g, :], ALU.mult).then_inc(norm_done, 1)
                    dve.wait_ge(out_done, b + 1)
                    nc.vector.scalar_tensor_tensor(xr(b), PO, bo[:, 0:1], xr(b), ALU.add, ALU.add).then_inc(out_read, 1)

            @block.scalar
            def _(act):
                act.wait_ge(loaded, 144)
                with act.Fori(0, SEQS) as b:
                    for i in range(2 * QUADS):
                        act.wait_ge(rot_ready, b * 2 * QUADS + (i + 1))
                        nc.scalar.activation(qk[:, i, :], raw[:, i, :], ACT.Copy)
                        nc.scalar.activation(part[:, i, :], raw[:, i, :], ACT.Copy,
                                             scale=split[:, i // QUADS, 1:2]).then_inc(hi_ready, 1)
                    for h in range(HEADS):
                        for j in range(TPS):
                            act.wait_ge(keyed_done, (b * HEADS + h) * TPS + (j + 1))
                            if j == 0 and h >= 2:
                                act.wait_ge(y_done, b * HEADS + (h - 1))
                            nc.scalar.activation(pt[:, h % 2, j, :], PS[j], ACT.Exp).then_inc(exp_done, 1)
                        if h % 4 == 3:
                            g = h // 4
                            act.wait_ge(y_done, b * HEADS + (h + 1))
                            nc.scalar.activation(yt[:, g, :], PY, ACT.Copy).then_inc(y_read, 1)

def transformer_stage(nc, ps, sem, w, xa, xb, ones, eps, ident):
    with ExitStack() as c:
        def sb(name, shape, dt=FP32):
            return c.enter_context(nc.sbuf_tensor(f"tr_{name}", shape, dt))

        NQKV = TPS * SEQS + 1
        UNITS = 8
        QKV0 = 3 * INNER

        wqkv = sb("wqkv", [128, QKV0])
        wo = sb("wo", [128, PAIRS, 128])
        w1 = sb("w1", [128, 2 * HID])
        w2 = sb("w2", [128, HT, 128])
        b1 = sb("b1", [128, 2 * HT])
        b2 = sb("b2", [128, 1])
        lng = sb("lng", [128, 1])
        lnb = sb("lnb", [128, 1])
        qks = sb("qks", [128, 2, DH])
        base = sb("base", [128, 4, TPS, DH])
        rope = sb("rope", [128, 4, TPS, DH])
        identb = sb("identb", [128, 128], BF16)
        mask = sb("mask", [128, 2, PAIRS * 2 * WIN], BF16)
        half = sb("half", [128, 2 * HEADS])
        xs = sb("xs", [128, 2, WIN + TILE])
        va = sb("va", [128, 2, INNER])
        vb = sb("vb", [128, 2, INNER])
        qm = sb("qm", [128, 2, 4, CH])
        raw = sb("raw", [128, 4, CH])
        sqr = sb("sqr", [128, 2, CH])
        ss = sb("ss", [128, 2 * HEADS])
        rn = sb("rn", [128, 2, 2 * HEADS])
        qt = sb("qt", [128, PAIRS, TILE])
        kt = sb("kt", [128, 2, PAIRS, WIN + TILE])
        mx = sb("mx", [128, 2, PAIRS])
        nb = sb("nb", [128, 2, PAIRS])
        pw = sb("pw", [128, HEADS + 1, 2 * WIN])
        rs = sb("rs", [128, HEADS])
        rr = sb("rr", [128, HEADS])
        pt = sb("pt", [128, HEADS, TILE])
        on = sb("on", [128, INNER])
        ot = sb("ot", [128, PAIRS, L])
        xf = sb("xf", [128, TOK])
        hb = sb("hb", [128, 2, HT, CH])
        fsq = ot[:, :, :].rearrange("p a b -> p (a b)")
        fsd = qm[:, :, :, :].rearrange("p a b c -> p (a b c)")

        const_loaded = sem("tr_const_loaded")
        pe_passed = sem("tr_pe_passed")
        dve_passed = sem("tr_dve_passed")
        pool_passed = sem("tr_pool_passed")
        attn_loaded = sem("tr_attn_loaded")
        mlp_loaded = sem("tr_mlp_loaded")
        init_done = sem("tr_init_done")
        scales_done = sem("tr_scales_done")
        xs_ready = sem("tr_xs_ready")
        proj_done = sem("tr_proj_done")
        v_copied = sem("tr_v_copied")
        rot_done = sem("tr_rot_done")
        raw_ready = sem("tr_raw_ready")
        ksq_done = sem("tr_ksq_done")
        qsq_done = sem("tr_qsq_done")
        ss_done = sem("tr_ss_done")
        pool_step = sem("tr_pool_step")
        q_ready = sem("tr_q_ready")
        norms_ready = sem("tr_norms_ready")
        k_ready = sem("tr_k_ready")
        turn_done = sem("tr_turn_done")
        turn_read = sem("tr_turn_read")
        kprev_done = sem("tr_kprev_done")
        scores_done = sem("tr_scores_done")
        max_done = sem("tr_max_done")
        bias_ready = sem("tr_bias_ready")
        exp_done = sem("tr_exp_done")
        again_done = sem("tr_again_done")
        pv_done = sem("tr_pv_done")
        rsum_done = sem("tr_rsum_done")
        on_ready = sem("tr_on_ready")
        wo_done = sem("tr_wo_done")
        xb_ready = sem("tr_xb_ready")
        xf_ready = sem("tr_xf_ready")
        mean_done = sem("tr_mean_done")
        centered = sem("tr_centered")
        squared = sem("tr_squared")
        var_done = sem("tr_var_done")
        std_done = sem("tr_std_done")
        rstd_done = sem("tr_rstd_done")
        normed = sem("tr_normed")
        xn_ready = sem("tr_xn_ready")
        hid_done = sem("tr_hid_done")
        gelu_done = sem("tr_gelu_done")
        hid_ready = sem("tr_hid_ready")
        mlp_done = sem("tr_mlp_done")
        xa_ready = sem("tr_xa_ready")

        P2 = [ps[:, 0:CH], ps[:, CH:2 * CH]]
        PT = [ps[:, 2 * CH:3 * CH], ps[:, 3 * CH:4 * CH]]
        PS = [ps[:, 4 * CH:5 * CH], ps[:, 5 * CH:6 * CH]]
        PV = [ps[:, 6 * CH:7 * CH], ps[:, 7 * CH:8 * CH]]
        TURNS = 10
        LTURNS = TURNS * TPS * SEQS + 4
        MLPU = 2 * HT

        attn_weights = ((wqkv[:, :], "tr_wqkv"), (wo[:, :, :].rearrange("p a b -> p (a b)"), "tr_wo"))
        mlp_weights = ((w1[:, :], "tr_w1"), (w2[:, :, :].rearrange("p a b -> p (a b)"), "tr_w2"),
                       (b1[:, :], "tr_b1"), (b2[:, :], "tr_b2"), (lng[:, :], "tr_lng"), (lnb[:, :], "tr_lnb"))
        CONST_LOADS = 48
        ATTN_LOADS = 16 * (len(attn_weights) + 1)
        MLP_LOADS = 16 * len(mlp_weights)

        def tile_heads(ap):
            return ap.rearrange("p (h d) -> p h d", d=DH)

        with nc.Block() as block:

            @block.sync
            def _(sp):
                sp.dma_start(base[:, :, :, :], w["c_xpos"]).then_inc(const_loaded, 16)
                sp.dma_start(identb[:, :], w["c_identb"]).then_inc(const_loaded, 16)
                sp.dma_start(mask[:, :, :], w["c_mask"]).then_inc(const_loaded, 16)
                with sp.Fori(0, DEPTH) as l:
                    sp.wait_ge(xb_ready, l * 2 * SEQS)
                    for dst, name in attn_weights:
                        sp.dma_start(dst, w[name][bass.ds(l * 128, 128), :]).then_inc(attn_loaded, 16)
                    sp.dma_start(qks[:, :, :].rearrange("p a b -> p (a b)"),
                                 w["tr_qks"][bass.ds(l * 128, 128), :]).then_inc(attn_loaded, 16)
                    sp.wait_ge(xa_ready, l * SEQS)
                    for dst, name in mlp_weights:
                        sp.dma_start(dst, w[name][bass.ds(l * 128, 128), :]).then_inc(mlp_loaded, 16)

            @block.gpsimd
            def _(pool):
                def square_k(q, i):
                    pool.wait_ge(raw_ready, q * 4 + (i + 1))
                    if i == 0:
                        pool.wait_ge(ss_done, q * 2)
                    nc.gpsimd.tensor_tensor(sqr[:, i, :], raw[:, 2 + i, :], raw[:, 2 + i, :],
                                            ALU.mult).then_inc(ksq_done, 1)

                def inverse_norms(q, par, i):
                    cols = slice(HEADS, 2 * HEADS) if i == 0 else slice(0, HEADS)
                    pool.wait_ge(ss_done, q * 2 + (i + 1))
                    stand_alone(pool, pool_passed)
                    nc.gpsimd.tensor_scalar(ss[:, cols], ss[:, cols], 1e-24, None, ALU.max).then_inc(pool_step, 1)
                    pool.wait_ge(pool_step, q * 5 + (2 + 2 * i))
                    nc.gpsimd.tensor_tensor(rn[:, par, cols], ss[:, cols], half[:, cols],
                                            ALU.pow).then_inc(pool_step, 1)
                    pool.wait_ge(pool_step, q * 5 + (3 + 2 * i))

                def finish(q, par):
                    pool.wait_ge(rot_done, q * 4 + 2)
                    nc.gpsimd.tensor_tensor(qm[:, 0, 2:4, :], qm[:, 0, 2:4, :], qm[:, 1, 2:4, :],
                                            ALU.add).then_inc(pool_step, 1)
                    inverse_norms(q, par, 0)
                    k3 = qm[:, 0, 2:4, :].rearrange("p a (h d) -> p (a h) d", d=DH)
                    nc.gpsimd.tensor_tensor(k3, k3, rn[:, par, HEADS:].unsqueeze(2).broadcast_to([128, HEADS, DH]),
                                            ALU.mult).then_inc(k_ready, 1)
                    pool.wait_ge(rot_done, q * 4 + 4)
                    nc.gpsimd.tensor_tensor(qm[:, 0, 0:2, :], qm[:, 0, 0:2, :], qm[:, 1, 0:2, :],
                                            ALU.add).then_inc(q_ready, 1)
                    inverse_norms(q, par, 1)
                    stand_alone(pool, pool_passed)
                    nc.gpsimd.tensor_scalar(rn[:, par, 0:HEADS], rn[:, par, 0:HEADS], 8.0, None,
                                            ALU.mult).then_inc(norms_ready, 1)

                nc.gpsimd.memset(half[:, :], -0.5).then_inc(init_done, 1)
                nc.gpsimd.memset(kt[:, :, :, :], 0.0).then_inc(init_done, 1)
                pool.wait_ge(init_done, 2)
                with pool.Fori(0, DEPTH) as l:
                    pool.wait_ge(exp_done, l * (HEADS * TPS * SEQS))
                    square_k(l * NQKV, 0)
                    square_k(l * NQKV, 1)
                    finish(l * NQKV, 0)
                    with pool.Fori(0, SEQS) as b:
                        for p in range(TPS):
                            q = l * NQKV + b * TPS + (p + 1)
                            n = (l * SEQS + b) * TPS + p
                            square_k(q, 0)
                            pool.wait_ge(exp_done, n * HEADS + 1)
                            stand_alone(pool, pool_passed)
                            nc.gpsimd.tensor_copy(pw[:, HEADS, :], pw[:, 0, :]).then_inc(again_done, 1)
                            square_k(q, 1)
                            finish(q, (p + 1) % 2)

            @block.tensor
            def _(pe):
                def project(q, par):
                    pe.wait_ge(xs_ready, q * 2 + 2)
                    for u in range(UNITS):
                        if u == 0:
                            pe.wait_ge(v_copied, q * 4)
                        elif u in (2, 3, 6, 7):
                            pe.wait_ge(raw_ready, q * 4 + (u - 1 if u < 4 else u - 3))
                        elif u >= 4:
                            pe.wait_ge(v_copied, q * 4 + (u - 3))
                        lhs = xs[:, par, 0:TILE] if u >= 6 else xs[:, par, WIN:WIN + TILE]
                        at = (1, 2, 0, 2)[u // 2] * INNER + (u % 2) * CH
                        nc.tensor.matmul(P2[u % 2], lhs, wqkv[:, at:at + CH], start=True, stop=True).then_inc(proj_done, 1)

                def turn(base, k, after_wo=False):
                    if after_wo is not False:
                        pe.wait_ge(xb_ready, after_wo)
                    else:
                        pe.wait_ge(turn_read, base + (k - 1))
                    return PT[k % 2]

                def turn_qk(q, base, first=False):
                    for k in range(4):
                        bank = PT[k % 2] if first and k < 2 else turn(base, k)
                        pe.wait_ge((k_ready, q_ready)[k // 2], q + 1)
                        for i in range(4):
                            last = nc.tensor.transpose(bank[:, i * 128:(i + 1) * 128],
                                                       qm[:, 0, (k + 2) % 4, i * 128:(i + 1) * 128], ident[:, :])
                        last.then_inc(turn_done, 1)

                with pe.Fori(0, DEPTH) as l:
                    pe.wait_ge(attn_loaded, (l + 1) * ATTN_LOADS)
                    project(l * NQKV, 0)
                    turn_qk(l * NQKV, l * LTURNS, first=True)
                    with pe.Fori(0, SEQS) as b:
                        for p in range(TPS):
                            q = l * NQKV + b * TPS + p
                            seq = l * SEQS + b
                            n = seq * TPS + p
                            par = p % 2
                            t0 = l * LTURNS + b * (TPS * TURNS) + (p * TURNS + 4)
                            pe.wait_ge(exp_done, n * HEADS)
                            pe.wait_ge(max_done, n * 2)
                            for e in range(2):
                                nc.tensor.matmul(PS[e], identb[:, :], mask[:, min(p, 1), :], start=True, stop=False,
                                                 skip_group_check=True)
                            pe.wait_ge(turn_read, t0 - 2 if p else t0)
                            pe.wait_ge(kprev_done, q + 1)
                            stand_alone(pe, pe_passed)
                            for hp in range(PAIRS):
                                for e in range(2):
                                    r = slice(64 * e, 64 * e + 64)
                                    for wi in range(WPT):
                                        last = nc.tensor.matmul(
                                            PS[e][wi * WIN:(wi + 1) * WIN, hp * 2 * WIN:(hp + 1) * 2 * WIN],
                                            qt[r, hp, wi * WIN:(wi + 1) * WIN],
                                            kt[r, par, hp, wi * WIN:(wi + 2) * WIN],
                                            start=False, stop=(hp == PAIRS - 1), skip_group_check=True)
                            last.then_inc(scores_done, 1)
                            project(q + 1, 1 - par)
                            for k in range(4):
                                bank = turn(t0, k, seq * 2 if p == 0 and k < 2 else False)
                                pe.wait_ge(exp_done, n * HEADS + min(4 * (k + 1) + 1, HEADS))
                                if k == 3:
                                    pe.wait_ge(again_done, n + 1)
                                for i in range(4):
                                    h = 4 * k + i
                                    last = nc.tensor.transpose(bank[:, i * 128:(i + 1) * 128],
                                                               pw[:, h:h + 2, :].rearrange("p a b -> p (a b)"),
                                                               ident[:, :])
                                last.then_inc(turn_done, 1)
                            pe.wait_ge(on_ready, n * 2)
                            pe.wait_ge(v_copied, q * 4 + 4)
                            for up in range(2):
                                for hh in range(2):
                                    pe.wait_ge(turn_read, t0 + (4 if up else 2 + 2 * hh))
                                    stand_alone(pe, pe_passed)
                                    for h in range(8 * hh, 8 * hh + 8):
                                        for wi in (2 * up, 2 * up + 1):
                                            r = slice(64 * up, 64 * up + 64)
                                            last = nc.tensor.matmul(
                                                PV[hh][wi * WIN:(wi + 1) * WIN, (h % 8) * DH:(h % 8 + 1) * DH],
                                                pt[r, (h - up) % HEADS, wi * WIN:(wi + 1) * WIN],
                                                (vb, va)[wi % 2][r, par, h * DH:(h + 1) * DH], start=True, stop=True)
                                    if up:
                                        last.then_inc(pv_done, 1)
                            turn_qk(q + 1, t0 + 4)
                            for k in range(2):
                                bank = turn(t0, 8 + k)
                                pe.wait_ge(on_ready, n * 2 + (k + 1))
                                for i in range(4):
                                    a = (4 * k + i) * 128
                                    last = nc.tensor.transpose(bank[:, i * 128:(i + 1) * 128], on[:, a:a + 128],
                                                               ident[:, :])
                                last.then_inc(turn_done, 1)
                        for k in range(2):
                            pe.wait_ge(turn_read, l * LTURNS + b * (TPS * TURNS) + (TPS * TURNS + 4))
                            for hp in range(PAIRS):
                                last = nc.tensor.matmul(PT[k][:, 0:L // 2], wo[:, hp, :],
                                                        ot[:, hp, k * (L // 2):(k + 1) * (L // 2)],
                                                        start=(hp == 0), stop=(hp == PAIRS - 1))
                            last.then_inc(wo_done, 1)
                    with pe.Fori(0, SEQS) as i:
                        pe.wait_ge(xf_ready, l * SEQS + (i + 1))
                        nc.tensor.matmul(ps[:, bass.ds(i * CH, CH)], ones[:, :], xf[:, bass.ds(i * CH, CH)],
                                         start=True, stop=True).then_inc(mean_done, 1)
                    with pe.Fori(0, SEQS) as i:
                        pe.wait_ge(squared, l * SEQS + (i + 1))
                        nc.tensor.matmul(ps[:, bass.ds(i * CH, CH)], ones[:, :], fsq[:, bass.ds(i * CH, CH)],
                                         start=True, stop=True).then_inc(var_done, 1)
                    pe.wait_ge(mlp_loaded, (l + 1) * MLP_LOADS)
                    pe.wait_ge(std_done, (l + 1) * SEQS)
                    stand_alone(pe, pe_passed)
                    with pe.Fori(0, SEQS // 2) as i2:
                        for par in range(2):
                            i = i2 * 2 + par
                            ch = l * SEQS + i
                            pe.wait_ge(xn_ready, ch + 1)
                            for j in range(HT):
                                for kind in range(2):
                                    pe.wait_ge((gelu_done, hid_ready)[kind], ch * HT)
                                    at = (1 - kind) * HID + j * 128
                                    nc.tensor.matmul(ps[0:HW[j], (2 * j + kind) * CH:(2 * j + kind + 1) * CH],
                                                     w1[:, at:at + HW[j]], xf[:, bass.ds(i * CH, CH)],
                                                     start=True, stop=True).then_inc(hid_done, 1)
                            pe.wait_ge(xa_ready, ch - par)
                            for j in range(HT):
                                pe.wait_ge(hid_ready, ch * HT + (j + 1))
                                last = nc.tensor.matmul(PV[par], w2[0:HW[j], j, :], hb[0:HW[j], par, j, :],
                                                        start=(j == 0), stop=(j == HT - 1))
                            last.then_inc(mlp_done, 1)

            @block.vector
            def _(dve):
                def shift(par, b, t):
                    c0 = b * SEQP + (PAD + 1 + t * TILE - WIN)
                    nc.vector.tensor_copy(xs[0:64, par, :], xa[0:64, bass.ds(c0, WIN + TILE)]).then_inc(xs_ready, 1)
                    nc.vector.tensor_copy(xs[64:128, par, :],
                                          xa[64:128, bass.ds(c0 - 1, WIN + TILE)]).then_inc(xs_ready, 1)

                def copy_v(q, par, i):
                    dve.wait_ge(proj_done, q * UNITS + (3, 4, 7, 8)[i])
                    nc.vector.tensor_copy((va, vb)[i // 2][:, par, (i % 2) * CH:(i % 2 + 1) * CH],
                                          P2[i % 2]).then_inc(v_copied, 1)

                def rotate(q, p, i):
                    u = (2, 3, 0, 1)[i]
                    dve.wait_ge(raw_ready, q * 4 + (i + 1))
                    src = tile_heads(raw[:, u, :])
                    cos, sin = (rope[:, 2 * (u // 2) + s, p, :].unsqueeze(1) for s in range(2))
                    nc.vector.tensor_tensor(tile_heads(qm[:, 0, u, :]), src, cos.broadcast_to([128, 8, DH]), ALU.mult)
                    rot = tile_heads(qm[:, 1, u, :])
                    h = DH // 2
                    nc.vector.tensor_tensor(rot[:, :, 0:h], src[:, :, h:DH], sin[:, :, 0:h].broadcast_to([128, 8, h]),
                                            ALU.mult)
                    nc.vector.tensor_tensor(rot[:, :, h:DH], src[:, :, 0:h], sin[:, :, h:DH].broadcast_to([128, 8, h]),
                                            ALU.mult).then_inc(rot_done, 1)

                def sum_squares(q, i):
                    cols = slice(HEADS, 2 * HEADS) if i == 0 else slice(0, HEADS)
                    if i == 0:
                        dve.wait_ge(norms_ready, q)
                    dve.wait_ge((ksq_done, qsq_done)[i], q * 2 + 2)
                    nc.vector.tensor_reduce(ss[:, cols], sqr[:, :, :].rearrange("p a (h d) -> p (a h) d", d=DH),
                                            AX.X, ALU.add).then_inc(ss_done, 1)

                def take(q, par, p):
                    rotate(q, p, 0)
                    copy_v(q, par, 0)
                    rotate(q, p, 1)
                    copy_v(q, par, 1)
                    sum_squares(q, 0)
                    rotate(q, p, 2)
                    copy_v(q, par, 2)
                    copy_v(q, par, 3)
                    rotate(q, p, 3)

                dve.wait_ge(const_loaded, CONST_LOADS)
                with dve.Fori(0, DEPTH) as l:
                    dve.wait_ge(attn_loaded, (l + 1) * ATTN_LOADS)
                    h = DH // 2
                    for s in range(2):
                        row = qks[:, s, :].unsqueeze(1)
                        nc.vector.tensor_tensor(rope[:, 2 * s, :, :], base[:, 2 * s, :, :],
                                                row.broadcast_to([128, TPS, DH]), ALU.mult)
                        nc.vector.tensor_tensor(rope[:, 2 * s + 1, :, 0:h], base[:, 2 * s + 1, :, 0:h],
                                                row[:, :, h:DH].broadcast_to([128, TPS, h]), ALU.mult)
                        last = nc.vector.tensor_tensor(rope[:, 2 * s + 1, :, h:DH], base[:, 2 * s + 1, :, h:DH],
                                                       row[:, :, 0:h].broadcast_to([128, TPS, h]), ALU.mult)
                    last.then_inc(scales_done, 1)
                    dve.wait_ge(scales_done, l + 1)
                    dve.wait_ge(xa_ready, l * SEQS)
                    shift(0, 0, 0)
                    take(l * NQKV, 0, 0)
                    sum_squares(l * NQKV, 1)
                    with dve.Fori(0, SEQS) as b:
                        for p in range(TPS):
                            q = l * NQKV + b * TPS + p
                            seq = l * SEQS + b
                            n = seq * TPS + p
                            par = p % 2
                            dve.wait_ge(proj_done, q * UNITS)
                            shift(1 - par, b + (p + 1) // TPS, (p + 1) % TPS)
                            dve.wait_ge(scores_done, n + 1)
                            for e in range(2):
                                nc.vector.tensor_reduce(mx[:, e, :], PS[e].rearrange("p (h j) -> p h j", j=2 * WIN),
                                                        AX.X, ALU.max).then_inc(max_done, 1)
                            dve.wait_ge(max_done, n * 2 + 2)
                            dve.wait_ge(norms_ready, q + 1)
                            nc.vector.scalar_tensor_tensor(
                                nb[:, :, :], mx[:, :, :], -1.0,
                                rn[:, par, 0:HEADS].rearrange("p (h e) -> p e h", e=2), ALU.mult,
                                ALU.mult).then_inc(bias_ready, 1)
                            dve.wait_ge(pv_done, n * 2)
                            take(q + 1, 1 - par, (p + 1) % TPS)
                            dve.wait_ge(exp_done, n * HEADS + HEADS)
                            nc.vector.reciprocal(rr[:, :], rs[:, :]).then_inc(rsum_done, 1)
                            sum_squares(q + 1, 1)
                            dve.wait_ge(rsum_done, n + 1)
                            for hh in range(2):
                                dve.wait_ge(pv_done, n * 2 + (hh + 1))
                                nc.vector.tensor_tensor(
                                    tile_heads(on[:, hh * CH:(hh + 1) * CH]), tile_heads(PV[hh]),
                                    rr[:, hh * 8:(hh + 1) * 8].unsqueeze(2).broadcast_to([128, 8, DH]),
                                    ALU.mult).then_inc(on_ready, 1)
                        for k in range(2):
                            dve.wait_ge(wo_done, (l * SEQS + b) * 2 + (k + 1))
                            cols = bass.ds(b * SEQP + (PAD + 1 + k * (L // 2)), L // 2)
                            nc.vector.tensor_tensor(xb[:, cols], PT[k][:, 0:L // 2], xa[:, cols],
                                                    ALU.add).then_inc(xb_ready, 1)
                    dve.wait_ge(xb_ready, (l + 1) * 2 * SEQS)
                    stand_alone(dve, dve_passed)
                    with dve.Fori(0, SEQS) as i:
                        nc.vector.tensor_copy(xf[0:64, bass.ds(i * CH, CH)], xb[0:64, bass.ds(i * SEQP + (PAD + 1), L)])
                        nc.vector.tensor_copy(xf[64:128, bass.ds(i * CH, CH)],
                                              xb[64:128, bass.ds(i * SEQP + PAD, L)]).then_inc(xf_ready, 1)
                    with dve.Fori(0, SEQS) as i:
                        dve.wait_ge(mean_done, l * SEQS + (i + 1))
                        x = xf[:, bass.ds(i * CH, CH)]
                        nc.vector.tensor_tensor(x, x, ps[:, bass.ds(i * CH, CH)], ALU.subtract).then_inc(centered, 1)
                    with dve.Fori(0, SEQS) as i:
                        dve.wait_ge(std_done, l * SEQS + (i + 1))
                        s = fsd[:, bass.ds(i * CH, CH)]
                        nc.vector.reciprocal(s, s).then_inc(rstd_done, 1)
                    with dve.Fori(0, SEQS) as i:
                        dve.wait_ge(rstd_done, l * SEQS + (i + 1))
                        x = xf[:, bass.ds(i * CH, CH)]
                        nc.vector.tensor_tensor(x, x, fsd[:, bass.ds(i * CH, CH)], ALU.mult).then_inc(normed, 1)
                    with dve.Fori(0, SEQS // 2) as i2:
                        for par in range(2):
                            i = i2 * 2 + par
                            ch = l * SEQS + i
                            for j in range(HT):
                                dve.wait_ge(hid_done, ch * MLPU + (2 * j + 2))
                                dve.wait_ge(gelu_done, ch * HT + (j + 1))
                                o = hb[0:HW[j], par, j, :]
                                nc.vector.scalar_tensor_tensor(o, ps[0:HW[j], (2 * j + 1) * CH:(2 * j + 2) * CH],
                                                               b1[0:HW[j], j:j + 1], o, ALU.add,
                                                               ALU.mult).then_inc(hid_ready, 1)
                            dve.wait_ge(mlp_done, ch + 1)
                            cols = bass.ds(i * SEQP + (PAD + 1), L)
                            nc.vector.scalar_tensor_tensor(xa[:, cols], PV[par], b2[:, 0:1], xb[:, cols], ALU.add,
                                                           ALU.add).then_inc(xa_ready, 1)

            @block.scalar
            def _(act):
                def take_raw(q, i):
                    if i == 0:
                        act.wait_ge(rot_done, q * 4)
                        act.wait_ge(ksq_done, q * 2)
                    act.wait_ge(proj_done, q * UNITS + (1, 2, 5, 6)[i])
                    nc.scalar.activation(raw[:, (2, 3, 0, 1)[i], :], P2[i % 2], ACT.Copy).then_inc(raw_ready, 1)

                def square_q(q):
                    act.wait_ge(ss_done, q * 2 + 1)
                    for i in range(2):
                        act.wait_ge(raw_ready, q * 4 + (i + 3))
                        nc.scalar.activation(sqr[:, i, :], raw[:, i, :], ACT.Square).then_inc(qsq_done, 1)

                def read_qk(par, base):
                    nc.scalar.activation(kt[:, par, :, 0:WIN], kt[:, 1 - par, :, TILE:WIN + TILE],
                                         ACT.Copy).then_inc(kprev_done, 1)
                    for k in range(4):
                        act.wait_ge(turn_done, base + (k + 1))
                        src = PT[k % 2].rearrange("p (i t) -> p i t", t=TILE)
                        o = 4 * (k % 2)
                        dst = kt[:, par, o:o + 4, WIN:WIN + TILE] if k < 2 else qt[:, o:o + 4, :]
                        nc.scalar.activation(dst, src, ACT.Copy).then_inc(turn_read, 1)

                act.wait_ge(init_done, 2)
                with act.Fori(0, DEPTH) as l:
                    for u in range(4):
                        take_raw(l * NQKV, u)
                    square_q(l * NQKV)
                    read_qk(0, l * LTURNS)
                    with act.Fori(0, SEQS) as b:
                        for p in range(TPS):
                            q = l * NQKV + b * TPS + p
                            seq = l * SEQS + b
                            n = seq * TPS + p
                            par = p % 2
                            t0 = l * LTURNS + b * (TPS * TURNS) + (p * TURNS + 4)
                            take_raw(q + 1, 0)
                            act.wait_ge(bias_ready, n + 1)
                            for j in range(4):
                                for hd in range(4 * j, 4 * j + 4):
                                    e, hp = hd % 2, hd // 2
                                    nc.scalar.activation(pw[:, hd, :], PS[e][:, hp * 2 * WIN:(hp + 1) * 2 * WIN],
                                                         ACT.Exp, bias=nb[:, e, hp:hp + 1],
                                                         scale=rn[:, par, hd:hd + 1],
                                                         accum_out=rs[:, hd:hd + 1]).then_inc(exp_done, 1)
                                if j < 3:
                                    take_raw(q + 1, j + 1)
                            for k in range(4):
                                act.wait_ge(turn_done, t0 + (k + 1))
                                nc.scalar.activation(pt[:, 4 * k:4 * k + 4, :],
                                                     PT[k % 2].rearrange("p (i t) -> p i t", t=TILE),
                                                     ACT.Copy).then_inc(turn_read, 1)
                            square_q(q + 1)
                            read_qk(1 - par, t0 + 4)
                            for k in range(2):
                                act.wait_ge(turn_done, t0 + (k + 9))
                                nc.scalar.activation(ot[:, 4 * k:4 * k + 4, p * TILE:(p + 1) * TILE],
                                                     PT[k % 2].rearrange("p (i t) -> p i t", t=TILE),
                                                     ACT.Copy).then_inc(turn_read, 1)
                    with act.Fori(0, SEQS) as i:
                        act.wait_ge(centered, l * SEQS + (i + 1))
                        nc.scalar.activation(fsq[:, bass.ds(i * CH, CH)], xf[:, bass.ds(i * CH, CH)],
                                             ACT.Square).then_inc(squared, 1)
                    with act.Fori(0, SEQS) as i:
                        act.wait_ge(var_done, l * SEQS + (i + 1))
                        nc.scalar.activation(fsd[:, bass.ds(i * CH, CH)], ps[:, bass.ds(i * CH, CH)], ACT.Sqrt,
                                             bias=eps[:, 0:1]).then_inc(std_done, 1)
                    act.wait_ge(mlp_loaded, (l + 1) * MLP_LOADS)
                    with act.Fori(0, SEQS) as i:
                        act.wait_ge(normed, l * SEQS + (i + 1))
                        x = xf[:, bass.ds(i * CH, CH)]
                        nc.scalar.activation(x, x, ACT.Identity, bias=lnb[:, 0:1], scale=lng[:, 0:1]).then_inc(xn_ready, 1)
                    with act.Fori(0, SEQS // 2) as i2:
                        for par in range(2):
                            ch = l * SEQS + (i2 * 2 + par)
                            for j in range(HT):
                                act.wait_ge(hid_done, ch * MLPU + (2 * j + 1))
                                if j == 0:
                                    act.wait_ge(mlp_done, ch - par)
                                nc.scalar.activation(hb[0:HW[j], par, j, :], ps[0:HW[j], 2 * j * CH:(2 * j + 1) * CH],
                                                     ACT.Gelu, bias=b1[0:HW[j], HT + j:HT + j + 1]).then_inc(gelu_done, 1)


def mlp_stage(nc, ps, sem, w, xn, xr, xcat, ones4, eps):
    with ExitStack() as c:
        def sb(name, shape, dt=FP32):
            return c.enter_context(nc.sbuf_tensor(f"ml_{name}", shape, dt))

        wf = sb("wf", [128, MLP])
        wp = sb("wp", [128, MT, 128])
        neg = sb("neg", [128, MLP])
        lnw = sb("lnw", [128, MT])
        lnb = sb("lnb", [128, MT])
        asum = sb("asum", [128, 2])
        ga = sb("ga", [128, 4])
        hid = sb("hid", [128, MT, TOK])
        sq = sb("sq", [128, 2, MT, CH])
        sd = sb("sd", [128, 2, CH])
        loaded = sem("ml_loaded")
        prep = sem("ml_prep")
        asum_done = sem("ml_asum_done")
        gamma_done = sem("ml_gamma_done")
        w_ready = sem("ml_w_ready")
        hid_done = sem("ml_hid_done")
        gelu_done = sem("ml_gelu_done")
        mean_done = sem("ml_mean_done")
        centered = sem("ml_centered")
        squared = sem("ml_squared")
        var_done = sem("ml_var_done")
        std_done = sem("ml_std_done")
        rstd_done = sem("ml_rstd_done")
        normed = sem("ml_normed")
        affine_done = sem("ml_affine_done")
        out_done = sem("ml_out_done")
        out_read = sem("ml_out_read")
        stored = sem("ml_stored")
        act_passed = sem("ml_act_passed")

        def bank(k):
            return ps[:, k * CH:(k + 1) * CH]

        with nc.Block() as block:

            @block.sync
            def _(sp):
                sp.dma_start(wf[:, :], w["ml_wf"]).then_inc(loaded, 16)
                sp.dma_start(wp[:, :, :], w["ml_wp"]).then_inc(loaded, 16)
                sp.dma_start(lnw[:, :], w["ml_lnw"]).then_inc(loaded, 16)
                sp.dma_start(lnb[:, :], w["ml_lnb"]).then_inc(loaded, 16)
                with sp.Fori(0, SEQS) as i:
                    sp.wait_ge(out_read, i + 1)
                    sp.dma_start(xcat[:, bass.ds(i * CH, CH)], xr(i)).then_inc(stored, 16)
                sp.wait_ge(stored, 16 * SEQS)

            @block.tensor
            def _(pe):
                pe.wait_ge(asum_done, 1)
                nc.tensor.matmul(bank(0)[:, 0:2], ones4[:, :], asum[:, :], start=True, stop=True).then_inc(gamma_done, 1)
                pe.wait_ge(w_ready, 1)
                with pe.Fori(0, SEQS) as i:
                    for j in range(MT):
                        pe.wait_ge(gelu_done, i * MT)
                        nc.tensor.matmul(bank(j), wf[:, j * 128:(j + 1) * 128], xn(i),
                                         start=True, stop=True).then_inc(hid_done, 1)
                with pe.Fori(0, SEQS // 2) as i2:
                    for par in range(2):
                        i = i2 * 2 + par
                        pe.wait_ge(gelu_done, SEQS * MT)
                        pe.wait_ge(centered, i * MT)
                        for j in range(MT):
                            last = nc.tensor.matmul(bank(par), ones4[:, :], hid[:, j, bass.ds(i * CH, CH)],
                                                    start=(j == 0), stop=(j == MT - 1))
                        last.then_inc(mean_done, 1)
                        pe.wait_ge(std_done, i)
                        for j in range(MT):
                            pe.wait_ge(squared, i * MT + (j + 1))
                            last = nc.tensor.matmul(bank(2 + par), ones4[:, :], sq[:, par, j, :],
                                                    start=(j == 0), stop=(j == MT - 1))
                        last.then_inc(var_done, 1)
                        pe.wait_ge(out_read, i)
                        for j in range(MT):
                            pe.wait_ge(affine_done, i * MT + (j + 1))
                            last = nc.tensor.matmul(bank(4 + par), wp[:, j, :], hid[:, j, bass.ds(i * CH, CH)],
                                                    start=(j == 0), stop=(j == MT - 1))
                        last.then_inc(out_done, 1)

            @block.vector
            def _(dve):
                steps = [0]

                def link(ins):
                    steps[0] += 1
                    ins.then_inc(prep, 1)
                    dve.wait_ge(prep, steps[0])

                dve.wait_ge(loaded, 64)
                link(nc.vector.tensor_reduce(asum[:, 0:1], wf[:, :], AX.X, ALU.add, apply_absolute_value=True))
                nc.vector.tensor_reduce(asum[:, 1:2], wp[:, :, :], AX.XY, ALU.add,
                                        apply_absolute_value=True).then_inc(asum_done, 1)
                dve.wait_ge(gamma_done, 1)
                link(nc.vector.tensor_scalar(ga[:, 0:2], bank(0)[:, 0:2], 1.0 / 128, 1e-6, ALU.mult, ALU.add))
                link(nc.vector.tensor_scalar(ga[:, 0:2], ga[:, 0:2], 0.5, None, ALU.mult))
                link(nc.vector.tensor_scalar(ga[:, 2:4], ga[:, 0:2], -1.0, None, ALU.mult))
                for k, m in ((0, wf[:, :]), (1, wp[:, :, :].rearrange("p a b -> p (a b)"))):
                    link(nc.vector.tensor_scalar(neg[:, :], m, ga[:, 2 + k:3 + k], None, ALU.is_lt))
                    link(nc.vector.tensor_scalar(m, m, ga[:, k:k + 1], None, ALU.is_gt))
                    link(nc.vector.tensor_tensor(m, m, neg[:, :], ALU.subtract))
                nc.vector.tensor_copy(ga[:, 0:1], ga[:, 1:2]).then_inc(w_ready, 1)
                with dve.Fori(0, SEQS // 2) as i2:
                    for par in range(2):
                        i = i2 * 2 + par
                        dve.wait_ge(mean_done, i + 1)
                        for j in range(MT):
                            h = hid[:, j, bass.ds(i * CH, CH)]
                            nc.vector.tensor_tensor(h, h, bank(par), ALU.subtract).then_inc(centered, 1)
                        dve.wait_ge(std_done, i + 1)
                        nc.vector.reciprocal(sd[:, par, :], sd[:, par, :]).then_inc(rstd_done, 1)
                        dve.wait_ge(rstd_done, i + 1)
                        for j in range(MT):
                            h = hid[:, j, bass.ds(i * CH, CH)]
                            nc.vector.scalar_tensor_tensor(h, h, lnw[:, j:j + 1], sd[:, par, :], ALU.mult,
                                                           ALU.mult).then_inc(normed, 1)
                        dve.wait_ge(out_done, i + 1)
                        nc.vector.tensor_tensor(xr(i), xr(i), bank(4 + par), ALU.add).then_inc(out_read, 1)

            @block.scalar
            def _(act):
                with act.Fori(0, SEQS) as i:
                    for j in range(MT):
                        act.wait_ge(hid_done, i * MT + (j + 1))
                        nc.scalar.activation(hid[:, j, bass.ds(i * CH, CH)], bank(j), ACT.Gelu).then_inc(gelu_done, 1)
                with act.Fori(0, SEQS // 2) as i2:
                    for par in range(2):
                        i = i2 * 2 + par
                        for j in range(MT):
                            act.wait_ge(centered, i * MT + (j + 1))
                            nc.scalar.activation(sq[:, par, j, :], hid[:, j, bass.ds(i * CH, CH)],
                                                 ACT.Square).then_inc(squared, 1)
                        act.wait_ge(var_done, i + 1)
                        nc.scalar.activation(sd[:, par, :], bank(2 + par), ACT.Sqrt, bias=eps[:, 0:1]).then_inc(std_done, 1)
                        for j in range(MT):
                            act.wait_ge(normed, i * MT + (j + 1))
                            stand_alone(act, act_passed)
                            h = hid[:, j, bass.ds(i * CH, CH)]
                            nc.scalar.activation(h, h, ACT.Identity, bias=lnb[:, j:j + 1]).then_inc(affine_done, 1)


def program(nc, w, out):
    ctx = ExitStack()
    with ctx:
        def sem(name):
            return ctx.enter_context(nc.semaphore(name))

        def sb(name, shape, dt=FP32):
            return ctx.enter_context(nc.sbuf_tensor(name, shape, dt))

        xr = sb("xr", [128, TOK])
        xa = sb("xa", [128, XCOLS])
        xb = sb("xb", [128, XCOLS])
        ones = sb("ones", [128, 128])
        ones4 = sb("ones4", [128, 128])
        eps = sb("eps", [128, 1])
        ident = sb("ident", [128, 128])
        ps = ctx.enter_context(nc.psum_tensor("ps", [128, 8 * CH], FP32))
        x_loaded = sem("x_loaded")

        def plain(i):
            return xr[:, bass.ds(i * L, L)]

        def padded(buf):
            return lambda i: buf[:, bass.ds(i * SEQP + (PAD + 1), L)]

        with nc.Block() as block:

            @block.sync
            def _(sp):
                sp.dma_start(xr[:, :], w["x"]).then_inc(x_loaded, 16)
                sp.dma_start(ident[:, :], w["c_ident"]).then_inc(x_loaded, 16)
                sp.wait_ge(x_loaded, 32)

            @block.vector
            def _(dve):
                nc.vector.memset(xa[:, :], 0.0)
                nc.vector.memset(ones[:, :], 1.0 / D)
                nc.vector.memset(ones4[:, :], 1.0 / MLP)
                nc.vector.memset(eps[:, :], LN_EPS)

            @block.gpsimd
            def _(pool):
                nc.gpsimd.memset(xb[:, :], 0.0)

        layernorm_stage(nc, ps, sem, "a", plain, padded(xa), ones, eps)
        retention_stage(nc, ps, sem, w, padded(xa), plain, eps)
        transformer_stage(nc, ps, sem, w, xa, xb, ones, eps, ident)
        layernorm_stage(nc, ps, sem, "b", plain, padded(xb), ones, eps, src2=padded(xa))
        softmax_stage(nc, ps, sem, w, padded(xb), plain, ident)
        mlp_stage(nc, ps, sem, w, padded(xb), plain, out, ones4, eps)


def constants():
    f = np.float32
    t = {}
    c = np.arange(L)[None, :] - np.arange(128)[:, None]
    t["c_lag"] = np.maximum(c, 0).astype(f)
    t["c_ident"] = np.eye(128, dtype=f)
    bf = mybir.dt.np(BF16)
    t["c_identb"] = np.eye(128).astype(bf)
    i, j = (np.arange(128) % WIN)[:, None], np.arange(2 * WIN)[None, :]
    seen = (j >= i) & (j <= i + WIN)
    first = seen & ((j >= WIN) | (np.arange(128) >= WIN)[:, None])
    m = np.stack([np.where(first, 0.0, -1e30), np.where(seen, 0.0, -1e30)], 1)
    t["c_mask"] = np.ascontiguousarray(np.tile(m, (1, 1, PAIRS))).astype(bf)
    half = np.arange(0, DH, 2, dtype=f)
    inv = (f(1.0) / f(10000.0) ** (half / f(DH))).astype(f)
    pos = np.arange(L, dtype=f)
    fr = pos[:, None] * inv[None, :]
    fr = np.concatenate([fr, fr], -1)
    bs = (half + f(0.4 * DH)) / f(1.4 * DH)
    power = (pos - L // 2) / f(WIN // 2)
    sc = bs[None, :] ** power[:, None]
    sc = np.concatenate([sc, sc], -1).astype(f)
    sgn = np.where(np.arange(DH) < DH // 2, -1, 1).astype(f)
    tb = np.stack([np.cos(fr) * sc, np.sin(fr) * sc * sgn, np.cos(fr) / sc, np.sin(fr) / sc * sgn])
    t["c_xpos"] = np.ascontiguousarray(tb.reshape(4, TPS, 128, DH).transpose(2, 0, 1, 3).astype(f))
    hh = DK // 2
    inv = (f(1.0) / f(10000.0) ** (np.arange(hh, dtype=f) / f(hh))).astype(f)
    ang = pos[:, None] * inv[None, :]
    rt = np.zeros((SLOT, 4, L), f)
    for k, s in ((0, f(DK ** -0.5)), (2, f(1.0))):
        for r in range(0, MROW, DK):
            rt[r:r + hh, k], rt[r + hh:r + DK, k] = np.cos(ang).T * s, np.cos(ang).T * s
            rt[r:r + hh, k + 1], rt[r + hh:r + DK, k + 1] = -np.sin(ang).T * s, np.sin(ang).T * s
    rt[MROW, 2] = 1.0
    t["c_rope"] = np.ascontiguousarray(np.tile(rt, (4, 1, 1)))
    sp = np.tile(np.array([1, 0], f), (SLOT, 2, 1))
    sp[DK:2 * DK, 0] = sp[2 * DK:3 * DK, 1] = (-1, 1)
    t["c_split"] = np.tile(sp, (4, 1, 1))
    b = np.zeros((SLOT, SLOT), f)
    b[DK, :] = 1.0
    t["c_bsel"] = np.kron(np.eye(4, dtype=f), b)
    return t


def slots(m, times=1):
    p = np.zeros((m.shape[0], HEADS, SLOT), m.dtype)
    p[:, :, :times * DK] = np.tile(m.reshape(m.shape[0], HEADS, DK), (1, 1, times))
    return p.reshape(m.shape[0], HEADS * SLOT)


def slot_rows(m):
    return np.ascontiguousarray(slots(np.ascontiguousarray(m.T)).T.reshape(QUADS, 128, -1).transpose(1, 0, 2))


def layout(inp):
    f = {k: np.asarray(v) for k, v in inp.items()}
    w = constants()
    w["x"] = np.ascontiguousarray(f["L0_attn_x"].reshape(TOK, D).T)
    qkv = f["L0_attn_W_qkv"]
    w["ret_wq"] = slots(qkv[0:D].T, SPLIT)
    w["ret_wk"] = np.ascontiguousarray(qkv[D:2 * D].T)
    w["ret_wv"] = slots(qkv[2 * D:3 * D].T)
    w["ret_wo"] = slot_rows(f["L0_attn_W_o"].T)
    w["log_gamma"] = f["L0_attn_log_gamma"]
    w["tr_wqkv"] = f["L0_ffn_Wqkv"].reshape(DEPTH * D, 3 * INNER)
    w["tr_wo"] = np.ascontiguousarray(f["L0_ffn_Wo"].reshape(DEPTH, PAIRS, 128, D).transpose(0, 2, 1, 3)
                                      ).reshape(DEPTH * 128, PAIRS * D)
    w["tr_w1"] = f["L0_ffn_W1"].reshape(DEPTH * D, 2 * HID)
    w2 = np.zeros((DEPTH, HT * 128, D), np.float32)
    w2[:, :HID] = f["L0_ffn_W2"]
    w["tr_w2"] = np.ascontiguousarray(w2.reshape(DEPTH, HT, 128, D).transpose(0, 2, 1, 3)).reshape(DEPTH * 128, HT * D)
    b1 = np.zeros((DEPTH, 2, HT * 128), np.float32)
    b1[:, :, :HID] = f["L0_ffn_b1"].reshape(DEPTH, 2, HID)
    w["tr_b1"] = np.ascontiguousarray(b1.reshape(DEPTH, 2 * HT, 128).transpose(0, 2, 1)).reshape(DEPTH * 128, 2 * HT)
    for name, key in (("tr_b2", "L0_ffn_b2"), ("tr_lng", "L0_ffn_ln_g"), ("tr_lnb", "L0_ffn_ln_b")):
        w[name] = f[key].reshape(DEPTH * 128, 1)
    s = np.concatenate([f["L0_ffn_q_scale"], f["L0_ffn_k_scale"]], 1)
    w["tr_qks"] = np.ascontiguousarray(np.repeat(s, 128, 0))
    def swap(m):
        return np.ascontiguousarray(m.reshape(-1, HEADS, 2, DK // 2)[:, :, ::-1]).reshape(m.shape)
    ws, bs = [], []
    for n in "qk":
        for fn in (lambda m: m, swap):
            ws.append(slots(fn(f[f"L1_attn_w{n}_w"]), SPLIT))
            bs.append(slots(fn(f[f"L1_attn_w{n}_b"][None]), SPLIT))
    w["sm_wp"] = np.ascontiguousarray(np.stack(ws, 1))
    bs[2].reshape(HEADS, SLOT)[:, MROW] = 1.0
    w["sm_bp"] = np.ascontiguousarray(np.stack(bs).reshape(4, QUADS, 128).transpose(2, 0, 1))
    w["sm_wv"] = slots(f["L1_attn_wv_w"])
    bv = slots(f["L1_attn_wv_b"][None])
    bv.reshape(HEADS, SLOT)[:, DK] = 1.0
    w["sm_bv"] = bv.reshape(-1)
    w["sm_wo"] = slot_rows(f["L1_attn_wo_w"])
    w["sm_bo"] = f["L1_attn_wo_b"].reshape(128, 1)
    w["ml_wf"] = np.ascontiguousarray(f["L1_ffn_W_fc"].T)
    w["ml_wp"] = np.ascontiguousarray(f["L1_ffn_W_proj"].T.reshape(MT, 128, D).transpose(1, 0, 2))
    w["ml_lnw"] = np.ascontiguousarray(f["L1_ffn_ln_w"].reshape(MT, 128).T)
    w["ml_lnb"] = np.ascontiguousarray(f["L1_ffn_ln_b"].reshape(MT, 128).T)
    return w


def kernel(**inputs):
    import concourse.bacc as bacc
    from concourse.bass_utils import run_bass_kernel_spmd

    nc = bacc.Bacc("TRN2", target_bir_lowering=False, num_devices=1)
    arrays, aps = {}, {}
    for name, a in layout(inputs).items():
        a = np.ascontiguousarray(a)
        arrays[f"in_{name}"] = a
        aps[name] = nc.dram_tensor(f"in_{name}", a.shape, mybir.dt.from_np(a.dtype), kind="ExternalInput").ap()
    out = nc.dram_tensor("out_x", (128, TOK), FP32, kind="ExternalOutput").ap()
    program(nc, aps, out)
    r = run_bass_kernel_spmd(nc, [arrays], core_ids=[0])
    return np.ascontiguousarray(r.results[0]["out_x"].T).reshape(SEQS, L, D)
```

```python
import concourse.bass as bass
from concourse import mybir
from contextlib import ExitStack
import numpy as np

FP32 = mybir.dt.float32
BF16 = mybir.dt.bfloat16
F32R = mybir.dt.float32r
ALU = mybir.AluOpType
ACT = mybir.ActivationFunctionType
AX = mybir.AxisListType

D = 128
SEQS = 8
L = 512
TOK = SEQS * L
CH = 512
TILE = 128
TPS = L // TILE
HEADS = 16
DK = D // HEADS
SLOT = 32
SPLIT = 3
MROW = SPLIT * DK
QUADS = HEADS * SLOT // 128
LN_EPS = 1e-5
FIRST = 1

DEPTH = 6
DH = 64
INNER = HEADS * DH
PAIRS = HEADS // 2
WIN = 32
WPT = TILE // WIN
HID = 341
HT = 3
HW = [128, 128, HID - 256]
PAD = 64
SEQP = L + 1
XCOLS = PAD + (SEQS + 1) * SEQP
MLP = 512
MT = MLP // 128


def col(b, t=0):
    return b * SEQP + (PAD + 1 + t)


def stand_alone(engine, passed):
    engine.sem_inc(passed, 1)


def layernorm_stage(nc, ps, sem, tag, src, dst, ones, eps, src2=None):
    with ExitStack() as c:
        sq = c.enter_context(nc.sbuf_tensor(f"sq_{tag}", [128, TOK], FP32))
        sd = c.enter_context(nc.sbuf_tensor(f"sd_{tag}", [128, TOK], FP32))
        summed = sem(f"summed_{tag}")
        mean_done = sem(f"mean_done_{tag}")
        centered = sem(f"centered_{tag}")
        squared = sem(f"squared_{tag}")
        var_done = sem(f"var_done_{tag}")
        std_done = sem(f"std_done_{tag}")
        rstd_done = sem(f"rstd_done_{tag}")
        with nc.Block() as block:

            @block.tensor
            def _(pe):
                with pe.Fori(0, SEQS) as i:
                    if src2 is not None:
                        pe.wait_ge(summed, i + 1)
                    nc.tensor.matmul(ps[:, bass.ds(i * CH, CH)], ones[:, :], src(i),
                                     start=True, stop=True).then_inc(mean_done, 1)
                with pe.Fori(0, SEQS) as i:
                    pe.wait_ge(squared, i + 1)
                    nc.tensor.matmul(ps[:, bass.ds(i * CH, CH)], ones[:, :], sq[:, bass.ds(i * CH, CH)],
                                     start=True, stop=True).then_inc(var_done, 1)

            @block.vector
            def _(dve):
                if src2 is not None:
                    with dve.Fori(0, SEQS) as i:
                        nc.vector.tensor_tensor(src(i), src(i), src2(i), ALU.add).then_inc(summed, 1)
                with dve.Fori(0, SEQS) as i:
                    dve.wait_ge(mean_done, i + 1)
                    nc.vector.tensor_tensor(dst(i), src(i), ps[:, bass.ds(i * CH, CH)],
                                            ALU.subtract).then_inc(centered, 1)
                with dve.Fori(0, SEQS) as i:
                    dve.wait_ge(std_done, i + 1)
                    nc.vector.reciprocal(sd[:, bass.ds(i * CH, CH)],
                                         sd[:, bass.ds(i * CH, CH)]).then_inc(rstd_done, 1)
                with dve.Fori(0, SEQS) as i:
                    dve.wait_ge(rstd_done, i + 1)
                    nc.vector.tensor_tensor(dst(i), dst(i), sd[:, bass.ds(i * CH, CH)], ALU.mult)

            @block.scalar
            def _(act):
                with act.Fori(0, SEQS) as i:
                    act.wait_ge(centered, i + 1)
                    nc.scalar.activation(sq[:, bass.ds(i * CH, CH)], dst(i), ACT.Square).then_inc(squared, 1)
                with act.Fori(0, SEQS) as i:
                    act.wait_ge(var_done, i + 1)
                    nc.scalar.activation(sd[:, bass.ds(i * CH, CH)], ps[:, bass.ds(i * CH, CH)], ACT.Sqrt,
                                         bias=eps[:, 0:1]).then_inc(std_done, 1)



def retention_stage(nc, ps, sem, w, xn, xr, eps):
    with ExitStack() as c:
        def sb(name, shape, dt=FP32):
            return c.enter_context(nc.sbuf_tensor(f"ret_{name}", shape, dt))

        wq = sb("wq", [128, 512])
        wk = sb("wk", [128, 512])
        wkc = sb("wkc", [128, 128])
        wv = sb("wv", [128, 512])
        wo = sb("wo", [128, QUADS, 128])
        small = sb("small", [128, HEADS])
        gam = sb("gam", [128, HEADS])
        lag = sb("lag", [128, L])
        decay = sb("decay", [128, HEADS, L])
        xcur = sb("xcur", [128, L])
        qt = sb("qt", [128, QUADS, L], F32R)
        kt = sb("kt", [128, QUADS, L], F32R)
        rest = sb("rest", [128, 2 * QUADS, L])
        split = sb("split", [128, 2, 2])
        vp = sb("vp", [128, TPS, 512])
        ksq = sb("ksq", [128, TPS, 128])
        krs = sb("krs", [128, TPS, HEADS])
        at = sb("at", [128, 2, TPS, L])
        yt = sb("yt", [128, QUADS, L])
        loaded = sem("ret_loaded")
        prep = sem("ret_prep")
        w_ready = sem("ret_w_ready")
        neg_ready = sem("ret_neg_ready")
        exp_ready = sem("ret_exp_ready")
        gamma_ready = sem("ret_gamma_ready")
        ln_ready = sem("ret_ln_ready")
        power_ready = sem("ret_power_ready")
        decay_ready = sem("ret_decay_ready")
        x_ready = sem("ret_x_ready")
        proj_done = sem("ret_proj_done")
        qk_read = sem("ret_qk_read")
        qk_ready = sem("ret_qk_ready")
        ksq_done = sem("ret_ksq_done")
        ksum_done = sem("ret_ksum_done")
        kstd_done = sem("ret_kstd_done")
        krs_done = sem("ret_krs_done")
        v_ready = sem("ret_v_ready")
        scores_done = sem("ret_scores_done")
        weights_done = sem("ret_weights_done")
        y_done = sem("ret_y_done")
        y_read = sem("ret_y_read")
        out_done = sem("ret_out_done")
        out_read = sem("ret_out_read")

        PQ = [ps[:, 0:CH], ps[:, CH:2 * CH]]
        PS = [ps[:, (2 + j) * CH:(3 + j) * CH] for j in range(TPS)]
        PY = ps[:, 6 * CH:7 * CH]
        PO = ps[:, 7 * CH:8 * CH]
        NQK = 2 * QUADS
        UNITS = NQK + 2 * TPS

        from_first = (ksq_done, out_read, v_ready, weights_done, y_read)

        with nc.Block() as block:

            @block.sync
            def _(sp):
                for counter in from_first:
                    sp.sem_inc(counter, FIRST)
                sp.dma_start(wq[:, :], w["ret_wq"]).then_inc(loaded, 16)
                sp.dma_start(wkc[:, :], w["ret_wk"]).then_inc(loaded, 16)
                sp.dma_start(wv[:, :], w["ret_wv"]).then_inc(loaded, 16)
                sp.dma_start(wo[:, :, :], w["ret_wo"]).then_inc(loaded, 16)
                sp.dma_start(gam[:, :], w["log_gamma"].partition_broadcast(128)).then_inc(loaded, 16)
                sp.dma_start(lag[:, :], w["c_lag"]).then_inc(loaded, 16)
                sp.dma_start(split[:, :, :], w["c_split"]).then_inc(loaded, 16)

            @block.gpsimd
            def _(pool):
                nc.gpsimd.tensor_copy(xcur[:, :], xn(0)).then_inc(x_ready, 1)
                pool.wait_ge(power_ready, 1)
                nc.gpsimd.affine_select(out=decay[:, :, :], in_=decay[:, :, :], compare_op=ALU.is_ge, fill=0.0,
                                        base=0, pattern=[[0, HEADS], [1, L]],
                                        channel_multiplier=-1).then_inc(decay_ready, 1)
                with pool.Fori(1, SEQS) as b:
                    pool.wait_ge(proj_done, b * UNITS)
                    nc.gpsimd.tensor_copy(xcur[:, :], xn(b)).then_inc(x_ready, 1)

            @block.tensor
            def _(pe):
                def score(b, h):
                    g, r = h // 4, SLOT * (h % 4)
                    for j in range(TPS):
                        pe.wait_ge(weights_done, ((b * HEADS + h) * TPS + (0 if h == 0 else j + 1 - TPS)) + FIRST)
                        t0 = min(j * TILE, L - 2 * TILE)
                        nc.tensor.matmul(PS[j][:, 0:L - t0], kt[r:r + SLOT, g, j * TILE:(j + 1) * TILE],
                                         qt[r:r + SLOT, g, t0:L], start=True, stop=True).then_inc(scores_done, 1)

                def weigh(b, h):
                    g, r = h // 4, SLOT * (h % 4)
                    if h % 4 == 0:
                        pe.wait_ge(y_read, b * QUADS + g + FIRST)
                    for j in range(TPS):
                        pe.wait_ge(weights_done, (b * HEADS + h) * TPS + (j + 1) + FIRST)
                        last = nc.tensor.matmul(PY[r:r + SLOT, j * TILE:L], vp[:, j, h * SLOT:(h + 1) * SLOT],
                                                at[:, h % 2, j, 0:L - j * TILE],
                                                start=(j == 0), stop=(j == TPS - 1))
                    last.then_inc(y_done, 1)

                pe.wait_ge(w_ready, SPLIT)
                with pe.Fori(0, SEQS) as b:
                    pe.wait_ge(x_ready, b + 1)
                    for u in range(UNITS):
                        if u == 0:
                            pe.wait_ge(ksq_done, b * TPS + FIRST)
                        elif u == 1:
                            pe.wait_ge(v_ready, b * TPS + FIRST)
                        elif u < NQK + 2:
                            pe.wait_ge(qk_read, b * NQK + (u - 1))
                        else:
                            pe.wait_ge((ksq_done, v_ready)[u % 2], b * TPS + (u - NQK) // 2 + FIRST)
                        if u < NQK:
                            g = u // 2
                            nc.tensor.matmul(PQ[u % 2], (wq, wk)[u % 2][:, g * 128:(g + 1) * 128], xcur[:, :],
                                             start=True, stop=True).then_inc(proj_done, 1)
                        else:
                            t = (u - NQK) // 2
                            rhs, n = ((wkc, 128), (wv, 512))[u % 2]
                            nc.tensor.matmul(PQ[u % 2][:, 0:n], xcur[:, t * TILE:(t + 1) * TILE], rhs[:, :],
                                             start=True, stop=True).then_inc(proj_done, 1)
                    pe.wait_ge(v_ready, b * TPS + TPS + FIRST)
                    pe.wait_ge(qk_ready, b * NQK + NQK)
                    score(b, 0)
                    for h in range(1, HEADS):
                        score(b, h)
                        weigh(b, h - 1)
                    weigh(b, HEADS - 1)
                    pe.wait_ge(y_read, b * QUADS + QUADS + FIRST)
                    pe.wait_ge(out_read, b + FIRST)
                    for g in range(QUADS):
                        last = nc.tensor.matmul(PO, wo[:, g, :], yt[:, g, :],
                                                start=(g == 0), stop=(g == QUADS - 1))
                    last.then_inc(out_done, 1)

            @block.vector
            def _(dve):
                steps = [0]

                def link(ins):
                    steps[0] += 1
                    ins.then_inc(prep, 1)
                    dve.wait_ge(prep, steps[0])

                dve.wait_ge(loaded, 112)
                wk3 = wkc[:, :].rearrange("p (h d) -> p h d", d=DK)
                link(nc.vector.tensor_reduce(small[:, :], wk3, AX.X, ALU.add))
                link(nc.vector.tensor_scalar(small[:, :], small[:, :], 1.0 / DK, None, ALU.mult))
                link(nc.vector.memset(wk[:, :], 0.0))
                link(nc.vector.tensor_tensor(wk3, wk3, small[:, :].unsqueeze(2).broadcast_to([128, HEADS, DK]),
                                             ALU.subtract))
                for i in range(SPLIT):
                    nc.vector.tensor_copy(wk[:, :].rearrange("p (h s) -> p h s", s=SLOT)[:, :, i * DK:(i + 1) * DK],
                                          wk3).then_inc(w_ready, 1)
                link(nc.vector.tensor_scalar(gam[:, :], gam[:, :], -1.0, 80.0, ALU.mult, ALU.min))
                nc.vector.tensor_scalar(gam[:, :], gam[:, :], -80.0, None, ALU.max).then_inc(neg_ready, 1)
                dve.wait_ge(exp_ready, 1)
                link(nc.vector.tensor_scalar(gam[:, :], gam[:, :], 1.0, None, ALU.add))
                link(nc.vector.reciprocal(gam[:, :], gam[:, :]))
                nc.vector.tensor_scalar(gam[:, :], gam[:, :], 2.0 ** -64, None, ALU.max).then_inc(gamma_ready, 1)
                with dve.Fori(0, SEQS) as b:
                    for u in range(UNITS):
                        t = (u - NQK) // 2
                        if u < NQK:
                            dve.wait_ge(qk_read, b * NQK + (u + 1))
                            o = (qt, kt)[u % 2][:, u // 2, :]
                            nc.vector.scalar_tensor_tensor(o, o.bitcast(FP32), split[:, u % 2, 0:1], rest[:, u, :],
                                                           ALU.mult, ALU.add).then_inc(qk_ready, 1)
                        elif u % 2 == 0:
                            dve.wait_ge(ksq_done, b * TPS + (t + 1) + FIRST)
                            nc.vector.tensor_reduce(krs[:, t, :], ksq[:, t, :].rearrange("p (h d) -> p h d", d=DK),
                                                    AX.X, ALU.add).then_inc(ksum_done, 1)
                        else:
                            dve.wait_ge(proj_done, b * UNITS + (u + 1))
                            dve.wait_ge(kstd_done, b * TPS + (t + 1))
                            nc.vector.reciprocal(krs[:, t, :], krs[:, t, :]).then_inc(krs_done, 1)
                            dve.wait_ge(krs_done, b * TPS + (t + 1))
                            nc.vector.tensor_tensor(vp[:, t, :].rearrange("p (h s) -> p h s", s=SLOT),
                                                    PQ[1].rearrange("p (h s) -> p h s", s=SLOT),
                                                    krs[:, t, :].unsqueeze(2).broadcast_to([128, HEADS, SLOT]),
                                                    ALU.mult).then_inc(v_ready, 1)
                    dve.wait_ge(decay_ready, 1)
                    for h in range(HEADS):
                        for j in range(TPS):
                            dve.wait_ge(scores_done, (b * HEADS + h) * TPS + (j + 1))
                            if j == 0 and h >= 2:
                                dve.wait_ge(y_done, b * HEADS + (h - 1))
                            n = L - j * TILE
                            o = j * TILE - min(j * TILE, L - 2 * TILE)
                            nc.vector.tensor_tensor(at[:, h % 2, j, 0:n], PS[j][:, o:o + n], decay[:, h, 0:n],
                                                    ALU.mult).then_inc(weights_done, 1)
                    dve.wait_ge(out_done, b + 1)
                    nc.vector.tensor_tensor(xr(b), xr(b), PO, ALU.add).then_inc(out_read, 1)

            @block.scalar
            def _(act):
                act.wait_ge(neg_ready, 1)
                nc.scalar.activation(gam[:, :], gam[:, :], ACT.Exp).then_inc(exp_ready, 1)
                act.wait_ge(gamma_ready, 1)
                nc.scalar.activation(small[:, :], gam[:, :], ACT.Ln).then_inc(ln_ready, 1)
                act.wait_ge(ln_ready, 1)
                for h in range(HEADS):
                    last = nc.scalar.activation(decay[:, h, :], lag[:, :], ACT.Exp, scale=small[:, h:h + 1])
                last.then_inc(power_ready, 1)
                with act.Fori(0, SEQS) as b:
                    for u in range(NQK):
                        act.wait_ge(proj_done, b * UNITS + (u + 1))
                        nc.scalar.activation((qt, kt)[u % 2][:, u // 2, :], PQ[u % 2], ACT.Copy)
                        nc.scalar.activation(rest[:, u, :], PQ[u % 2], ACT.Copy,
                                             scale=split[:, u % 2, 1:2]).then_inc(qk_read, 1)
                    for t in range(TPS):
                        act.wait_ge(proj_done, b * UNITS + (NQK + 2 * t + 1))
                        nc.scalar.activation(ksq[:, t, :], PQ[0][:, 0:128], ACT.Square).then_inc(ksq_done, 1)
                        act.wait_ge(ksum_done, b * TPS + (t + 1))
                        nc.scalar.activation(krs[:, t, :], krs[:, t, :], ACT.Sqrt, scale=1.0 / DK,
                                             bias=eps[:, 0:1]).then_inc(kstd_done, 1)
                    for g in range(QUADS):
                        act.wait_ge(y_done, b * HEADS + 4 * (g + 1))
                        nc.scalar.activation(yt[:, g, :], PY, ACT.Copy).then_inc(y_read, 1)


def softmax_stage(nc, ps, sem, w, xn, xr, ident):
    with ExitStack() as c:
        def sb(name, shape, dt=FP32):
            return c.enter_context(nc.sbuf_tensor(f"sm_{name}", shape, dt))

        NP = 4 * QUADS
        wp = sb("wp", [128, 4, 512])
        bp = sb("bp", [128, 4, QUADS])
        wv = sb("wv", [128, 512])
        bv = sb("bv", [128, 512])
        wo = sb("wo", [128, QUADS, 128])
        bo = sb("bo", [128, 1])
        rope = sb("rope", [128, 4, L])
        bsel = sb("bsel", [128, 128])
        xcur = sb("xcur", [128, L])
        raw = sb("raw", [128, 2 * QUADS, L])
        part = sb("part", [128, 2 * QUADS, L])
        qk = sb("qk", [128, 2 * QUADS, L], F32R)
        split = sb("split", [128, 2, 2])
        vp = sb("vp", [128, TPS, 512])
        nmax = sb("nmax", [128, QUADS, TPS, 128])
        pt = sb("pt", [128, 2, TPS, L])
        yt = sb("yt", [128, QUADS, L])
        rden = sb("rden", [128, QUADS, L])
        loaded = sem("sm_loaded")
        nmax_zero = sem("sm_nmax_zero")
        pool_passed = sem("sm_pool_passed")
        x_ready = sem("sm_x_ready")
        proj_done = sem("sm_proj_done")
        proj_read = sem("sm_proj_read")
        rot_ready = sem("sm_rot_ready")
        hi_ready = sem("sm_hi_ready")
        qk_ready = sem("sm_qk_ready")
        scores_done = sem("sm_scores_done")
        max_done = sem("sm_max_done")
        maxt_done = sem("sm_maxt_done")
        q_ready = sem("sm_q_ready")
        keyed_done = sem("sm_keyed_done")
        exp_done = sem("sm_exp_done")
        y_done = sem("sm_y_done")
        y_read = sem("sm_y_read")
        den_done = sem("sm_den_done")
        rden_done = sem("sm_rden_done")
        norm_done = sem("sm_norm_done")
        out_done = sem("sm_out_done")
        out_read = sem("sm_out_read")

        PQ = [ps[:, 0:CH], ps[:, CH:2 * CH]]
        PS = [ps[:, (2 + j) * CH:(3 + j) * CH] for j in range(TPS)]
        PY = ps[:, 6 * CH:7 * CH]
        PO = ps[:, 7 * CH:8 * CH]
        UNITS = NP + TPS

        from_first = (out_read, proj_read, rden_done, y_read)

        with nc.Block() as block:

            @block.sync
            def _(sp):
                for counter in from_first:
                    sp.sem_inc(counter, FIRST)
                for dst, name in ((wp[:, :, :], "sm_wp"), (bp[:, :, :], "sm_bp"), (wv[:, :], "sm_wv"),
                                  (wo[:, :, :], "sm_wo"), (bo[:, :], "sm_bo"), (rope[:, :, :], "c_rope"),
                                  (bsel[:, :], "c_bsel"), (split[:, :, :], "c_split")):
                    sp.dma_start(dst, w[name]).then_inc(loaded, 16)
                sp.dma_start(bv[:, :], w["sm_bv"].partition_broadcast(128)).then_inc(loaded, 16)

            @block.gpsimd
            def _(pool):
                nc.gpsimd.memset(nmax[:, :, :, :], 0.0).then_inc(nmax_zero, 1)
                nc.gpsimd.tensor_copy(xcur[:, :], xn(0)).then_inc(x_ready, 1)
                with pool.Fori(0, SEQS) as b:
                    for i in range(2 * QUADS):
                        pool.wait_ge(proj_read, b * UNITS + 2 * (i + 1) + FIRST)
                        nc.gpsimd.tensor_tensor(raw[:, i, :], raw[:, i, :], part[:, i, :],
                                                ALU.add).then_inc(rot_ready, 1)
                    pool.wait_ge(proj_done, b * UNITS + UNITS)
                    stand_alone(pool, pool_passed)
                    nc.gpsimd.tensor_copy(xcur[:, :], xn(b + 1)).then_inc(x_ready, 1)

            @block.tensor
            def _(pe):
                def maxima(b, g):
                    if g == 0:
                        pe.wait_ge(qk_ready, b * 2 * QUADS + 2 * QUADS)
                    elif g == 1:
                        pe.wait_ge(max_done, b * HEADS * TPS + 4 * TPS)
                    else:
                        pe.wait_ge(exp_done, b * HEADS * TPS + 4 * (g - 1) * TPS)
                    for i in range(TPS):
                        for r in range(4):
                            n = (g * TPS + i) * 4 + r
                            if i:
                                pe.wait_ge(max_done, b * HEADS * TPS + (n - 3))
                            nc.tensor.matmul(PS[r], qk[r * SLOT:(r + 1) * SLOT, g, i * TILE:(i + 1) * TILE],
                                             qk[r * SLOT:(r + 1) * SLOT, QUADS + g, :],
                                             start=True, stop=True).then_inc(scores_done, 1)

                def transposed_maxima(b, g):
                    pe.wait_ge(max_done, b * HEADS * TPS + (g + 1) * 4 * TPS)
                    if g == 0:
                        pe.wait_ge(out_read, b + FIRST)
                    else:
                        pe.wait_ge(q_ready, b * QUADS + g)
                    for i in range(TPS):
                        last = nc.tensor.transpose(PO[:, i * TILE:(i + 1) * TILE], nmax[:, g, i, :], ident[:, :])
                    last.then_inc(maxt_done, 1)

                def keyed(b, h):
                    g, r = h // 4, SLOT * (h % 4)
                    if r == 0:
                        pe.wait_ge(q_ready, b * QUADS + (g + 1))
                        if g + 1 < QUADS:
                            pe.wait_ge(max_done, b * HEADS * TPS + (g + 2) * 4 * TPS)
                        else:
                            pe.wait_ge(exp_done, (b * HEADS + h) * TPS)
                    for j in range(TPS):
                        if r:
                            pe.wait_ge(exp_done, (b * HEADS + h) * TPS + (j + 1 - TPS))
                        nc.tensor.matmul(PS[j], qk[r:r + SLOT, QUADS + g, j * TILE:(j + 1) * TILE],
                                         qk[r:r + SLOT, g, :], start=True, stop=True).then_inc(keyed_done, 1)

                def weigh(b, h):
                    g, r = h // 4, SLOT * (h % 4)
                    if r == 0:
                        pe.wait_ge(y_read, b * QUADS + g + FIRST)
                    for j in range(TPS):
                        pe.wait_ge(exp_done, (b * HEADS + h) * TPS + (j + 1))
                        last = nc.tensor.matmul(PY[r:r + SLOT, :], vp[:, j, h * SLOT:(h + 1) * SLOT],
                                                pt[:, h % 2, j, :], start=(j == 0), stop=(j == TPS - 1))
                    last.then_inc(y_done, 1)

                def denominators(b, g):
                    pe.wait_ge(y_read, b * QUADS + (g + 1) + FIRST)
                    if g >= 2:
                        pe.wait_ge(rden_done, b * QUADS + (g - 1) + FIRST)
                    nc.tensor.matmul(PQ[g % 2], bsel[:, :], yt[:, g, :], start=True, stop=True).then_inc(den_done, 1)

                pe.wait_ge(loaded, 144)
                pe.wait_ge(nmax_zero, 1)
                with pe.Fori(0, SEQS) as b:
                    pe.wait_ge(x_ready, b + 1)
                    for u in range(UNITS):
                        if u == 0:
                            pe.wait_ge(rden_done, b * QUADS + FIRST)
                        pe.wait_ge(proj_read, b * UNITS + max(u - 1, 0) + FIRST)
                        if u < NP:
                            g, kind = (u // 2) % QUADS, 2 * (u // (2 * QUADS)) + u % 2
                            nc.tensor.matmul(PQ[u % 2], wp[:, kind, g * 128:(g + 1) * 128], xcur[:, :],
                                             start=True, stop=True).then_inc(proj_done, 1)
                        else:
                            t = u - NP
                            nc.tensor.matmul(PQ[u % 2], xcur[:, t * TILE:(t + 1) * TILE], wv[:, :],
                                             start=True, stop=True).then_inc(proj_done, 1)
                    maxima(b, 0)
                    pe.wait_ge(proj_read, b * UNITS + UNITS + FIRST)
                    for h in range(HEADS):
                        if h % 4 == 0:
                            if h // 4 + 1 < QUADS:
                                maxima(b, h // 4 + 1)
                            transposed_maxima(b, h // 4)
                        keyed(b, h)
                        if h:
                            weigh(b, h - 1)
                        if h % 4 == 1 and h > 4:
                            denominators(b, h // 4 - 1)
                    weigh(b, HEADS - 1)
                    denominators(b, QUADS - 1)
                    for g in range(QUADS):
                        pe.wait_ge(norm_done, b * QUADS + (g + 1))
                        last = nc.tensor.matmul(PO, wo[:, g, :], yt[:, g, :], start=(g == 0), stop=(g == QUADS - 1))
                    last.then_inc(out_done, 1)

            @block.vector
            def _(dve):
                dve.wait_ge(loaded, 144)
                dve.wait_ge(nmax_zero, 1)
                with dve.Fori(0, SEQS) as b:
                    def unite(i):
                        dve.wait_ge(hi_ready, b * 2 * QUADS + (i + 1))
                        nc.vector.scalar_tensor_tensor(qk[:, i, :], qk[:, i, :].bitcast(FP32),
                                                       split[:, i // QUADS, 0:1], part[:, i, :], ALU.mult,
                                                       ALU.add).then_inc(qk_ready, 1)

                    for u in range(UNITS):
                        dve.wait_ge(proj_done, b * UNITS + (u + 1))
                        if u < NP:
                            g, kind = (u // 2) % QUADS, 2 * (u // (2 * QUADS)) + u % 2
                            nc.vector.scalar_tensor_tensor((raw, part)[u % 2][:, u // 2, :], PQ[u % 2],
                                                           bp[:, kind, g:g + 1], rope[:, kind, :], ALU.add,
                                                           ALU.mult).then_inc(proj_read, 1)
                        else:
                            nc.vector.tensor_tensor(vp[:, u - NP, :], PQ[u % 2], bv[:, :],
                                                    ALU.add).then_inc(proj_read, 1)
                        if u >= 4 and u % 2 == 0:
                            unite((u - 4) // 2)

                    def take_maxima(g):
                        for i in range(TPS):
                            for r in range(4):
                                n = (g * TPS + i) * 4 + r
                                dve.wait_ge(scores_done, b * HEADS * TPS + (n + 1))
                                nc.vector.tensor_reduce(nmax[:, g, i, r * SLOT + MROW:r * SLOT + MROW + 1],
                                                        PS[r],
                                                        AX.X, ALU.max, negate=True).then_inc(max_done, 1)

                    def normalize(g):
                        dve.wait_ge(den_done, b * QUADS + (g + 1))
                        nc.vector.reciprocal(rden[:, g, :], PQ[g % 2]).then_inc(rden_done, 1)
                        dve.wait_ge(rden_done, b * QUADS + (g + 1) + FIRST)
                        nc.vector.tensor_tensor(yt[:, g, :], yt[:, g, :], rden[:, g, :], ALU.mult).then_inc(norm_done, 1)

                    take_maxima(0)
                    for g in range(QUADS):
                        if g + 1 < QUADS:
                            take_maxima(g + 1)
                        dve.wait_ge(maxt_done, b * QUADS + (g + 1))
                        nc.vector.tensor_tensor(qk[:, g, :], qk[:, g, :].bitcast(FP32), PO,
                                                ALU.add).then_inc(q_ready, 1)
                        if g:
                            normalize(g - 1)
                    normalize(QUADS - 1)
                    dve.wait_ge(out_done, b + 1)
                    nc.vector.scalar_tensor_tensor(xr(b), PO, bo[:, 0:1], xr(b), ALU.add, ALU.add).then_inc(out_read, 1)

            @block.scalar
            def _(act):
                act.wait_ge(loaded, 144)
                with act.Fori(0, SEQS) as b:
                    for i in range(2 * QUADS):
                        act.wait_ge(rot_ready, b * 2 * QUADS + (i + 1))
                        nc.scalar.activation(qk[:, i, :], raw[:, i, :], ACT.Copy)
                        nc.scalar.activation(part[:, i, :], raw[:, i, :], ACT.Copy,
                                             scale=split[:, i // QUADS, 1:2]).then_inc(hi_ready, 1)
                    for h in range(HEADS):
                        for j in range(TPS):
                            act.wait_ge(keyed_done, (b * HEADS + h) * TPS + (j + 1))
                            if j == 0 and h >= 2:
                                act.wait_ge(y_done, b * HEADS + (h - 1))
                            nc.scalar.activation(pt[:, h % 2, j, :], PS[j], ACT.Exp).then_inc(exp_done, 1)
                        if h % 4 == 3:
                            g = h // 4
                            act.wait_ge(y_done, b * HEADS + (h + 1))
                            nc.scalar.activation(yt[:, g, :], PY, ACT.Copy).then_inc(y_read, 1)

def transformer_stage(nc, ps, sem, w, xa, xb, ones, eps, ident):
    with ExitStack() as c:
        def sb(name, shape, dt=FP32):
            return c.enter_context(nc.sbuf_tensor(f"tr_{name}", shape, dt))

        NQKV = TPS * SEQS + 1
        NXS = NQKV + 1
        UNITS = 8
        QKV0 = 3 * INNER

        whi = sb("whi", [128, QKV0], F32R)
        wlo = sb("wlo", [128, QKV0], F32R)
        wo = sb("wo", [128, PAIRS, 128])
        w1 = sb("w1", [128, 2 * HID])
        w2 = sb("w2", [128, HT, 128])
        b1 = sb("b1", [128, 2 * HT])
        b2 = sb("b2", [128, 1])
        lng = sb("lng", [128, 1])
        lnb = sb("lnb", [128, 1])
        qks = sb("qks", [128, 2, DH])
        base = sb("base", [128, 4, TPS, DH])
        rope = sb("rope", [128, 4, TPS, DH])
        identb = sb("identb", [128, 128], BF16)
        mask = sb("mask", [128, 2, PAIRS * 2 * WIN], BF16)
        half = sb("half", [128, 2 * HEADS])
        xhi = sb("xhi", [128, 2, WIN + TILE], F32R)
        xlo = sb("xlo", [128, 2, WIN + TILE], F32R)
        vs = sb("vs", [128, 2, 2, INNER])
        va, vb = vs[:, 0], vs[:, 1]
        qm = sb("qm", [128, 2, 4, CH])
        sqr = sb("sqr", [128, 2, CH])
        ss = sb("ss", [128, 2 * HEADS])
        rn = sb("rn", [128, 2, 2 * HEADS])
        qt = sb("qt", [128, PAIRS, TILE])
        kt = sb("kt", [128, 2, PAIRS, WIN + TILE])
        mx = sb("mx", [128, 2, PAIRS])
        nb = sb("nb", [128, 2, PAIRS])
        pw = sb("pw", [128, HEADS + 1, 2 * WIN])
        rs = sb("rs", [128, HEADS])
        rr = sb("rr", [128, HEADS])
        pt = sb("pt", [128, HEADS, TILE])
        on = sb("on", [128, INNER])
        ot = sb("ot", [128, PAIRS, L])
        xf = sb("xf", [128, TOK])
        fsq = ot[:, :, :].rearrange("p a b -> p (a b)")
        fsd = qm[:, :, :, :].rearrange("p a b c -> p (a b c)")
        wraw = fsq[:, 0:QKV0]
        hb = vs[:, :, :, :].rearrange("p a b c -> p (a b c)")[:, 0:2 * HT * CH].rearrange(
            "p (a j c) -> p a j c", a=2, c=CH)

        const_loaded = sem("tr_const_loaded")
        pe_passed = sem("tr_pe_passed")
        dve_passed = sem("tr_dve_passed")
        pool_passed = sem("tr_pool_passed")
        attn_loaded = sem("tr_attn_loaded")
        mlp_loaded = sem("tr_mlp_loaded")
        init_done = sem("tr_init_done")
        scales_done = sem("tr_scales_done")
        wraw_loaded = sem("tr_wraw_loaded")
        whi_ready = sem("tr_whi_ready")
        wlo_ready = sem("tr_wlo_ready")
        xhi_ready = sem("tr_xhi_ready")
        xs_ready = sem("tr_xs_ready")
        proj_done = sem("tr_proj_done")
        v_copied = sem("tr_v_copied")
        rot_done = sem("tr_rot_done")
        sq_done = sem("tr_sq_done")
        ss_done = sem("tr_ss_done")
        pool_step = sem("tr_pool_step")
        q_ready = sem("tr_q_ready")
        norms_ready = sem("tr_norms_ready")
        k_ready = sem("tr_k_ready")
        turn_done = sem("tr_turn_done")
        turn_read = sem("tr_turn_read")
        kprev_done = sem("tr_kprev_done")
        scores_done = sem("tr_scores_done")
        max_done = sem("tr_max_done")
        bias_ready = sem("tr_bias_ready")
        exp_done = sem("tr_exp_done")
        again_done = sem("tr_again_done")
        pv_done = sem("tr_pv_done")
        rsum_done = sem("tr_rsum_done")
        on_ready = sem("tr_on_ready")
        wo_done = sem("tr_wo_done")
        xb_ready = sem("tr_xb_ready")
        xf_ready = sem("tr_xf_ready")
        mean_done = sem("tr_mean_done")
        centered = sem("tr_centered")
        squared = sem("tr_squared")
        var_done = sem("tr_var_done")
        std_done = sem("tr_std_done")
        rstd_done = sem("tr_rstd_done")
        normed = sem("tr_normed")
        xn_ready = sem("tr_xn_ready")
        hid_done = sem("tr_hid_done")
        gelu_done = sem("tr_gelu_done")
        hid_ready = sem("tr_hid_ready")
        mlp_done = sem("tr_mlp_done")
        xa_ready = sem("tr_xa_ready")

        PK = [ps[:, 0:CH], ps[:, CH:2 * CH]]
        PT = [ps[:, 2 * CH:3 * CH], ps[:, 3 * CH:4 * CH]]
        PS = [ps[:, 4 * CH:5 * CH], ps[:, 5 * CH:6 * CH]]
        PV = [ps[:, 6 * CH:7 * CH], ps[:, 7 * CH:8 * CH]]
        BANK = PT + PS + PK + PT + PT
        TURNS = 10
        LTURNS = TURNS * TPS * SEQS + 4
        MLPU = 2 * HT

        attn_weights = ((wo[:, :, :].rearrange("p a b -> p (a b)"), "tr_wo"),)
        mlp_weights = ((w1[:, :], "tr_w1"), (w2[:, :, :].rearrange("p a b -> p (a b)"), "tr_w2"),
                       (b1[:, :], "tr_b1"), (b2[:, :], "tr_b2"), (lng[:, :], "tr_lng"), (lnb[:, :], "tr_lnb"))
        CONST_LOADS = 48
        ATTN_LOADS = 16 * (len(attn_weights) + 1)
        MLP_LOADS = 16 * len(mlp_weights)

        def tile_heads(ap):
            return ap.rearrange("p (h d) -> p h d", d=DH)

        from_first = (exp_done, gelu_done, hid_ready, max_done, mlp_done, norms_ready, on_ready, pv_done, ss_done,
                      xa_ready, xb_ready, var_done)

        with nc.Block() as block:

            @block.sync
            def _(sp):
                for counter in from_first:
                    sp.sem_inc(counter, FIRST)
                sp.dma_start(base[:, :, :, :], w["c_xpos"]).then_inc(const_loaded, 16)
                sp.dma_start(identb[:, :], w["c_identb"]).then_inc(const_loaded, 16)
                sp.dma_start(mask[:, :, :], w["c_mask"]).then_inc(const_loaded, 16)
                with sp.Fori(0, DEPTH) as l:
                    sp.wait_ge(xb_ready, l * 2 * SEQS + FIRST)
                    for dst, name in attn_weights:
                        sp.dma_start(dst, w[name][bass.ds(l * 128, 128), :]).then_inc(attn_loaded, 16)
                    sp.dma_start(qks[:, :, :].rearrange("p a b -> p (a b)"),
                                 w["tr_qks"][bass.ds(l * 128, 128), :]).then_inc(attn_loaded, 16)
                    sp.wait_ge(var_done, l * SEQS + FIRST)
                    sp.dma_start(wraw, w["tr_wqkv"][bass.ds(l * 128, 128), :]).then_inc(wraw_loaded, 16)
                    sp.wait_ge(xa_ready, l * SEQS + FIRST)
                    for dst, name in mlp_weights:
                        sp.dma_start(dst, w[name][bass.ds(l * 128, 128), :]).then_inc(mlp_loaded, 16)

            @block.gpsimd
            def _(pool):
                def inverse_norms(q, par, i):
                    cols = slice(HEADS, 2 * HEADS) if i == 0 else slice(0, HEADS)
                    pool.wait_ge(ss_done, q * 2 + (i + 1) + FIRST)
                    stand_alone(pool, pool_passed)
                    nc.gpsimd.tensor_scalar(ss[:, cols], ss[:, cols], 1e-24, None, ALU.max).then_inc(pool_step, 1)
                    pool.wait_ge(pool_step, q * 5 + (2 + 2 * i))
                    nc.gpsimd.tensor_tensor(rn[:, par, cols], ss[:, cols], half[:, cols],
                                            ALU.pow).then_inc(pool_step, 1)
                    pool.wait_ge(pool_step, q * 5 + (3 + 2 * i))

                def finish(q, par, n=None):
                    pool.wait_ge(rot_done, q * 4 + 2)
                    nc.gpsimd.tensor_tensor(qm[:, 0, 2:4, :], qm[:, 0, 2:4, :], qm[:, 1, 2:4, :],
                                            ALU.add).then_inc(pool_step, 1)
                    inverse_norms(q, par, 0)
                    if n is not None:
                        pool.wait_ge(exp_done, n * HEADS + 1 + FIRST)
                        stand_alone(pool, pool_passed)
                        nc.gpsimd.tensor_copy(pw[:, HEADS, :], pw[:, 0, :]).then_inc(again_done, 1)
                    k3 = qm[:, 0, 2:4, :].rearrange("p a (h d) -> p (a h) d", d=DH)
                    nc.gpsimd.tensor_tensor(k3, k3, rn[:, par, HEADS:].unsqueeze(2).broadcast_to([128, HEADS, DH]),
                                            ALU.mult).then_inc(k_ready, 1)
                    pool.wait_ge(rot_done, q * 4 + 4)
                    nc.gpsimd.tensor_tensor(qm[:, 0, 0:2, :], qm[:, 0, 0:2, :], qm[:, 1, 0:2, :],
                                            ALU.add).then_inc(q_ready, 1)
                    inverse_norms(q, par, 1)
                    stand_alone(pool, pool_passed)
                    nc.gpsimd.tensor_scalar(rn[:, par, 0:HEADS], rn[:, par, 0:HEADS], 8.0, None,
                                            ALU.mult).then_inc(norms_ready, 1)

                nc.gpsimd.memset(half[:, :], -0.5).then_inc(init_done, 1)
                nc.gpsimd.memset(kt[:, :, :, :], 0.0).then_inc(init_done, 1)
                pool.wait_ge(init_done, 2)
                with pool.Fori(0, DEPTH) as l:
                    pool.wait_ge(exp_done, l * (HEADS * TPS * SEQS) + FIRST)
                    finish(l * NQKV, 0)
                    with pool.Fori(0, SEQS) as b:
                        for p in range(TPS):
                            q = l * NQKV + b * TPS + (p + 1)
                            n = (l * SEQS + b) * TPS + p
                            finish(q, (p + 1) % 2, n)

            @block.tensor
            def _(pe):
                def project(q, par, units, shifted, turns, outputs):
                    pe.wait_ge(xs_ready, shifted)
                    for u in units:
                        i = u % 2
                        if u == 0 and turns is not None:
                            pe.wait_ge(turn_read, turns)
                        elif u == 2:
                            pe.wait_ge(on_ready, outputs + FIRST)
                        elif 4 <= u < 6:
                            pe.wait_ge(rot_done, q * 4 + (i + 1))
                        elif u >= 6:
                            pe.wait_ge(v_copied, q * 4 + (i + 1))
                        tokens = slice(0, TILE) if u >= 6 else slice(WIN, WIN + TILE)
                        at = (1, 2, 0, 2)[u // 2] * INNER + (u % 2) * CH
                        for k, (x, wt) in enumerate(((xhi, whi), (xlo, whi), (xhi, wlo))):
                            last = nc.tensor.matmul((PK, PV)[u // 2 % 2][i], x[:, par, tokens], wt[:, at:at + CH],
                                                    start=(k == 0), stop=(k == 2))
                        last.then_inc(proj_done, 1)

                def turn_qk(q, turns=None):
                    for k in range(4):
                        bank = BANK[4 + k]
                        if k < 2:
                            pe.wait_ge(sq_done, q * 4 + (k + 3))
                        elif turns is not None:
                            pe.wait_ge(turn_read, turns + (k - 1))
                        pe.wait_ge((k_ready, q_ready)[k // 2], q + 1)
                        for i in range(4):
                            last = nc.tensor.transpose(bank[:, i * 128:(i + 1) * 128],
                                                       qm[:, 0, (k + 2) % 4, i * 128:(i + 1) * 128], ident[:, :])
                        last.then_inc(turn_done, 1)

                def turn_result(n, turns):
                    for k in range(2):
                        bank = BANK[8 + k]
                        pe.wait_ge(turn_read, turns + (k + 7))
                        pe.wait_ge(on_ready, n * 2 + 2 + FIRST)
                        for i in range(4):
                            a = (4 * k + i) * 128
                            last = nc.tensor.transpose(bank[:, i * 128:(i + 1) * 128], on[:, a:a + 128], ident[:, :])
                        last.then_inc(turn_done, 1)

                with pe.Fori(0, DEPTH) as l:
                    pe.wait_ge(attn_loaded, (l + 1) * ATTN_LOADS)
                    pe.wait_ge(wlo_ready, l * 3 + 3)
                    project(l * NQKV, 0, range(UNITS), l * (2 * NXS) + 2, None, l * (2 * TPS * SEQS))
                    turn_qk(l * NQKV)
                    with pe.Fori(0, SEQS) as b:
                        for p in range(TPS):
                            q = l * NQKV + b * TPS + p
                            seq = l * SEQS + b
                            n = seq * TPS + p
                            par = p % 2
                            t0 = l * LTURNS + b * (TPS * TURNS) + (p * TURNS + 4)
                            xs_next = (l * NXS + b * TPS + p) * 2 + 4
                            project(q + 1, 1 - par, range(2), xs_next, t0 - 4 if p else t0 - 2, n * 2)
                            pe.wait_ge(exp_done, n * HEADS + FIRST)
                            pe.wait_ge(max_done, n * 2 + FIRST)
                            for e in range(2):
                                nc.tensor.matmul(PS[e], identb[:, :], mask[:, min(p, 1), :], start=True, stop=False,
                                                 skip_group_check=True)
                            pe.wait_ge(turn_read, t0 - 2 if p else t0)
                            pe.wait_ge(kprev_done, q + 1)
                            stand_alone(pe, pe_passed)
                            for hp in range(PAIRS):
                                for e in range(2):
                                    r = slice(64 * e, 64 * e + 64)
                                    for wi in range(WPT):
                                        last = nc.tensor.matmul(
                                            PS[e][wi * WIN:(wi + 1) * WIN, hp * 2 * WIN:(hp + 1) * 2 * WIN],
                                            qt[r, hp, wi * WIN:(wi + 1) * WIN],
                                            kt[r, par, hp, wi * WIN:(wi + 2) * WIN],
                                            start=False, stop=(hp == PAIRS - 1), skip_group_check=True)
                            last.then_inc(scores_done, 1)
                            if p:
                                turn_result(n - 1, t0 - TURNS)
                            project(q + 1, 1 - par, range(2, UNITS), xs_next, None, n * 2)
                            def weights_across(ks):
                                for k in ks:
                                    bank = BANK[k]
                                    if k == 2:
                                        pe.wait_ge(max_done, n * 2 + 2 + FIRST)
                                    elif k < 2 and p == 0:
                                        pe.wait_ge(xb_ready, seq * 2 + FIRST)
                                    elif k < 2:
                                        pe.wait_ge(turn_read, t0)
                                    pe.wait_ge(exp_done, n * HEADS + min(4 * (k + 1) + 1, HEADS) + FIRST)
                                    if k == 3:
                                        pe.wait_ge(again_done, n + 1)
                                    for i in range(4):
                                        h = 4 * k + i
                                        last = nc.tensor.transpose(bank[:, i * 128:(i + 1) * 128],
                                                                   pw[:, h:h + 2, :].rearrange("p a b -> p (a b)"),
                                                                   ident[:, :])
                                    last.then_inc(turn_done, 1)

                            def weigh(up, e):
                                pe.wait_ge(turn_read, t0 + (4 if up or e else 2))
                                stand_alone(pe, pe_passed)
                                for hp in range(PAIRS):
                                    for wi in (2 * up, 2 * up + 1):
                                        r = slice(64 * up, 64 * up + 64)
                                        h, place = 2 * hp + e, e * PAIRS + hp
                                        last = nc.tensor.matmul(
                                            PV[e][wi * WIN:(wi + 1) * WIN, hp * DH:(hp + 1) * DH],
                                            pt[r, (place - up) % HEADS, wi * WIN:(wi + 1) * WIN],
                                            (vb, va)[wi % 2][r, par, h * DH:(h + 1) * DH], start=True, stop=True)
                                if up:
                                    last.then_inc(pv_done, 1)

                            weights_across(range(4))
                            pe.wait_ge(v_copied, q * 4 + 8)
                            weigh(0, 0)
                            weigh(0, 1)
                            weigh(1, 0)
                            weigh(1, 1)
                            turn_qk(q + 1, t0)
                            if p == TPS - 1:
                                turn_result(n, t0)
                        for k in range(2):
                            pe.wait_ge(turn_read, l * LTURNS + b * (TPS * TURNS) + (TPS * TURNS + 4))
                            for hp in range(PAIRS):
                                last = nc.tensor.matmul(PT[k][:, 0:L // 2], wo[:, hp, :],
                                                        ot[:, hp, k * (L // 2):(k + 1) * (L // 2)],
                                                        start=(hp == 0), stop=(hp == PAIRS - 1))
                            last.then_inc(wo_done, 1)
                    with pe.Fori(0, SEQS) as i:
                        pe.wait_ge(xf_ready, l * SEQS + (i + 1))
                        nc.tensor.matmul(ps[:, bass.ds(i * CH, CH)], ones[:, :], xf[:, bass.ds(i * CH, CH)],
                                         start=True, stop=True).then_inc(mean_done, 1)
                    with pe.Fori(0, SEQS) as i:
                        pe.wait_ge(squared, l * SEQS + (i + 1))
                        nc.tensor.matmul(ps[:, bass.ds(i * CH, CH)], ones[:, :], fsq[:, bass.ds(i * CH, CH)],
                                         start=True, stop=True).then_inc(var_done, 1)
                    pe.wait_ge(mlp_loaded, (l + 1) * MLP_LOADS)
                    pe.wait_ge(std_done, (l + 1) * SEQS)
                    stand_alone(pe, pe_passed)
                    with pe.Fori(0, SEQS // 2) as i2:
                        for par in range(2):
                            i = i2 * 2 + par
                            ch = l * SEQS + i
                            pe.wait_ge(xn_ready, ch + 1)
                            for j in range(HT):
                                for kind in range(2):
                                    pe.wait_ge((gelu_done, hid_ready)[kind], ch * HT + FIRST)
                                    at = (1 - kind) * HID + j * 128
                                    nc.tensor.matmul(ps[0:HW[j], (2 * j + kind) * CH:(2 * j + kind + 1) * CH],
                                                     w1[:, at:at + HW[j]], xf[:, bass.ds(i * CH, CH)],
                                                     start=True, stop=True).then_inc(hid_done, 1)
                            pe.wait_ge(xa_ready, ch - par + FIRST)
                            for j in range(HT):
                                pe.wait_ge(hid_ready, ch * HT + (j + 1) + FIRST)
                                last = nc.tensor.matmul(PV[par], w2[0:HW[j], j, :], hb[0:HW[j], par, j, :],
                                                        start=(j == 0), stop=(j == HT - 1))
                            last.then_inc(mlp_done, 1)

            @block.vector
            def _(dve):
                def shift(j, par, b, t):
                    c0 = b * SEQP + (PAD + 1 + t * TILE - WIN)
                    halves = ((slice(0, 64), c0), (slice(64, 128), c0 - 1))
                    for r, at in halves:
                        nc.vector.tensor_copy(xhi[r, par, :], xa[r, bass.ds(at, WIN + TILE)]).then_inc(xhi_ready, 1)
                    dve.wait_ge(xhi_ready, j * 2 + 2)
                    for r, at in halves:
                        nc.vector.tensor_tensor(xlo[r, par, :], xa[r, bass.ds(at, WIN + TILE)],
                                                xhi[r, par, :].bitcast(FP32), ALU.subtract).then_inc(xs_ready, 1)

                def copy_v(q, par, i):
                    dve.wait_ge(proj_done, q * UNITS + (3, 4, 7, 8)[i])
                    nc.vector.tensor_copy((va, vb)[i // 2][:, par, (i % 2) * CH:(i % 2 + 1) * CH],
                                          PV[i % 2]).then_inc(v_copied, 1)

                def rotate(q, p, i):
                    u = (2, 3, 0, 1)[i]
                    dve.wait_ge(proj_done, q * UNITS + (1, 2, 5, 6)[i])
                    if i < 2:
                        dve.wait_ge(sq_done, q * 4 + (i + 1))
                    src = tile_heads(PK[i % 2])
                    cos, sin = (rope[:, 2 * (u // 2) + s, p, :].unsqueeze(1) for s in range(2))
                    nc.vector.tensor_tensor(tile_heads(qm[:, 0, u, :]), src, cos.broadcast_to([128, 8, DH]), ALU.mult)
                    rot = tile_heads(qm[:, 1, u, :])
                    h = DH // 2
                    nc.vector.tensor_tensor(rot[:, :, 0:h], src[:, :, h:DH], sin[:, :, 0:h].broadcast_to([128, 8, h]),
                                            ALU.mult)
                    nc.vector.tensor_tensor(rot[:, :, h:DH], src[:, :, 0:h], sin[:, :, h:DH].broadcast_to([128, 8, h]),
                                            ALU.mult).then_inc(rot_done, 1)

                def sum_squares(q, i):
                    cols = slice(HEADS, 2 * HEADS) if i == 0 else slice(0, HEADS)
                    if i == 0:
                        dve.wait_ge(norms_ready, q + FIRST)
                    dve.wait_ge(sq_done, q * 4 + (2 * i + 2))
                    nc.vector.tensor_reduce(ss[:, cols], sqr[:, :, :].rearrange("p a (h d) -> p (a h) d", d=DH),
                                            AX.X, ALU.add).then_inc(ss_done, 1)

                def take_vq(q, par, p):
                    copy_v(q, par, 0)
                    copy_v(q, par, 1)
                    rotate(q, p, 2)
                    copy_v(q, par, 2)
                    copy_v(q, par, 3)
                    rotate(q, p, 3)

                dve.wait_ge(const_loaded, CONST_LOADS)
                with dve.Fori(0, DEPTH) as l:
                    for i in (1, 2, 0):
                        dve.wait_ge(whi_ready, l * 3 + ((2, 0, 1)[i] + 1))
                        cols = slice(i * INNER, (i + 1) * INNER)
                        nc.vector.tensor_tensor(wlo[:, cols], wraw[:, cols], whi[:, cols].bitcast(FP32),
                                                ALU.subtract).then_inc(wlo_ready, 1)
                    dve.wait_ge(attn_loaded, (l + 1) * ATTN_LOADS)
                    h = DH // 2
                    for s in range(2):
                        row = qks[:, s, :].unsqueeze(1)
                        nc.vector.tensor_tensor(rope[:, 2 * s, :, :], base[:, 2 * s, :, :],
                                                row.broadcast_to([128, TPS, DH]), ALU.mult)
                        nc.vector.tensor_tensor(rope[:, 2 * s + 1, :, 0:h], base[:, 2 * s + 1, :, 0:h],
                                                row[:, :, h:DH].broadcast_to([128, TPS, h]), ALU.mult)
                        last = nc.vector.tensor_tensor(rope[:, 2 * s + 1, :, h:DH], base[:, 2 * s + 1, :, h:DH],
                                                       row[:, :, 0:h].broadcast_to([128, TPS, h]), ALU.mult)
                    last.then_inc(scales_done, 1)
                    dve.wait_ge(scales_done, l + 1)
                    dve.wait_ge(xa_ready, l * SEQS + FIRST)
                    shift(l * NXS, 0, 0, 0)
                    shift(l * NXS + 1, 1, 0, 1)
                    rotate(l * NQKV, 0, 0)
                    rotate(l * NQKV, 0, 1)
                    sum_squares(l * NQKV, 0)
                    take_vq(l * NQKV, 0, 0)
                    sum_squares(l * NQKV, 1)
                    with dve.Fori(0, SEQS) as b:
                        for p in range(TPS):
                            q = l * NQKV + b * TPS + p
                            seq = l * SEQS + b
                            n = seq * TPS + p
                            par = p % 2
                            dve.wait_ge(proj_done, (q + 1) * UNITS)
                            shift(l * NXS + b * TPS + (p + 2), par, b + (p + 2) // TPS, (p + 2) % TPS)
                            rotate(q + 1, (p + 1) % TPS, 0)
                            sum_squares(q + 1, 0)
                            rotate(q + 1, (p + 1) % TPS, 1)
                            dve.wait_ge(scores_done, n + 1)
                            for e in range(2):
                                nc.vector.tensor_reduce(mx[:, e, :], PS[e].rearrange("p (h j) -> p h j", j=2 * WIN),
                                                        AX.X, ALU.max).then_inc(max_done, 1)
                            dve.wait_ge(max_done, n * 2 + 2 + FIRST)
                            dve.wait_ge(norms_ready, q + 1 + FIRST)
                            nc.vector.scalar_tensor_tensor(
                                nb[:, :, :], mx[:, :, :], -1.0,
                                rn[:, par, 0:HEADS].rearrange("p (h e) -> p e h", e=2), ALU.mult,
                                ALU.mult).then_inc(bias_ready, 1)
                            dve.wait_ge(pv_done, n * 2 + FIRST)
                            take_vq(q + 1, 1 - par, (p + 1) % TPS)
                            dve.wait_ge(exp_done, (n + 1) * HEADS + FIRST)
                            nc.vector.tensor_reduce(rs[:, :], pw[:, 0:HEADS, :], AX.X, ALU.add).then_inc(rsum_done, 1)
                            sum_squares(q + 1, 1)
                            dve.wait_ge(rsum_done, n * 2 + 1)
                            nc.vector.reciprocal(rr[:, :], rs[:, :]).then_inc(rsum_done, 1)
                            dve.wait_ge(rsum_done, n * 2 + 2)
                            for e in range(2):
                                dve.wait_ge(pv_done, n * 2 + (e + 1) + FIRST)
                                nc.vector.tensor_tensor(
                                    on[:, :].rearrange("p (h e d) -> p e h d", e=2, d=DH)[:, e], tile_heads(PV[e]),
                                    rr[:, e * PAIRS:(e + 1) * PAIRS].unsqueeze(2).broadcast_to([128, PAIRS, DH]),
                                    ALU.mult).then_inc(on_ready, 1)
                        for k in range(2):
                            dve.wait_ge(wo_done, (l * SEQS + b) * 2 + (k + 1))
                            cols = bass.ds(b * SEQP + (PAD + 1 + k * (L // 2)), L // 2)
                            nc.vector.tensor_tensor(xb[:, cols], PT[k][:, 0:L // 2], xa[:, cols],
                                                    ALU.add).then_inc(xb_ready, 1)
                    dve.wait_ge(xb_ready, (l + 1) * 2 * SEQS + FIRST)
                    stand_alone(dve, dve_passed)
                    with dve.Fori(0, SEQS) as i:
                        nc.vector.tensor_copy(xf[0:64, bass.ds(i * CH, CH)], xb[0:64, bass.ds(i * SEQP + (PAD + 1), L)])
                        nc.vector.tensor_copy(xf[64:128, bass.ds(i * CH, CH)],
                                              xb[64:128, bass.ds(i * SEQP + PAD, L)]).then_inc(xf_ready, 1)
                    with dve.Fori(0, SEQS) as i:
                        dve.wait_ge(mean_done, l * SEQS + (i + 1))
                        x = xf[:, bass.ds(i * CH, CH)]
                        nc.vector.tensor_tensor(x, x, ps[:, bass.ds(i * CH, CH)], ALU.subtract).then_inc(centered, 1)
                    def norm(i):
                        dve.wait_ge(std_done, l * SEQS + (i + 1))
                        s = fsd[:, bass.ds(i * CH, CH)]
                        nc.vector.reciprocal(s, s).then_inc(rstd_done, 1)
                        dve.wait_ge(rstd_done, l * SEQS + (i + 1))
                        x = xf[:, bass.ds(i * CH, CH)]
                        nc.vector.tensor_tensor(x, x, s, ALU.mult).then_inc(normed, 1)

                    def mlp_pair(i2, last):
                        for par in range(2):
                            i = i2 * 2 + par
                            ch = l * SEQS + i
                            if not (last and par):
                                norm(i + 1)
                            for j in range(HT):
                                dve.wait_ge(hid_done, ch * MLPU + (2 * j + 2))
                                dve.wait_ge(gelu_done, ch * HT + (j + 1) + FIRST)
                                o = hb[0:HW[j], par, j, :]
                                nc.vector.scalar_tensor_tensor(o, ps[0:HW[j], (2 * j + 1) * CH:(2 * j + 2) * CH],
                                                               b1[0:HW[j], j:j + 1], o, ALU.add,
                                                               ALU.mult).then_inc(hid_ready, 1)
                            dve.wait_ge(mlp_done, ch + 1 + FIRST)
                            cols = bass.ds(i * SEQP + (PAD + 1), L)
                            nc.vector.scalar_tensor_tensor(xa[:, cols], PV[par], b2[:, 0:1], xb[:, cols], ALU.add,
                                                           ALU.add).then_inc(xa_ready, 1)

                    norm(0)
                    with dve.Fori(0, SEQS // 2 - 1) as i2:
                        mlp_pair(i2, False)
                    mlp_pair(SEQS // 2 - 1, True)

            @block.scalar
            def _(act):
                def square(q, i):
                    act.wait_ge(ss_done, q * 2 + (i // 2) + FIRST)
                    if i < 2:
                        act.wait_ge(proj_done, q * UNITS + (i + 1))
                    else:
                        act.wait_ge(rot_done, q * 4 + (i + 1))
                    nc.scalar.activation(sqr[:, i % 2, :], PK[i % 2], ACT.Square).then_inc(sq_done, 1)

                def read_qk(par, base):
                    nc.scalar.activation(kt[:, par, :, 0:WIN], kt[:, 1 - par, :, TILE:WIN + TILE],
                                         ACT.Copy).then_inc(kprev_done, 1)
                    for k in range(4):
                        act.wait_ge(turn_done, base + (k + 1))
                        src = BANK[4 + k].rearrange("p (i t) -> p i t", t=TILE)
                        o = 4 * (k % 2)
                        dst = kt[:, par, o:o + 4, WIN:WIN + TILE] if k < 2 else qt[:, o:o + 4, :]
                        nc.scalar.activation(dst, src, ACT.Copy).then_inc(turn_read, 1)

                act.wait_ge(init_done, 2)
                with act.Fori(0, DEPTH) as l:
                    act.wait_ge(wraw_loaded, (l + 1) * 16)
                    for i in (1, 2, 0):
                        cols = slice(i * INNER, (i + 1) * INNER)
                        nc.scalar.activation(whi[:, cols], wraw[:, cols], ACT.Copy).then_inc(whi_ready, 1)
                    for i in range(4):
                        square(l * NQKV, i)
                    read_qk(0, l * LTURNS)
                    with act.Fori(0, SEQS) as b:
                        for p in range(TPS):
                            q = l * NQKV + b * TPS + p
                            seq = l * SEQS + b
                            n = seq * TPS + p
                            par = p % 2
                            t0 = l * LTURNS + b * (TPS * TURNS) + (p * TURNS + 4)
                            def read_weights(k):
                                act.wait_ge(turn_done, t0 + (k + 1))
                                nc.scalar.activation(pt[:, 4 * k:4 * k + 4, :],
                                                     BANK[k].rearrange("p (i t) -> p i t", t=TILE),
                                                     ACT.Copy).then_inc(turn_read, 1)

                            def read_result(p, turns):
                                for k in range(2):
                                    act.wait_ge(turn_done, turns + (k + 9))
                                    nc.scalar.activation(ot[:, 4 * k:4 * k + 4, p * TILE:(p + 1) * TILE],
                                                         BANK[8 + k].rearrange("p (i t) -> p i t", t=TILE),
                                                         ACT.Copy).then_inc(turn_read, 1)

                            square(q + 1, 0)
                            square(q + 1, 1)
                            if p:
                                read_result(p - 1, t0 - TURNS)
                            act.wait_ge(bias_ready, n + 1)
                            for i in range(HEADS):
                                e, hp = i // PAIRS, i % PAIRS
                                hd = 2 * hp + e
                                nc.scalar.activation(pw[:, i, :], PS[e][:, hp * 2 * WIN:(hp + 1) * 2 * WIN],
                                                     ACT.Exp, bias=nb[:, e, hp:hp + 1],
                                                     scale=rn[:, par, hd:hd + 1]).then_inc(exp_done, 1)
                            for k in range(4):
                                read_weights(k)
                            square(q + 1, 2)
                            square(q + 1, 3)
                            read_qk(1 - par, t0 + 4)
                            if p == TPS - 1:
                                read_result(p, t0)
                    with act.Fori(0, SEQS) as i:
                        act.wait_ge(centered, l * SEQS + (i + 1))
                        nc.scalar.activation(fsq[:, bass.ds(i * CH, CH)], xf[:, bass.ds(i * CH, CH)],
                                             ACT.Square).then_inc(squared, 1)
                    for i in range(SEQS):
                        act.wait_ge(var_done, l * SEQS + (i + 1) + FIRST)
                        nc.scalar.activation(fsd[:, i * CH:(i + 1) * CH], ps[:, i * CH:(i + 1) * CH], ACT.Sqrt,
                                             bias=eps[:, 0:1]).then_inc(std_done, 1)
                    act.wait_ge(mlp_loaded, (l + 1) * MLP_LOADS)

                    def affine(i):
                        act.wait_ge(normed, l * SEQS + (i + 1))
                        x = xf[:, bass.ds(i * CH, CH)]
                        nc.scalar.activation(x, x, ACT.Identity, bias=lnb[:, 0:1], scale=lng[:, 0:1]).then_inc(xn_ready, 1)

                    def gelu_pair(i2, last):
                        for par in range(2):
                            ch = l * SEQS + (i2 * 2 + par)
                            for j in range(HT):
                                act.wait_ge(hid_done, ch * MLPU + (2 * j + 1))
                                if j == 0:
                                    act.wait_ge(mlp_done, ch - par + FIRST)
                                nc.scalar.activation(hb[0:HW[j], par, j, :], ps[0:HW[j], 2 * j * CH:(2 * j + 1) * CH],
                                                     ACT.Gelu, bias=b1[0:HW[j], HT + j:HT + j + 1]).then_inc(gelu_done, 1)
                                if j == 0 and not (last and par):
                                    affine(i2 * 2 + par + 1)

                    affine(0)
                    with act.Fori(0, SEQS // 2 - 1) as i2:
                        gelu_pair(i2, False)
                    gelu_pair(SEQS // 2 - 1, True)


def mlp_stage(nc, ps, sem, w, xn, xr, xcat, ones4, eps):
    with ExitStack() as c:
        def sb(name, shape, dt=FP32):
            return c.enter_context(nc.sbuf_tensor(f"ml_{name}", shape, dt))

        wf = sb("wf", [128, MLP])
        wp = sb("wp", [128, MT, 128])
        neg = sb("neg", [128, MLP])
        lnw = sb("lnw", [128, MT])
        lnb = sb("lnb", [128, MT])
        asum = sb("asum", [128, 2])
        ga = sb("ga", [128, 4])
        hid = sb("hid", [128, MT, TOK])
        sq = sb("sq", [128, 2, MT, CH])
        sd = sb("sd", [128, 2, CH])
        loaded = sem("ml_loaded")
        prep = sem("ml_prep")
        asum_done = sem("ml_asum_done")
        gamma_done = sem("ml_gamma_done")
        w_ready = sem("ml_w_ready")
        hid_done = sem("ml_hid_done")
        gelu_done = sem("ml_gelu_done")
        mean_done = sem("ml_mean_done")
        centered = sem("ml_centered")
        squared = sem("ml_squared")
        var_done = sem("ml_var_done")
        std_done = sem("ml_std_done")
        rstd_done = sem("ml_rstd_done")
        normed = sem("ml_normed")
        affine_done = sem("ml_affine_done")
        out_done = sem("ml_out_done")
        out_read = sem("ml_out_read")
        stored = sem("ml_stored")
        act_passed = sem("ml_act_passed")

        def bank(k):
            return ps[:, k * CH:(k + 1) * CH]

        from_first = (centered, gelu_done, out_read, std_done)

        with nc.Block() as block:

            @block.sync
            def _(sp):
                for counter in from_first:
                    sp.sem_inc(counter, FIRST)
                sp.dma_start(wf[:, :], w["ml_wf"]).then_inc(loaded, 16)
                sp.dma_start(wp[:, :, :], w["ml_wp"]).then_inc(loaded, 16)
                sp.dma_start(lnw[:, :], w["ml_lnw"]).then_inc(loaded, 16)
                sp.dma_start(lnb[:, :], w["ml_lnb"]).then_inc(loaded, 16)
                with sp.Fori(0, SEQS) as i:
                    sp.wait_ge(out_read, i + 1 + FIRST)
                    sp.dma_start(xcat[:, bass.ds(i * CH, CH)], xr(i)).then_inc(stored, 16)
                sp.wait_ge(stored, 16 * SEQS)

            @block.tensor
            def _(pe):
                pe.wait_ge(asum_done, 1)
                nc.tensor.matmul(bank(0)[:, 0:2], ones4[:, :], asum[:, :], start=True, stop=True).then_inc(gamma_done, 1)
                pe.wait_ge(w_ready, 1)
                with pe.Fori(0, SEQS) as i:
                    for j in range(MT):
                        pe.wait_ge(gelu_done, i * MT + FIRST)
                        nc.tensor.matmul(bank(j), wf[:, j * 128:(j + 1) * 128], xn(i),
                                         start=True, stop=True).then_inc(hid_done, 1)
                with pe.Fori(0, SEQS // 2) as i2:
                    for par in range(2):
                        i = i2 * 2 + par
                        pe.wait_ge(gelu_done, SEQS * MT + FIRST)
                        pe.wait_ge(centered, i * MT + FIRST)
                        for j in range(MT):
                            last = nc.tensor.matmul(bank(par), ones4[:, :], hid[:, j, bass.ds(i * CH, CH)],
                                                    start=(j == 0), stop=(j == MT - 1))
                        last.then_inc(mean_done, 1)
                        pe.wait_ge(std_done, i + FIRST)
                        for j in range(MT):
                            pe.wait_ge(squared, i * MT + (j + 1))
                            last = nc.tensor.matmul(bank(2 + par), ones4[:, :], sq[:, par, j, :],
                                                    start=(j == 0), stop=(j == MT - 1))
                        last.then_inc(var_done, 1)
                        pe.wait_ge(out_read, i + FIRST)
                        for j in range(MT):
                            pe.wait_ge(affine_done, i * MT + (j + 1))
                            last = nc.tensor.matmul(bank(4 + par), wp[:, j, :], hid[:, j, bass.ds(i * CH, CH)],
                                                    start=(j == 0), stop=(j == MT - 1))
                        last.then_inc(out_done, 1)

            @block.vector
            def _(dve):
                steps = [0]

                def link(ins):
                    steps[0] += 1
                    ins.then_inc(prep, 1)
                    dve.wait_ge(prep, steps[0])

                dve.wait_ge(loaded, 64)
                link(nc.vector.tensor_reduce(asum[:, 0:1], wf[:, :], AX.X, ALU.add, apply_absolute_value=True))
                nc.vector.tensor_reduce(asum[:, 1:2], wp[:, :, :], AX.XY, ALU.add,
                                        apply_absolute_value=True).then_inc(asum_done, 1)
                dve.wait_ge(gamma_done, 1)
                link(nc.vector.tensor_scalar(ga[:, 0:2], bank(0)[:, 0:2], 1.0 / 128, 1e-6, ALU.mult, ALU.add))
                link(nc.vector.tensor_scalar(ga[:, 0:2], ga[:, 0:2], 0.5, None, ALU.mult))
                link(nc.vector.tensor_scalar(ga[:, 2:4], ga[:, 0:2], -1.0, None, ALU.mult))
                for k, m in ((0, wf[:, :]), (1, wp[:, :, :].rearrange("p a b -> p (a b)"))):
                    link(nc.vector.tensor_scalar(neg[:, :], m, ga[:, 2 + k:3 + k], None, ALU.is_lt))
                    link(nc.vector.tensor_scalar(m, m, ga[:, k:k + 1], None, ALU.is_gt))
                    link(nc.vector.tensor_tensor(m, m, neg[:, :], ALU.subtract))
                nc.vector.tensor_copy(ga[:, 0:1], ga[:, 1:2]).then_inc(w_ready, 1)
                with dve.Fori(0, SEQS // 2) as i2:
                    for par in range(2):
                        i = i2 * 2 + par
                        dve.wait_ge(mean_done, i + 1)
                        for j in range(MT):
                            h = hid[:, j, bass.ds(i * CH, CH)]
                            nc.vector.tensor_tensor(h, h, bank(par), ALU.subtract).then_inc(centered, 1)
                        dve.wait_ge(std_done, i + 1 + FIRST)
                        nc.vector.reciprocal(sd[:, par, :], sd[:, par, :]).then_inc(rstd_done, 1)
                        dve.wait_ge(rstd_done, i + 1)
                        for j in range(MT):
                            h = hid[:, j, bass.ds(i * CH, CH)]
                            nc.vector.scalar_tensor_tensor(h, h, lnw[:, j:j + 1], sd[:, par, :], ALU.mult,
                                                           ALU.mult).then_inc(normed, 1)
                        dve.wait_ge(out_done, i + 1)
                        nc.vector.tensor_tensor(xr(i), xr(i), bank(4 + par), ALU.add).then_inc(out_read, 1)

            @block.scalar
            def _(act):
                with act.Fori(0, SEQS) as i:
                    for j in range(MT):
                        act.wait_ge(hid_done, i * MT + (j + 1))
                        nc.scalar.activation(hid[:, j, bass.ds(i * CH, CH)], bank(j), ACT.Gelu).then_inc(gelu_done, 1)
                with act.Fori(0, SEQS // 2) as i2:
                    for par in range(2):
                        i = i2 * 2 + par
                        for j in range(MT):
                            act.wait_ge(centered, i * MT + (j + 1) + FIRST)
                            nc.scalar.activation(sq[:, par, j, :], hid[:, j, bass.ds(i * CH, CH)],
                                                 ACT.Square).then_inc(squared, 1)
                        act.wait_ge(var_done, i + 1)
                        nc.scalar.activation(sd[:, par, :], bank(2 + par), ACT.Sqrt, bias=eps[:, 0:1]).then_inc(std_done, 1)
                        for j in range(MT):
                            act.wait_ge(normed, i * MT + (j + 1))
                            stand_alone(act, act_passed)
                            h = hid[:, j, bass.ds(i * CH, CH)]
                            nc.scalar.activation(h, h, ACT.Identity, bias=lnb[:, j:j + 1]).then_inc(affine_done, 1)


def program(nc, w, out):
    ctx = ExitStack()
    with ctx:
        def sem(name):
            return ctx.enter_context(nc.semaphore(name))

        def sb(name, shape, dt=FP32):
            return ctx.enter_context(nc.sbuf_tensor(name, shape, dt))

        xr = sb("xr", [128, TOK])
        xa = sb("xa", [128, XCOLS])
        xb = sb("xb", [128, XCOLS])
        ones = sb("ones", [128, 128])
        ones4 = sb("ones4", [128, 128])
        eps = sb("eps", [128, 1])
        ident = sb("ident", [128, 128])
        ps = ctx.enter_context(nc.psum_tensor("ps", [128, 8 * CH], FP32))
        x_loaded = sem("x_loaded")

        def plain(i):
            return xr[:, bass.ds(i * L, L)]

        def padded(buf):
            return lambda i: buf[:, bass.ds(i * SEQP + (PAD + 1), L)]

        with nc.Block() as block:

            @block.sync
            def _(sp):
                sp.dma_start(xr[:, :], w["x"]).then_inc(x_loaded, 16)
                sp.dma_start(ident[:, :], w["c_ident"]).then_inc(x_loaded, 16)
                sp.wait_ge(x_loaded, 32)

            @block.vector
            def _(dve):
                nc.vector.memset(xa[:, :], 0.0)
                nc.vector.memset(ones[:, :], 1.0 / D)
                nc.vector.memset(ones4[:, :], 1.0 / MLP)
                nc.vector.memset(eps[:, :], LN_EPS)

            @block.gpsimd
            def _(pool):
                nc.gpsimd.memset(xb[:, :], 0.0)

        layernorm_stage(nc, ps, sem, "a", plain, padded(xa), ones, eps)
        retention_stage(nc, ps, sem, w, padded(xa), plain, eps)
        transformer_stage(nc, ps, sem, w, xa, xb, ones, eps, ident)
        layernorm_stage(nc, ps, sem, "b", plain, padded(xb), ones, eps, src2=padded(xa))
        softmax_stage(nc, ps, sem, w, padded(xb), plain, ident)
        mlp_stage(nc, ps, sem, w, padded(xb), plain, out, ones4, eps)


def constants():
    f = np.float32
    t = {}
    c = np.arange(L)[None, :] - np.arange(128)[:, None]
    t["c_lag"] = np.maximum(c, 0).astype(f)
    t["c_ident"] = np.eye(128, dtype=f)
    bf = mybir.dt.np(BF16)
    t["c_identb"] = np.eye(128).astype(bf)
    i, j = (np.arange(128) % WIN)[:, None], np.arange(2 * WIN)[None, :]
    seen = (j >= i) & (j <= i + WIN)
    first = seen & ((j >= WIN) | (np.arange(128) >= WIN)[:, None])
    m = np.stack([np.where(first, 0.0, -1e30), np.where(seen, 0.0, -1e30)], 1)
    t["c_mask"] = np.ascontiguousarray(np.tile(m, (1, 1, PAIRS))).astype(bf)
    half = np.arange(0, DH, 2, dtype=f)
    inv = (f(1.0) / f(10000.0) ** (half / f(DH))).astype(f)
    pos = np.arange(L, dtype=f)
    fr = pos[:, None] * inv[None, :]
    fr = np.concatenate([fr, fr], -1)
    bs = (half + f(0.4 * DH)) / f(1.4 * DH)
    power = (pos - L // 2) / f(WIN // 2)
    sc = bs[None, :] ** power[:, None]
    sc = np.concatenate([sc, sc], -1).astype(f)
    sgn = np.where(np.arange(DH) < DH // 2, -1, 1).astype(f)
    tb = np.stack([np.cos(fr) * sc, np.sin(fr) * sc * sgn, np.cos(fr) / sc, np.sin(fr) / sc * sgn])
    t["c_xpos"] = np.ascontiguousarray(tb.reshape(4, TPS, 128, DH).transpose(2, 0, 1, 3).astype(f))
    hh = DK // 2
    inv = (f(1.0) / f(10000.0) ** (np.arange(hh, dtype=f) / f(hh))).astype(f)
    ang = pos[:, None] * inv[None, :]
    rt = np.zeros((SLOT, 4, L), f)
    for k, s in ((0, f(DK ** -0.5)), (2, f(1.0))):
        for r in range(0, MROW, DK):
            rt[r:r + hh, k], rt[r + hh:r + DK, k] = np.cos(ang).T * s, np.cos(ang).T * s
            rt[r:r + hh, k + 1], rt[r + hh:r + DK, k + 1] = -np.sin(ang).T * s, np.sin(ang).T * s
    rt[MROW, 2] = 1.0
    t["c_rope"] = np.ascontiguousarray(np.tile(rt, (4, 1, 1)))
    sp = np.tile(np.array([1, 0], f), (SLOT, 2, 1))
    sp[DK:2 * DK, 0] = sp[2 * DK:3 * DK, 1] = (-1, 1)
    t["c_split"] = np.tile(sp, (4, 1, 1))
    b = np.zeros((SLOT, SLOT), f)
    b[DK, :] = 1.0
    t["c_bsel"] = np.kron(np.eye(4, dtype=f), b)
    return t


def slots(m, times=1):
    p = np.zeros((m.shape[0], HEADS, SLOT), m.dtype)
    p[:, :, :times * DK] = np.tile(m.reshape(m.shape[0], HEADS, DK), (1, 1, times))
    return p.reshape(m.shape[0], HEADS * SLOT)


def slot_rows(m):
    return np.ascontiguousarray(slots(np.ascontiguousarray(m.T)).T.reshape(QUADS, 128, -1).transpose(1, 0, 2))


def layout(inp):
    f = {k: np.asarray(v) for k, v in inp.items()}
    w = constants()
    w["x"] = np.ascontiguousarray(f["L0_attn_x"].reshape(TOK, D).T)
    qkv = f["L0_attn_W_qkv"]
    w["ret_wq"] = slots(qkv[0:D].T, SPLIT)
    w["ret_wk"] = np.ascontiguousarray(qkv[D:2 * D].T)
    w["ret_wv"] = slots(qkv[2 * D:3 * D].T)
    w["ret_wo"] = slot_rows(f["L0_attn_W_o"].T)
    w["log_gamma"] = f["L0_attn_log_gamma"]
    w["tr_wqkv"] = f["L0_ffn_Wqkv"].reshape(DEPTH * D, 3 * INNER)
    w["tr_wo"] = np.ascontiguousarray(f["L0_ffn_Wo"].reshape(DEPTH, PAIRS, 128, D).transpose(0, 2, 1, 3)
                                      ).reshape(DEPTH * 128, PAIRS * D)
    w["tr_w1"] = f["L0_ffn_W1"].reshape(DEPTH * D, 2 * HID)
    w2 = np.zeros((DEPTH, HT * 128, D), np.float32)
    w2[:, :HID] = f["L0_ffn_W2"]
    w["tr_w2"] = np.ascontiguousarray(w2.reshape(DEPTH, HT, 128, D).transpose(0, 2, 1, 3)).reshape(DEPTH * 128, HT * D)
    b1 = np.zeros((DEPTH, 2, HT * 128), np.float32)
    b1[:, :, :HID] = f["L0_ffn_b1"].reshape(DEPTH, 2, HID)
    w["tr_b1"] = np.ascontiguousarray(b1.reshape(DEPTH, 2 * HT, 128).transpose(0, 2, 1)).reshape(DEPTH * 128, 2 * HT)
    for name, key in (("tr_b2", "L0_ffn_b2"), ("tr_lng", "L0_ffn_ln_g"), ("tr_lnb", "L0_ffn_ln_b")):
        w[name] = f[key].reshape(DEPTH * 128, 1)
    s = np.concatenate([f["L0_ffn_q_scale"], f["L0_ffn_k_scale"]], 1)
    w["tr_qks"] = np.ascontiguousarray(np.repeat(s, 128, 0))
    def swap(m):
        return np.ascontiguousarray(m.reshape(-1, HEADS, 2, DK // 2)[:, :, ::-1]).reshape(m.shape)
    ws, bs = [], []
    for n in "qk":
        for fn in (lambda m: m, swap):
            ws.append(slots(fn(f[f"L1_attn_w{n}_w"]), SPLIT))
            bs.append(slots(fn(f[f"L1_attn_w{n}_b"][None]), SPLIT))
    w["sm_wp"] = np.ascontiguousarray(np.stack(ws, 1))
    bs[2].reshape(HEADS, SLOT)[:, MROW] = 1.0
    w["sm_bp"] = np.ascontiguousarray(np.stack(bs).reshape(4, QUADS, 128).transpose(2, 0, 1))
    w["sm_wv"] = slots(f["L1_attn_wv_w"])
    bv = slots(f["L1_attn_wv_b"][None])
    bv.reshape(HEADS, SLOT)[:, DK] = 1.0
    w["sm_bv"] = bv.reshape(-1)
    w["sm_wo"] = slot_rows(f["L1_attn_wo_w"])
    w["sm_bo"] = f["L1_attn_wo_b"].reshape(128, 1)
    w["ml_wf"] = np.ascontiguousarray(f["L1_ffn_W_fc"].T)
    w["ml_wp"] = np.ascontiguousarray(f["L1_ffn_W_proj"].T.reshape(MT, 128, D).transpose(1, 0, 2))
    w["ml_lnw"] = np.ascontiguousarray(f["L1_ffn_ln_w"].reshape(MT, 128).T)
    w["ml_lnb"] = np.ascontiguousarray(f["L1_ffn_ln_b"].reshape(MT, 128).T)
    return w


def kernel(**inputs):
    import concourse.bacc as bacc
    from concourse.bass_utils import run_bass_kernel_spmd

    nc = bacc.Bacc("TRN2", target_bir_lowering=False, num_devices=1)
    arrays, aps = {}, {}
    for name, a in layout(inputs).items():
        a = np.ascontiguousarray(a)
        arrays[f"in_{name}"] = a
        aps[name] = nc.dram_tensor(f"in_{name}", a.shape, mybir.dt.from_np(a.dtype), kind="ExternalInput").ap()
    out = nc.dram_tensor("out_x", (128, TOK), FP32, kind="ExternalOutput").ap()
    program(nc, aps, out)
    r = run_bass_kernel_spmd(nc, [arrays], core_ids=[0])
    return np.ascontiguousarray(r.results[0]["out_x"].T).reshape(SEQS, L, D)
```
